# Optimizing a Trainium2 kernel written in Bass

```python
import numpy as np
import jax
import jax.numpy as jnp

def _softmax(x, axis=-1):
    return jax.nn.softmax(x, axis=axis)

def _gelu(x):
    return jax.nn.gelu(x, approximate=True)

def _silu(x):
    return jax.nn.silu(x)

def _sigmoid(x):
    return jax.nn.sigmoid(x)

def _layernorm(x, axis=-1, eps=1e-05):
    m = jnp.mean(x, axis=axis, keepdims=True)
    v = jnp.var(x, axis=axis, keepdims=True)
    return (x - m) / jnp.sqrt(v + eps)

def _scatter_add(tgt, idx, src, axis=0):
    return tgt.at[idx].add(src)

def _segment_sum(src, seg, n):
    return jax.ops.segment_sum(src, seg, n)
kernel_name = 'mk_gnn_resnorm_d2_gnn_r8_86a6dd'

def setup_inputs(seed: int=0):
    np.random.seed(seed)
    _w = jnp.asarray

    def _rec_inputs():
        import jax
        import jax.numpy as jnp
        _gk = jax.random.key(seed)
        x = -0.0001006 + 1 * jax.random.normal(jax.random.fold_in(_gk, 1), (6250, 48), jnp.float32)
        src = jax.random.randint(jax.random.fold_in(_gk, 2), (200000,), 0, 6250, jnp.int32)
        dst = jax.random.randint(jax.random.fold_in(_gk, 3), (200000,), 0, 6250, jnp.int32)
        _o = jnp.argsort(dst, stable=True)
        src = src[_o]
        dst = dst[_o]
        edge_attr_40 = jax.random.uniform(jax.random.fold_in(_gk, 12), (200000, 40), jnp.float32, 0.0, 1)
        edge_weight = jax.random.uniform(jax.random.fold_in(_gk, 14), (200000,), jnp.float32, 0.0, 6.99999)
        node_type_119 = jax.random.randint(jax.random.fold_in(_gk, 15), (6250,), 0, 119, jnp.int32)
        node_vec = jax.random.uniform(jax.random.fold_in(_gk, 16), (6250,), jnp.float32, 0.0, 1.49999)
        return (x, src, dst, edge_attr_40, edge_weight, node_type_119, node_vec)
    x, src, dst, edge_attr_40, edge_weight, node_type_119, node_vec = _rec_inputs()

    def _L0_gnn_setup():
        import jax, jax.numpy as jnp
        import numpy as np
        N = 12500
        E = 200000
        D = 48
        K = 5
        ALPHA = 0.8
        key = jax.random.key(seed)
        k1, k2 = jax.random.split(key)
        x = jax.random.normal(k1, (N, D), dtype=jnp.float32)
        edge_index = jax.random.randint(k2, (2, E), 0, N, dtype=jnp.int32)
        return {'x': x, 'edge_index': edge_index}
    _L0_gnn_all = _L0_gnn_setup()
    _L0_gnn_in = {k: v for k, v in _L0_gnn_all.items() if k in ()}
    del _L0_gnn_all

    def _L1_gnn_setup():
        import jax, jax.numpy as jnp
        import numpy as np
        CUTOFF = 6.0
        LN_EPS = 1e-05
        key = jax.random.key(seed)
        ks = jax.random.split(key, 16)
        N, E, H, R, NEL, G = (6250, 100000, 48, 40, 119, 32)
        inp = {'h': jax.random.normal(ks[0], (N, H), jnp.float32), 'edge_index': jax.random.randint(ks[1], (2, E), 0, N, jnp.int64), 'edge_attr': jax.random.uniform(ks[2], (E, R), jnp.float32), 'distances': jax.random.uniform(ks[3], (E,), jnp.float32) * 7.0, 'atom_z': jax.random.randint(ks[4], (N,), 0, NEL, jnp.int64), 'node_mult': jax.random.uniform(ks[5], (N,), jnp.float32) + 0.5, 'batch': jnp.zeros((N,), jnp.int64), 'W1': jax.random.normal(ks[6], (H, R), jnp.float32) / np.sqrt(R), 'b1': jax.random.normal(ks[7], (H,), jnp.float32) * 0.01, 'W2': jax.random.normal(ks[8], (H, H), jnp.float32) / np.sqrt(H), 'b2': jax.random.normal(ks[9], (H,), jnp.float32) * 0.01, 'emb': jax.random.normal(ks[10], (NEL, G), jnp.float32) * 0.01, 'adaptW': jax.random.normal(ks[11], (G, G), jnp.float32) * 0.01, 'gamma': jnp.ones((H,), jnp.float32), 'beta': jnp.zeros((H,), jnp.float32)}
        return inp
    _L1_gnn_all = _L1_gnn_setup()
    _L1_gnn_in = {k: v for k, v in _L1_gnn_all.items() if k in ('W1', 'b1', 'W2', 'b2', 'emb', 'adaptW', 'gamma', 'beta')}
    del _L1_gnn_all
    return {'x': x, 'src': src, 'dst': dst, 'edge_attr_40': edge_attr_40, 'edge_weight': edge_weight, 'node_type_119': node_type_119, 'node_vec': node_vec, 'L1_gnn_W1': _L1_gnn_in['W1'], 'L1_gnn_b1': _L1_gnn_in['b1'], 'L1_gnn_W2': _L1_gnn_in['W2'], 'L1_gnn_b2': _L1_gnn_in['b2'], 'L1_gnn_emb': _L1_gnn_in['emb'], 'L1_gnn_adaptW': _L1_gnn_in['adaptW'], 'L1_gnn_gamma': _L1_gnn_in['gamma'], 'L1_gnn_beta': _L1_gnn_in['beta']}

def reference(x, src, dst, edge_attr_40, edge_weight, node_type_119, node_vec, L1_gnn_W1, L1_gnn_b1, L1_gnn_W2, L1_gnn_b2, L1_gnn_emb, L1_gnn_adaptW, L1_gnn_gamma, L1_gnn_beta):
    import jax
    import jax.numpy as jnp

    def _L0_gnn_ref(x, edge_index):
        import jax, jax.numpy as jnp
        import numpy as np
        N = 12500
        E = 200000
        D = 48
        K = 5
        ALPHA = 0.8
        n = x.shape[0]
        loops = jnp.arange(n, dtype=edge_index.dtype)
        row = jnp.concatenate([edge_index[0], loops])
        col = jnp.concatenate([edge_index[1], loops])
        deg = jax.ops.segment_sum(jnp.ones(row.shape, x.dtype), col, num_segments=n)
        dinv = jnp.where(deg > 0, jax.lax.rsqrt(deg), jnp.zeros((), x.dtype))
        w = dinv[row] * dinv[col]

        def step(h, _):
            m = jax.ops.segment_sum(w[:, None] * h[row], col, num_segments=n)
            h = (1.0 - ALPHA) * m + ALPHA * x
            return (h, None)
        h, _ = jax.lax.scan(step, x, None, length=K)
        return h

    def _L1_gnn_ref(h, edge_index, edge_attr, distances, atom_z, node_mult, batch, W1, b1, W2, b2, emb, adaptW, gamma, beta):
        import jax, jax.numpy as jnp
        import numpy as np
        CUTOFF = 6.0
        LN_EPS = 1e-05
        src, dst = (edge_index[0], edge_index[1])
        N = h.shape[0]
        gate = jax.nn.silu(edge_attr @ W1.T + b1) @ W2.T + b2
        ei = emb[atom_z[src]]
        ej = emb[atom_z[dst]]
        adapt_logit = jnp.sum(ei * (ej @ adaptW.T), axis=-1, keepdims=True)
        gate = gate + adapt_logit
        cw = jnp.where(distances < CUTOFF, 0.5 * (jnp.cos(jnp.pi * distances / CUTOFF) + 1.0), 0.0)
        mj = node_mult[dst]
        msg = gate * h[dst] * (cw * mj)[:, None]
        agg = jax.ops.segment_sum(msg, src, num_segments=N)
        tot = jax.ops.segment_sum(mj, src, num_segments=N)
        agg = agg / jnp.clip(tot, 1e-08, None)[:, None]
        x = h + agg
        mu = jnp.mean(x, axis=-1, keepdims=True)
        var = jnp.mean(jnp.square(x - mu), axis=-1, keepdims=True)
        return (x - mu) / jnp.sqrt(var + LN_EPS) * gamma + beta
    edge_index = jnp.stack([src, dst])
    batch0 = jnp.zeros((6250,), jnp.int32)
    x = _layernorm(x + _L0_gnn_ref(x, edge_index), axis=-1)
    x = _layernorm(x + _L1_gnn_ref(x, edge_index, edge_attr_40, edge_weight, node_type_119, node_vec, batch0, L1_gnn_W1, L1_gnn_b1, L1_gnn_W2, L1_gnn_b2, L1_gnn_emb, L1_gnn_adaptW, L1_gnn_gamma, L1_gnn_beta), axis=-1)
    return x

_drawn_inputs = setup_inputs


def setup_inputs(seed=0):
    import zlib

    import numpy as np

    out = dict(_drawn_inputs(seed))
    spreads = {'L1_gnn_gamma': (1.0, 0.2), 'L1_gnn_beta': (0.0, 0.1)}
    factors = {'edge_attr_40': 5.909,
     'edge_weight': 4.977,
     'node_vec': 6.443,
     'L1_gnn_W1': 3.545,
     'L1_gnn_b1': 64.0,
     'L1_gnn_W2': 3.339,
     'L1_gnn_b2': 200.0,
     'L1_gnn_emb': 64.0,
     'L1_gnn_adaptW': 64.0}
    for name, (base, spread) in spreads.items():
        noise = np.random.default_rng([zlib.crc32(name.encode()), seed]).standard_normal(out[name].shape)
        drawn = base * np.exp(spread * noise) if base else spread * noise
        out[name] = jnp.asarray(drawn.astype(out[name].dtype))
    for name, factor in factors.items():
        out[name] = (out[name] * factor).astype(out[name].dtype)
    return out
```

```python
from contextlib import ExitStack, contextmanager
from math import pi

import concourse.bass as bass
from concourse import mybir

F32 = mybir.dt.float32
I32 = mybir.dt.int32
U32 = mybir.dt.uint32
ALU = mybir.AluOpType
ACT = mybir.ActivationFunctionType
AX = mybir.AxisListType.X

P = 128
STEPS, ALPHA = 5, 0.8
CUTOFF, EPS = 6.0, 1e-5


class Chain:

    def __init__(self, engine, sem, base=0):
        self.engine, self.sem, self.base, self.n = engine, sem, base, 0

    def __call__(self, ins):
        self.n += 1
        ins.then_inc(self.sem, 1)
        self.engine.wait_ge(self.sem, self.base + self.n)


def gnn(nc, x, src, dst, edge_attr, edge_weight, node_type, node_vec, W1, b1, W2, b2, emb, adaptW, gamma, beta, out):
    N, H = x.shape
    E, R = edge_attr.shape
    NT, G = emb.shape
    NB = -(-N // P)
    LAST = N - (NB - 1) * P
    NP = NB * P
    SP_ = 125
    ST = E // SP_
    assert SP_ * ST == E
    WD = H + 1 + G

    with ExitStack() as ctx:
        def sb(name, shape, dt=F32, c=ctx):
            return c.enter_context(nc.sbuf_tensor(name, shape, dt))

        def ps(name, shape, dt=F32, c=ctx):
            return c.enter_context(nc.psum_tensor(name, shape, dt))

        def sem(name):
            return nc.alloc_semaphore(name=name)

        @contextmanager
        def own_semaphores():
            before = nc.snapshot_sems()
            yield
            nc.all_engine_barrier()
            nc.clear_and_free_semaphores(nc.allocated_since(before))
            nc.all_engine_barrier()

        def dram(name, shape, dt=F32):
            return nc.dram_tensor(name, shape, dt, kind="Internal").ap()

        gT = dram("g_table", [NP, H])
        sumT = dram("sum_table", [NP, H])
        dstT = dram("dst_table", [NP, WD])
        srcT = dram("src_table", [NP, G])
        aggT = dram("agg_table", [NP, H + 1])
        nodes = lambda t: t.rearrange("(b p) w -> p b w", p=P)

        x_sb = sb("x_sb", [P, NB, H])
        h_sb = sb("h_sb", [P, NB, H])
        u_sb = sb("u_sb", [P, NB, H])
        v_sb = sb("v_sb", [P, NB, H])
        dinv = sb("dinv", [P, NB])
        emb_n = sb("emb_n", [P, NB, G])
        dst_n = sb("dst_n", [P, NB, WD])
        mult = sb("mult", [P, NB])
        z_sb = sb("z_sb", [P, NB], I32)
        ident = sb("ident", [P, P])
        ones = sb("ones", [P, P])
        below = sb("below", [P, P])
        w1 = sb("w1", [H, R])
        w1T = sb("w1T", [R, H])
        b1c = sb("b1c", [H, 1])
        w2T = sb("w2T", [H + 1, H])
        w2 = sb("w2", [H, H])
        aw = sb("aw", [G, G])
        awT = sb("awT", [G, G])
        gb = sb("gb", [P, 2, H])
        s1 = sb("s1", [P, NB])
        s2 = sb("s2", [P, NB])
        ew = sb("ew", [SP_, ST])
        cw = sb("cw", [SP_, ST])
        src_sb = sb("src_sb", [SP_, ST], I32)
        dst_sb = sb("dst_sb", [SP_, ST], I32)
        zrow = sb("zrow", [P, NB, H + 1])
        halfpi = sb("halfpi", [P, 1])
        epsc = sb("epsc", [P, 1])

        s_load, s_const, s_mask = sem("s_load"), sem("s_const"), sem("s_mask")
        s_wT, s_wTc = sem("s_wT"), sem("s_wTc")
        s_emb, s_eT, s_eTc, s_q, s_qc = sem("s_emb"), sem("s_eT"), sem("s_eTc"), sem("s_q"), sem("s_qc")
        s_cw0, s_cw1, s_cwd = sem("s_cw0"), sem("s_cw1"), sem("s_cwd")

        def node_in(eng, tile, table, s):
            eng.dma_start(tile[:, 0:NB - 1, :], table[0:(NB - 1) * P, :].rearrange("(b p) w -> p b w", p=P)).then_inc(s, 16)
            eng.dma_start(tile[0:LAST, NB - 1, :], table[(NB - 1) * P:N, :]).then_inc(s, 16)

        with nc.Block() as block, ExitStack() as c:
            tp = ps("tp", [P, 512], c=c)

            @block.gpsimd
            def _(pool):
                pool.wait_ge(s_const, 1)
                nc.gpsimd.affine_select(out=ident[:, :], in_=ident[:, :], compare_op=ALU.not_equal, fill=1.0, base=0,
                                        pattern=[[-1, P]], channel_multiplier=1).then_inc(s_mask, 1)
                nc.gpsimd.affine_select(out=below[:, :], in_=ones[:, :], compare_op=ALU.is_gt, fill=0.0, base=0,
                                        pattern=[[-1, P]], channel_multiplier=1).then_inc(s_mask, 1)

            @block.vector
            def _(dve):
                nc.vector.memset(ident[:, :], 0.0)
                nc.vector.memset(ones[:, :], 1.0)
                nc.vector.memset(zrow[:, :, :], 0.0)
                nc.vector.memset(x_sb[:, NB - 1, :], 0.0)
                nc.vector.memset(mult[:, NB - 1:NB], 0.0)
                nc.vector.memset(z_sb[:, NB - 1:NB], 0)
                nc.vector.memset(halfpi[:, :], pi / 2)
                nc.vector.memset(epsc[:, :], EPS)
                nc.vector.drain().then_inc(s_const, 1)
                dve.wait_ge(s_wT, 1)
                nc.vector.tensor_copy(w1T[:, :], tp[0:R, 0:H])
                nc.vector.tensor_copy(w2T[0:H, :], tp[0:H, P:P + H])
                nc.vector.tensor_copy(awT[:, :], tp[0:G, 2 * P:2 * P + G]).then_inc(s_wTc, 1)

            @block.sync
            def _(sp):
                sp.wait_ge(s_const, 1)
                node_in(sp, x_sb, x, s_load)
                with nc.allow_non_contiguous_dma(reason="one word per node, twice"):
                    node_in(sp, mult.rearrange("p (b o) -> p b o", o=1), node_vec.rearrange("(n o) -> n o", o=1), s_load)
                    node_in(sp, z_sb.rearrange("p (b o) -> p b o", o=1), node_type.rearrange("(n o) -> n o", o=1), s_load)
                sp.dma_start(w1[:, :], W1).then_inc(s_load, 16)
                sp.dma_start(w2[:, :], W2).then_inc(s_load, 16)
                sp.dma_start(aw[:, :], adaptW).then_inc(s_load, 16)
                with nc.allow_non_contiguous_dma(reason="one word per hidden unit"):
                    sp.dma_start(b1c[:, :], b1.rearrange("(n o) -> n o", o=1)).then_inc(s_load, 16)
                sp.dma_start(w2T[H:H + 1, :], b2.rearrange("(o n) -> o n", o=1)).then_inc(s_load, 16)
                sp.dma_start(gb[:, 0, :], gamma.rearrange("(o n) -> o n", o=1).to_broadcast([P, H])).then_inc(s_load, 16)
                sp.dma_start(gb[:, 1, :], beta.rearrange("(o n) -> o n", o=1).to_broadcast([P, H])).then_inc(s_load, 16)
                sp.dma_start(src_sb[:, :], src.rearrange("(p j) -> p j", p=SP_)).then_inc(s_load, 16)
                sp.dma_start(dst_sb[:, :], dst.rearrange("(p j) -> p j", p=SP_)).then_inc(s_load, 16)
                sp.dma_start(ew[:, :], edge_weight.rearrange("(p j) -> p j", p=SP_)).then_inc(s_load, 16)
                sp.wait_ge(s_load, 16 * 16)

            @block.tensor
            def _(pe):
                pe.wait_ge(s_load, 16 * 16)
                pe.wait_ge(s_mask, 2)
                nc.tensor.transpose(tp[0:R, 0:H], w1[:, :], ident[0:H, 0:H])
                nc.tensor.transpose(tp[0:H, P:P + H], w2[:, :], ident[0:H, 0:H])
                nc.tensor.transpose(tp[0:G, 2 * P:2 * P + G], aw[:, :], ident[0:G, 0:G]).then_inc(s_wT, 1)

        with nc.Block() as block, ExitStack() as c:
            eT = sb("eT", [G, 2, P], c=c)
            pt = ps("pt", [G, 2, 512], c=c)
            pq = ps("pq", [P, 2, 512], c=c)

            @block.gpsimd
            def _(pool):
                for b in range(NB):
                    pool.indirect_dma_start(emb_n[:, b, :], None, emb, bass.IndirectOffsetOnAxis(
                        ap=z_sb[:, b:b + 1].bitcast(U32), axis=0)).then_inc(s_emb, 16)

            @block.tensor
            def _(pe):
                pe.wait_ge(s_emb, 16 * NB)
                for b in range(NB):
                    if b >= 2:
                        pe.wait_ge(s_eTc, b - 1)
                    nc.tensor.transpose(pt[:, b % 2, 0:P], emb_n[:, b, :], ident[:, :]).then_inc(s_eT, 1)
                    pe.wait_ge(s_eTc, b + 1)
                    if b >= 2:
                        pe.wait_ge(s_qc, b - 1)
                    nc.tensor.matmul(pq[:, b % 2, 0:G], eT[:, b % 2, :], awT[:, :]).then_inc(s_q, 1)

            @block.vector
            def _(dve):
                for b in range(NB):
                    dve.wait_ge(s_eT, b + 1)
                    if b >= 2:
                        dve.wait_ge(s_q, b - 1)
                    nc.vector.tensor_copy(eT[:, b % 2, :], pt[:, b % 2, 0:P]).then_inc(s_eTc, 1)
                    dve.wait_ge(s_q, b + 1)
                    nc.vector.tensor_copy(dst_n[:, b, H + 1:WD], pq[:, b % 2, 0:G]).then_inc(s_qc, 1)
                nc.vector.tensor_copy(dst_n[:, :, H:H + 1], mult[:, :].unsqueeze(2))
                nc.vector.tensor_scalar(cw[:, :], ew[:, :], CUTOFF, None, ALU.min).then_inc(s_cw0, 1)
                dve.wait_ge(s_cw1, 1)
                nc.vector.tensor_scalar(ew[:, :], ew[:, :], CUTOFF, None, ALU.is_lt)
                nc.vector.tensor_scalar(cw[:, :], cw[:, :], 1.0, 0.5, ALU.add, ALU.mult)
                nc.vector.drain()
                nc.vector.tensor_tensor(cw[:, :], cw[:, :], ew[:, :], ALU.mult)

            @block.scalar
            def _(act):
                act.wait_ge(s_cw0, 1)
                nc.scalar.activation(cw[:, :], cw[:, :], ACT.Sin, bias=halfpi[0:SP_, :], scale=-pi / CUTOFF).then_inc(s_cw1, 1)

        def node_block(name, vector, scalar=None, load=None, store=()):
            s_in, s_v, s_out = sem(name + "_in"), sem(name + "_vec"), sem(name + "_out")
            with nc.Block() as block:
                @block.sync
                def _(sp):
                    if load:
                        sp.dma_start(load[0], load[1]).then_inc(s_in, 16)
                        sp.wait_ge(s_in, 16)
                    sp.wait_ge(s_v, 1)
                    for to, what in store:
                        sp.dma_start(to, what).then_inc(s_out, 16)
                    if store:
                        sp.wait_ge(s_out, 16 * len(store))

                @block.vector
                def _(dve):
                    if load:
                        dve.wait_ge(s_in, 16)
                    vector(dve)
                    nc.vector.drain().then_inc(s_v, 1)

                if scalar:
                    block.scalar(scalar)

        def layer_norm(name, t, tmp):
            s_var, s_std = sem(name + "_var"), sem(name + "_std")

            def vector(dve):
                nc.vector.tensor_reduce(s1[:, :], t[:, :, :], AX, ALU.add)
                nc.vector.drain()
                nc.vector.tensor_scalar(s1[:, :], s1[:, :], 1.0 / H, None, ALU.mult)
                nc.vector.drain()
                nc.vector.tensor_tensor(t[:, :, :], t[:, :, :], s1[:, :].unsqueeze(2).to_broadcast([P, NB, H]), ALU.subtract)
                nc.vector.drain()
                nc.vector.tensor_tensor(tmp[:, :, :], t[:, :, :], t[:, :, :], ALU.mult)
                nc.vector.drain()
                nc.vector.tensor_reduce(s2[:, :], tmp[:, :, :], AX, ALU.add).then_inc(s_var, 1)
                dve.wait_ge(s_std, 1)
                nc.vector.reciprocal(s2[:, :], s1[:, :])
                nc.vector.drain()
                nc.vector.tensor_tensor(t[:, :, :], t[:, :, :], s2[:, :].unsqueeze(2).to_broadcast([P, NB, H]), ALU.mult)
                nc.vector.drain()

            def scalar(act):
                act.wait_ge(s_var, 1)
                nc.scalar.activation(s1[:, :], s2[:, :], ACT.Sqrt, bias=epsc[:, :], scale=1.0 / H).then_inc(s_std, 1)

            return vector, scalar

        c = ctx
        kf = sb("kf", [SP_, 1])
        ku = sb("ku", [SP_, 1], U32)
        su = sb("su", [SP_, 1], U32)
        wf = sb("wf", [SP_, 1])
        wu = sb("wu", [SP_, 1], U32)
        cwc = sb("cwc", [SP_, 1])
        diag = sb("diag", [SP_, SP_])
        eq = sb("eq", [SP_, SP_])
        dup = sb("dup", [SP_, SP_])
        rows = sb("rows", [SP_, H + 1])
        cur = sb("cur", [SP_, H + 1])
        dstrow = sb("dstrow", [SP_, WD])
        srcrow = sb("srcrow", [SP_, G])
        prod = sb("prod", [SP_, G])
        ad = sb("ad", [SP_, 1])
        attr = sb("attr", [SP_, R])
        attrT = sb("attrT", [R, SP_])
        hid = sb("hid", [H + 1, SP_])
        pk = ps("pk", [P, 512])
        psum_rows = ps("psum_rows", [P, 512])
        pa = ps("pa", [P, 512])
        ph = ps("ph", [P, 512])
        pg = ps("pg", [P, 512])

        def zero_table(name, table, W):
            s = sem(name)
            with nc.Block() as block:
                @block.sync
                def _(sp):
                    sp.dma_start(nodes(table), zrow[:, :, 0:W]).then_inc(s, 16)
                    sp.wait_ge(s, 16)

        def add_pass(name, table, W, key, other, messages):
            s_free = sem(name + "_free")
            s_key = sem(name + "_key")
            s_go = sem(name + "_go")
            s_gath = [sem(f"{name}_gath{n}") for n in range(3 if messages else 2)]
            s_kt = sem(name + "_kt")
            s_eq = sem(name + "_eq")
            s_msg = sem(name + "_msg")
            s_sum = sem(name + "_sum")
            s_new = sem(name + "_new")
            s_scat = sem(name + "_scat")
            s_attr, s_aT, s_aTc = sem(name + "_attr"), sem(name + "_aT"), sem(name + "_aTc")
            s_h, s_hc, s_g = sem(name + "_h"), sem(name + "_hc"), sem(name + "_g")
            s_v, s_pe = sem(name + "_v"), sem(name + "_pe")
            NV = 13 if messages else 7

            with nc.Block() as block:
                @block.gpsimd
                def _(pool):
                    pool.sem_inc(s_free, 1)
                    with pool.Fori(0, ST) as t:
                        pool.wait_ge(s_key, t + 1)
                        pool.sem_inc(s_go, 1)
                        off = lambda a: bass.IndirectOffsetOnAxis(ap=a[:, :], axis=0)
                        pool.indirect_dma_start(cur[:, 0:W], None, table, off(ku)).then_inc(s_gath[0], 16)
                        if messages:
                            pool.indirect_dma_start(dstrow[:, :], None, dstT, off(su)).then_inc(s_gath[1], 16)
                            pool.indirect_dma_start(srcrow[:, :], None, srcT, off(ku)).then_inc(s_gath[2], 16)
                        else:
                            pool.indirect_dma_start(rows[:, 0:W], None, gT, off(su)).then_inc(s_gath[1], 16)
                        pool.wait_ge(s_new, t + 1)
                        pool.sem_inc(s_go, 1)
                        pool.indirect_dma_start(table, off(wu), cur[:, 0:W], None, bounds_check=NP - 1,
                                                oob_is_err=False).then_inc(s_scat, 16)
                        pool.wait_ge(s_scat, t * 16 + 16)
                        pool.sem_inc(s_free, 1)

                @block.vector
                def _(dve):
                    with dve.Fori(0, ST) as t:
                        step = Chain(dve, s_v, t * NV)
                        dve.wait_ge(s_free, t + 1)
                        nc.vector.tensor_copy(kf[:, :], key[:, bass.ds(t, 1)])
                        nc.vector.tensor_copy(ku[:, :], key[:, bass.ds(t, 1)])
                        step(nc.vector.tensor_copy(su[:, :], other[:, bass.ds(t, 1)]))
                        dve.sem_inc(s_key, 1)
                        step(nc.vector.tensor_scalar(diag[:, :], ident[0:SP_, 0:SP_], kf[:, :], None, ALU.mult))
                        dve.sem_inc(s_eq, 1)
                        dve.wait_ge(s_kt, t + 1)
                        step(nc.vector.tensor_scalar(eq[:, :], pk[0:SP_, 0:SP_], kf[:, :], None, ALU.is_equal))
                        step(nc.vector.tensor_tensor(dup[:, :], eq[:, :], below[0:SP_, 0:SP_], ALU.mult))
                        step(nc.vector.tensor_reduce(wf[:, :], dup[:, :], AX, ALU.max))
                        step(nc.vector.tensor_scalar(wu[:, :], wf[:, :], float(1 << 20), kf[:, :], ALU.mult, ALU.add))
                        for s in s_gath:
                            dve.wait_ge(s, t * 16 + 16)
                        if messages:
                            step(nc.vector.tensor_copy(cwc[:, :], cw[:, bass.ds(t, 1)]))
                            step(nc.vector.tensor_tensor(prod[:, :], dstrow[:, H + 1:WD], srcrow[:, :], ALU.mult))
                            step(nc.vector.tensor_reduce(ad[:, :], prod[:, :], AX, ALU.add))
                            dve.wait_ge(s_g, t + 1)
                            step(nc.vector.tensor_scalar(rows[:, 0:H], pg[0:SP_, 0:H], ad[:, :], cwc[:, :], ALU.add, ALU.mult))
                            step(nc.vector.tensor_tensor(rows[:, 0:H], rows[:, 0:H], dstrow[:, 0:H], ALU.mult))
                            step(nc.vector.tensor_copy(rows[:, H:H + 1], dstrow[:, H:H + 1]))
                        dve.sem_inc(s_msg, 1)
                        dve.wait_ge(s_sum, t + 1)
                        step(nc.vector.tensor_tensor(cur[:, 0:W], cur[:, 0:W], psum_rows[0:SP_, 0:W], ALU.add))
                        dve.sem_inc(s_new, 1)
                        assert step.n == NV

                @block.tensor
                def _(pe):
                    with pe.Fori(0, ST) as t:
                        if messages:
                            pe.wait_ge(s_attr, t * 16 + 16)
                            pe.sem_inc(s_pe, 1)
                            nc.tensor.transpose(pa[0:R, 0:SP_], attr[:, :], ident[0:SP_, 0:SP_]).then_inc(s_aT, 1)
                            pe.wait_ge(s_aTc, t + 1)
                            pe.sem_inc(s_pe, 1)
                            nc.tensor.matmul(ph[0:H, 0:SP_], w1T[:, :], attrT[:, :]).then_inc(s_h, 1)
                            pe.wait_ge(s_hc, t + 2)
                            pe.sem_inc(s_pe, 1)
                            nc.tensor.matmul(pg[0:SP_, 0:H], hid[:, :], w2T[:, :]).then_inc(s_g, 1)
                        pe.wait_ge(s_eq, t + 1)
                        nc.tensor.matmul(pk[0:SP_, 0:SP_], ones[0:SP_, 0:SP_], diag[:, :]).then_inc(s_kt, 1)
                        pe.wait_ge(s_msg, t + 1)
                        nc.tensor.matmul(psum_rows[0:SP_, 0:W], eq[:, :], rows[:, 0:W]).then_inc(s_sum, 1)

                if messages:
                    @block.sync
                    def _(sp):
                        tiles = edge_attr.rearrange("(p j) f -> p j f", p=SP_)
                        with sp.Fori(0, ST) as t:
                            sp.wait_ge(s_free, t + 1)
                            sp.dma_start(attr[:, :], tiles[:, bass.ds(t, 1), :].rearrange("p o f -> p (o f)")).then_inc(s_attr, 16)

                    @block.scalar
                    def _(act):
                        nc.scalar.activation(hid[:, :], ones[0:H + 1, 0:SP_], ACT.Copy).then_inc(s_hc, 1)
                        act.wait_ge(s_hc, 1)
                        with act.Fori(0, ST) as t:
                            act.wait_ge(s_aT, t + 1)
                            nc.scalar.activation(attrT[:, :], pa[0:R, 0:SP_], ACT.Copy).then_inc(s_aTc, 1)
                            act.wait_ge(s_h, t + 1)
                            nc.scalar.activation(hid[0:H, :], ph[0:H, 0:SP_], ACT.Silu, bias=b1c[:, :]).then_inc(s_hc, 1)

        bcast = lambda a: a[:, :].unsqueeze(2).to_broadcast([P, NB, H])

        def general_path():
            def fill_ones(dve):
                nc.vector.memset(u_sb[:, :, :], 1.0)
            node_block("ones", fill_ones, store=[(nodes(gT), u_sb[:, :, :])])
            with own_semaphores():
                zero_table("zero_deg", sumT, H)
                add_pass("deg", sumT, H, dst_sb, src_sb, False)

            s_dv, s_ds = sem("s_dv"), sem("s_ds")

            def degree(dve):
                nc.vector.tensor_scalar(s1[:, :], v_sb[:, :, 0], 1.0, None, ALU.add).then_inc(s_dv, 1)
                dve.wait_ge(s_ds, 1)
                nc.vector.reciprocal(dinv[:, :], s2[:, :])
                nc.vector.drain()
                nc.vector.tensor_tensor(h_sb[:, :, :], x_sb[:, :, :], bcast(dinv), ALU.mult)

            def degree_root(act):
                act.wait_ge(s_dv, 1)
                nc.scalar.activation(s2[:, :], s1[:, :], ACT.Sqrt).then_inc(s_ds, 1)
            node_block("deg_n", degree, degree_root, load=(v_sb[:, :, :], nodes(sumT)), store=[(nodes(gT), h_sb[:, :, :])])

            for k in range(STEPS):
                with own_semaphores():
                    zero_table(f"zero{k}", sumT, H)
                    add_pass(f"prop{k}", sumT, H, dst_sb, src_sb, False)

                def update(dve, last=k == STEPS - 1):
                    nc.vector.tensor_tensor(v_sb[:, :, :], v_sb[:, :, :], h_sb[:, :, :], ALU.add)
                    nc.vector.drain()
                    nc.vector.tensor_tensor(v_sb[:, :, :], v_sb[:, :, :], bcast(dinv), ALU.mult)
                    nc.vector.tensor_scalar(u_sb[:, :, :], x_sb[:, :, :], ALPHA, None, ALU.mult)
                    nc.vector.drain()
                    nc.vector.scalar_tensor_tensor(h_sb[:, :, :], v_sb[:, :, :], 1.0 - ALPHA, u_sb[:, :, :], ALU.mult, ALU.add)
                    nc.vector.drain()
                    if not last:
                        nc.vector.tensor_tensor(h_sb[:, :, :], h_sb[:, :, :], bcast(dinv), ALU.mult)
                node_block(f"upd{k}", update, load=(v_sb[:, :, :], nodes(sumT)), store=[(nodes(gT), h_sb[:, :, :])])

            ln0, ln0s = layer_norm("ln0", x_sb, u_sb)

            def first_norm(dve):
                nc.vector.tensor_tensor(x_sb[:, :, :], x_sb[:, :, :], h_sb[:, :, :], ALU.add)
                nc.vector.drain()
                ln0(dve)
                nc.vector.tensor_tensor(dst_n[:, :, 0:H], x_sb[:, :, :], bcast(mult), ALU.mult)
            node_block("norm0", first_norm, ln0s, store=[
                (nodes(dstT), dst_n[:, :, :]), (nodes(srcT), emb_n[:, :, :])])

            zero_table("zero_agg", aggT, H + 1)
            add_pass("conv", aggT, H + 1, src_sb, dst_sb, True)
            final_block(load=(zrow[:, :, :], nodes(aggT)))

        def final_block(load=None):
            ln1, ln1s = layer_norm("ln1", v_sb, u_sb)
            ln2, ln2s = layer_norm("ln2", h_sb, u_sb)

            def last(dve):
                nc.vector.tensor_scalar(s1[:, :], zrow[:, :, H], 1e-8, None, ALU.max)
                nc.vector.drain()
                nc.vector.reciprocal(s2[:, :], s1[:, :])
                nc.vector.drain()
                nc.vector.tensor_tensor(v_sb[:, :, :], zrow[:, :, 0:H], bcast(s2), ALU.mult)
                nc.vector.drain()
                nc.vector.tensor_tensor(v_sb[:, :, :], v_sb[:, :, :], x_sb[:, :, :], ALU.add)
                nc.vector.drain()
                ln1(dve)
                nc.vector.tensor_tensor(v_sb[:, :, :], v_sb[:, :, :], gb[:, 0, :].unsqueeze(1).to_broadcast([P, NB, H]), ALU.mult)
                nc.vector.drain()
                nc.vector.tensor_tensor(v_sb[:, :, :], v_sb[:, :, :], gb[:, 1, :].unsqueeze(1).to_broadcast([P, NB, H]), ALU.add)
                nc.vector.drain()
                nc.vector.tensor_tensor(h_sb[:, :, :], v_sb[:, :, :], x_sb[:, :, :], ALU.add)
                nc.vector.drain()
                ln2(dve)

            def last_s(act):
                ln1s(act)
                ln2s(act)
            node_block("final", last, last_s, load=load, store=[
                (out[0:(NB - 1) * P, :].rearrange("(b p) w -> p b w", p=P), h_sb[:, 0:NB - 1, :]),
                (out[(NB - 1) * P:N, :], h_sb[0:LAST, NB - 1, :])])

        general_path()


_INS = ["x", "src", "dst", "edge_attr_40", "edge_weight", "node_type_119", "node_vec", "L1_gnn_W1", "L1_gnn_b1",
        "L1_gnn_W2", "L1_gnn_b2", "L1_gnn_emb", "L1_gnn_adaptW", "L1_gnn_gamma", "L1_gnn_beta"]


def kernel(**inputs):
    import numpy as _np
    import concourse.bacc as _bacc
    from concourse.bass_utils import run_bass_kernel_spmd as _run

    nc = _bacc.Bacc("TRN2", target_bir_lowering=False, num_devices=1)
    arrays, args = {}, []
    for name in _INS:
        a = _np.ascontiguousarray(inputs[name])
        arrays[f"in_{name}_dram"] = a
        args.append(nc.dram_tensor(f"in_{name}_dram", a.shape, mybir.dt.from_np(a.dtype), kind="ExternalInput").ap())
    args.append(nc.dram_tensor("out_0_dram", inputs["x"].shape, F32, kind="ExternalOutput").ap())
    gnn(nc, *args)
    r = _run(nc, [arrays], core_ids=[0])
    return r.results[0]["out_0_dram"]
```

```python
from contextlib import ExitStack, contextmanager
from math import pi

import concourse.bass as bass
from concourse import mybir

F32 = mybir.dt.float32
BF16 = mybir.dt.bfloat16
F16 = mybir.dt.float16
I32 = mybir.dt.int32
U32 = mybir.dt.uint32
ALU = mybir.AluOpType
ACT = mybir.ActivationFunctionType
AX = mybir.AxisListType.X

P = 128
STEPS, ALPHA = 5, 0.8
CUTOFF, EPS = 6.0, 1e-5


class Chain:

    def __init__(self, engine, sem, base=0):
        self.engine, self.sem, self.base, self.n = engine, sem, base, 0

    def __call__(self, ins):
        self.n += 1
        ins.then_inc(self.sem, 1)
        self.engine.wait_ge(self.sem, self.base + self.n)


def gnn(nc, x, src, dst, edge_attr, edge_weight, node_type, node_vec, W1, b1, W2, b2, emb, adaptW, gamma, beta, out):
    N, H = x.shape
    E, R = edge_attr.shape
    NT, G = emb.shape
    NB = -(-N // P)
    LAST = N - (NB - 1) * P
    NP = NB * P
    SP_ = 125
    ST = E // SP_
    assert SP_ * ST == E
    WD = H + 1 + G

    with ExitStack() as ctx:
        def sb(name, shape, dt=F32, c=ctx):
            return c.enter_context(nc.sbuf_tensor(name, shape, dt))

        def ps(name, shape, dt=F32, c=ctx):
            return c.enter_context(nc.psum_tensor(name, shape, dt))

        seen = set()

        def sem(name):
            while name in seen:
                name += "_"
            seen.add(name)
            return nc.alloc_semaphore(name=name)

        @contextmanager
        def own_semaphores():
            before = nc.snapshot_sems()
            yield
            nc.all_engine_barrier()
            nc.clear_and_free_semaphores(nc.allocated_since(before))
            nc.all_engine_barrier()

        def dram(name, shape, dt=F32):
            return nc.dram_tensor(name, shape, dt, kind="Internal").ap()

        gT = dram("g_table", [NP, H])
        sumT = dram("sum_table", [NP, H])
        dstT = dram("dst_table", [NP, WD])
        srcT = dram("src_table", [NP, G])
        aggT = dram("agg_table", [NP, H + 1])
        nodes = lambda t: t.rearrange("(b p) w -> p b w", p=P)

        ND = 2 * -(-NB // 2)
        GR = 8
        GB = P // GR
        GT = 3
        GE = GT * P
        NQ = ND * GB + 1
        QC = -(-NQ // P)
        WT = 35
        WE = WT * P
        KG = NB * GR
        PW = H + 4
        SLOTS = ND * NB * P
        DROP = float(1 << 22)
        H3, T3 = 3 * H, 3 * WD
        CH = 7
        assert NB % CH == 0 and ND * GB * GR >= N and ND // 5 * 5 == ND

        keyT = dram("key_table", [E], I32)
        cwT = dram("cw_table", [E])
        startT = dram("start_table", [QC * P])
        adjT = dram("adj_table", [ND, P, NB * P], BF16)
        slotT = dram("slot_table", [SLOTS, PW])

        x_sb = sb("x_sb", [P, NB, H])
        emb_n = sb("emb_n", [P, NB, G])
        dst_n = sb("dst_n", [P, NB, WD])
        mult = sb("mult", [P, NB])
        z_sb = sb("z_sb", [P, NB], I32)
        ident = sb("ident", [P, P])
        ident_b = sb("ident_b", [P, P], BF16)
        ones = sb("ones", [P, P])
        ones_b = sb("ones_b", [P, 2], BF16)
        below = sb("below", [P, P])
        above_b = sb("above_b", [P, P], BF16)
        w1 = sb("w1", [H, R])
        w1T = sb("w1T", [R, H])
        b1c = sb("b1c", [H, 1])
        w2T = sb("w2T", [H + 1, H])
        w2 = sb("w2", [H, H])
        aw = sb("aw", [G, G])
        awT = sb("awT", [G, G])
        gb = sb("gb", [P, 2, H])
        s1 = sb("s1", [P, NB])
        s2 = sb("s2", [P, NB])
        halfpi = sb("halfpi", [P, 1])
        epsc = sb("epsc", [P, 1])
        start_row = sb("start_row", [1, QC * P])
        group_at = sb("group_at", [1, ND * GB], I32)
        block_at = sb("block_at", [1, ND], I32)
        flags = sb("flags", [1, 4])
        flag_i = sb("flag_i", [1, 1], I32)
        deg = sb("deg", [P, ND])

        def node_in(eng, tile, table, s):
            eng.dma_start(tile[:, 0:NB - 1, :], table[0:(NB - 1) * P, :].rearrange("(b p) w -> p b w", p=P)).then_inc(s, 16)
            eng.dma_start(tile[0:LAST, NB - 1, :], table[(NB - 1) * P:N, :]).then_inc(s, 16)

        def setup():
            s_load, s_const, s_mask = sem("s_load"), sem("s_const"), sem("s_mask")
            s_wT, s_wTc = sem("s_wT"), sem("s_wTc")
            s_emb, s_eT, s_eTc, s_q, s_qc = sem("s_emb"), sem("s_eT"), sem("s_eTc"), sem("s_q"), sem("s_qc")
            LOADS = 16 * 13
            with nc.Block() as block, ExitStack() as c:
                tp = ps("tp", [P, 512], c=c)

                @block.gpsimd
                def _(pool):
                    pool.wait_ge(s_const, 1)
                    nc.gpsimd.affine_select(out=ident[:, :], in_=ident[:, :], compare_op=ALU.not_equal, fill=1.0, base=0,
                                            pattern=[[-1, P]], channel_multiplier=1).then_inc(s_mask, 1)
                    nc.gpsimd.affine_select(out=below[:, :], in_=ones[:, :], compare_op=ALU.is_gt, fill=0.0, base=0,
                                            pattern=[[-1, P]], channel_multiplier=1).then_inc(s_mask, 1)

                @block.vector
                def _(dve):
                    nc.vector.memset(ident[:, :], 0.0)
                    nc.vector.memset(ones[:, :], 1.0)
                    nc.vector.memset(ones_b[:, :], 1.0)
                    nc.vector.memset(x_sb[:, NB - 1, :], 0.0)
                    nc.vector.memset(mult[:, NB - 1:NB], 0.0)
                    nc.vector.memset(z_sb[:, NB - 1:NB], 0)
                    nc.vector.memset(halfpi[:, :], pi / 2)
                    nc.vector.memset(epsc[:, :], EPS)
                    nc.vector.drain().then_inc(s_const, 1)
                    dve.wait_ge(s_mask, 2)
                    nc.vector.tensor_copy(ident_b[:, :], ident[:, :])
                    nc.vector.tensor_tensor(above_b[:, :], ones[:, :], below[:, :], ALU.subtract)
                    nc.vector.drain()
                    nc.vector.tensor_tensor(above_b[:, :], above_b[:, :], ident_b[:, :], ALU.subtract)
                    dve.wait_ge(s_wT, 1)
                    nc.vector.tensor_copy(w1T[:, :], tp[0:R, 0:H])
                    nc.vector.tensor_copy(w2T[0:H, :], tp[0:H, P:P + H])
                    nc.vector.tensor_copy(awT[:, :], tp[0:G, 2 * P:2 * P + G]).then_inc(s_wTc, 1)

                @block.sync
                def _(sp):
                    sp.wait_ge(s_const, 1)
                    node_in(sp, x_sb, x, s_load)
                    with nc.allow_non_contiguous_dma(reason="one word per node"):
                        node_in(sp, mult.rearrange("p (b o) -> p b o", o=1), node_vec.rearrange("(n o) -> n o", o=1), s_load)
                        node_in(sp, z_sb.rearrange("p (b o) -> p b o", o=1), node_type.rearrange("(n o) -> n o", o=1), s_load)
                        sp.dma_start(b1c[:, :], b1.rearrange("(n o) -> n o", o=1)).then_inc(s_load, 16)
                    sp.dma_start(w1[:, :], W1).then_inc(s_load, 16)
                    sp.dma_start(w2[:, :], W2).then_inc(s_load, 16)
                    sp.dma_start(aw[:, :], adaptW).then_inc(s_load, 16)
                    sp.dma_start(w2T[H:H + 1, :], b2.rearrange("(o n) -> o n", o=1)).then_inc(s_load, 16)
                    sp.dma_start(gb[:, 0, :], gamma.rearrange("(o n) -> o n", o=1).to_broadcast([P, H])).then_inc(s_load, 16)
                    sp.dma_start(gb[:, 1, :], beta.rearrange("(o n) -> o n", o=1).to_broadcast([P, H])).then_inc(s_load, 16)
                    sp.wait_ge(s_load, LOADS)

                @block.tensor
                def _(pe):
                    pe.wait_ge(s_load, LOADS)
                    pe.wait_ge(s_mask, 2)
                    nc.tensor.transpose(tp[0:R, 0:H], w1[:, :], ident[0:H, 0:H])
                    nc.tensor.transpose(tp[0:H, P:P + H], w2[:, :], ident[0:H, 0:H])
                    nc.tensor.transpose(tp[0:G, 2 * P:2 * P + G], aw[:, :], ident[0:G, 0:G]).then_inc(s_wT, 1)

            with nc.Block() as block, ExitStack() as c:
                eT = sb("eT", [G, 2, P], c=c)
                pt = ps("pt", [G, 2, 512], c=c)
                pq = ps("pq", [P, 2, 512], c=c)

                @block.gpsimd
                def _(pool):
                    for b in range(NB):
                        pool.indirect_dma_start(emb_n[:, b, :], None, emb, bass.IndirectOffsetOnAxis(
                            ap=z_sb[:, b:b + 1].bitcast(U32), axis=0)).then_inc(s_emb, 16)

                @block.tensor
                def _(pe):
                    pe.wait_ge(s_emb, 16 * NB)
                    for b in range(NB):
                        if b >= 2:
                            pe.wait_ge(s_eTc, b - 1)
                        nc.tensor.transpose(pt[:, b % 2, 0:P], emb_n[:, b, :], ident[:, :]).then_inc(s_eT, 1)
                        pe.wait_ge(s_eTc, b + 1)
                        if b >= 2:
                            pe.wait_ge(s_qc, b - 1)
                        nc.tensor.matmul(pq[:, b % 2, 0:G], eT[:, b % 2, :], awT[:, :]).then_inc(s_q, 1)

                @block.vector
                def _(dve):
                    nc.vector.tensor_copy(dst_n[:, :, H:H + 1], mult[:, :].unsqueeze(2))
                    for b in range(NB):
                        dve.wait_ge(s_eT, b + 1)
                        if b >= 2:
                            dve.wait_ge(s_q, b - 1)
                        nc.vector.tensor_copy(eT[:, b % 2, :], pt[:, b % 2, 0:P]).then_inc(s_eTc, 1)
                        dve.wait_ge(s_q, b + 1)
                        nc.vector.tensor_copy(dst_n[:, b, H + 1:WD], pq[:, b % 2, 0:G]).then_inc(s_qc, 1)

        def cutoff(name, block, ew, cw, s_ready):
            s_arg, s_sin = sem(name + "_arg"), sem(name + "_sin")

            def vector(dve):
                nc.vector.tensor_scalar(cw[:, :], ew[:, :], CUTOFF, None, ALU.min).then_inc(s_arg, 1)
                dve.wait_ge(s_sin, 1)
                nc.vector.tensor_scalar(ew[:, :], ew[:, :], CUTOFF, None, ALU.is_lt)
                nc.vector.tensor_scalar(cw[:, :], cw[:, :], 1.0, 0.5, ALU.add, ALU.mult)
                nc.vector.drain()
                nc.vector.tensor_tensor(cw[:, :], cw[:, :], ew[:, :], ALU.mult)

            @block.scalar
            def _(act):
                act.wait_ge(s_arg, 1)
                nc.scalar.activation(cw[:, :], cw[:, :], ACT.Sin, bias=halfpi[0:SP_, :], scale=-pi / CUTOFF).then_inc(s_sin, 1)
            return vector

        def index_edges():
            with ExitStack() as c:
                src_sb = sb("src_sb", [SP_, ST], I32, c)
                dst_sb = sb("dst_sb", [SP_, ST], I32, c)
                next_d = sb("next_d", [SP_, 1], I32, c)
                key_sb = sb("key_sb", [SP_, ST], I32, c)
                ew = sb("ew", [SP_, ST], F32, c)
                cw = sb("cw", [SP_, ST], F32, c)
                first_i = sb("first_i", [P, SP_], I32, c)
                first = sb("first", [P, SP_], F32, c)
                junk = sb("junk", [P, SP_], F32, c)
                bound_i = sb("bound_i", [P, QC], I32, c)
                bound = sb("bound", [P, QC], F32, c)
                row = sb("row", [P, QC], F32, c)
                row_u = sb("row_u", [P, QC], U32, c)
                cnt = sb("cnt", [P, QC], F32, c)
                got = sb("got", [P, 2, ST], I32, c)
                gotf = sb("gotf", [P, ST], F32, c)
                gotj = sb("gotj", [P, ST], F32, c)
                bad = sb("bad", [P, 2], F32, c)
                pair = sb("pair", [SP_, ST], F32, c)
                clamp = sb("clamp", [1, ND * GB], F32, c)
                clampd = sb("clampd", [1, ND], F32, c)
                over = sb("over", [1, ND * GB], F32, c)
                bad_row = ps("bad_row", [1, 512], c=c)
                s_ld, s_first, s_io, s_row, s_got = sem("i_ld"), sem("i_first"), sem("i_io"), sem("i_row"), [sem("i_got0"), sem("i_got1")]
                s_st, s_key, s_stT, s_back, s_cwr = sem("i_st"), sem("i_key"), sem("i_stT"), sem("i_back"), sem("i_cwr")
                s_bad, s_badT, s_gotd = sem("i_bad"), sem("i_badT"), sem("i_gotd")
                with nc.Block() as block:
                    cut = cutoff("icut", block, ew, cw, None)

                    @block.sync
                    def _(sp):
                        with nc.allow_non_contiguous_dma(reason="one word per row of edges"):
                            sp.dma_start(first_i[:, :], dst.rearrange("(o p j) -> o p j", o=1, j=ST)[:, :, 0].to_broadcast([P, SP_])).then_inc(s_first, 16)
                            sp.dma_start(next_d[0:SP_ - 1, :], dst[ST:E].rearrange("(p j) -> p j", j=ST)[:, 0:1]).then_inc(s_ld, 16)
                        sp.dma_start(dst_sb[:, :], dst.rearrange("(p j) -> p j", p=SP_)).then_inc(s_ld, 16)
                        sp.dma_start(src_sb[:, :], src.rearrange("(p j) -> p j", p=SP_)).then_inc(s_ld, 16)
                        sp.dma_start(ew[:, :], edge_weight.rearrange("(p j) -> p j", p=SP_)).then_inc(s_ld, 16)
                        sp.wait_ge(s_stT, 1)
                        with nc.allow_non_contiguous_dma(reason="a few words"):
                            sp.dma_start(startT.rearrange("(c p) -> p c", p=P), cnt[:, :]).then_inc(s_st, 16)
                        sp.wait_ge(s_st, 16)
                        sp.dma_start(start_row[:, :], startT.rearrange("(o n) -> o n", o=1)).then_inc(s_back, 16)
                        sp.wait_ge(s_key, 1)
                        sp.dma_start(keyT.rearrange("(p j) -> p j", p=SP_), key_sb[:, :]).then_inc(s_st, 16)
                        sp.wait_ge(s_cwr, 1)
                        sp.dma_start(cwT.rearrange("(p j) -> p j", p=SP_), cw[:, :]).then_inc(s_st, 16)
                        sp.wait_ge(s_st, 48)
                        sp.wait_ge(s_back, 16)

                    @block.gpsimd
                    def _(pool):
                        nc.gpsimd.iota(bound_i[:, :], pattern=[[GR * P, QC]], base=0, channel_multiplier=GR).then_inc(s_io, 1)
                        pool.wait_ge(s_row, 1)
                        for n in range(QC):
                            if n >= 2:
                                pool.wait_ge(s_gotd, n - 1)
                            pool.indirect_dma_start(got[:, n % 2, :], None, dst.rearrange("(p j) -> p j", p=SP_),
                                                    bass.IndirectOffsetOnAxis(ap=row_u[:, n:n + 1], axis=0)).then_inc(s_got[n % 2], 16)

                    @block.tensor
                    def _(pe):
                        pe.wait_ge(s_bad, 1)
                        nc.tensor.matmul(bad_row[:, 0:2], ones[:, 0:1], bad[:, :]).then_inc(s_badT, 1)

                    @block.vector
                    def _(dve):
                        nc.vector.memset(bad[:, :], 0.0)
                        dve.wait_ge(s_io, 1)
                        nc.vector.tensor_copy(bound[:, :], bound_i[:, :])
                        dve.wait_ge(s_first, 16)
                        nc.vector.tensor_copy(first[:, :], first_i[:, :])
                        nc.vector.drain()
                        for n in range(QC):
                            nc.vector.tensor_scalar(junk[:, :], first[:, :], bound[:, n:n + 1], None, ALU.is_lt, ALU.add,
                                                    accum_out=row[:, n:n + 1])
                            nc.vector.drain()
                        nc.vector.tensor_scalar(row[:, :], row[:, :], -1.0, 0.0, ALU.add, ALU.max)
                        nc.vector.drain()
                        nc.vector.tensor_copy(row_u[:, :], row[:, :]).then_inc(s_row, 1)
                        dve.wait_ge(s_ld, 64)
                        nc.vector.scalar_tensor_tensor(key_sb[:, :], dst_sb[:, :], 13, src_sb[:, :], ALU.logical_shift_left,
                                                       ALU.bitwise_or).then_inc(s_key, 1)
                        cut(dve)
                        nc.vector.drain().then_inc(s_cwr, 1)
                        nc.vector.tensor_tensor(pair[:, 0:ST - 1], dst_sb[:, 0:ST - 1], dst_sb[:, 1:ST], ALU.is_gt)
                        nc.vector.tensor_tensor(bad[0:SP_ - 1, 1:2], dst_sb[0:SP_ - 1, ST - 1:ST], next_d[0:SP_ - 1, :], ALU.is_gt)
                        nc.vector.drain()
                        nc.vector.tensor_reduce(bad[0:SP_, 0:1], pair[:, 0:ST - 1], AX, ALU.max)
                        nc.vector.drain().then_inc(s_bad, 1)
                        for n in range(QC):
                            dve.wait_ge(s_got[n % 2], 16 * (n // 2) + 16)
                            nc.vector.tensor_copy(gotf[:, :], got[:, n % 2, :]).then_inc(s_gotd, 1)
                            nc.vector.drain()
                            nc.vector.tensor_scalar(gotj[:, :], gotf[:, :], bound[:, n:n + 1], None, ALU.is_lt, ALU.add,
                                                    accum_out=cnt[:, n:n + 1])
                            nc.vector.drain()
                        nc.vector.scalar_tensor_tensor(cnt[:, :], row[:, :], float(ST), cnt[:, :], ALU.mult, ALU.add)
                        nc.vector.drain().then_inc(s_stT, 1)
                        dve.wait_ge(s_back, 16)
                        nc.vector.tensor_scalar(clamp[:, :], start_row[:, 0:ND * GB], float(E - GE), None, ALU.min)
                        blocks = start_row[:, 0:ND * GB].rearrange("o (d g) -> o d g", g=GB)
                        nc.vector.tensor_scalar(clampd[:, :], blocks[:, :, 0], float(E - WE), None, ALU.min)
                        nc.vector.drain()
                        nc.vector.tensor_copy(group_at[:, :], clamp[:, :])
                        nc.vector.tensor_copy(block_at[:, :], clampd[:, :])
                        nc.vector.tensor_tensor(over[:, :], start_row[:, 1:ND * GB + 1], clamp[:, :], ALU.subtract)
                        nc.vector.drain()
                        nc.vector.tensor_reduce(flags[:, 0:1], over[:, :], AX, ALU.max)
                        nc.vector.drain()
                        nc.vector.tensor_tensor(over[:, 0:ND], start_row[:, GB:ND * GB + 1].rearrange("o (d g) -> o d g", g=GB)[:, :, 0]
                                                if False else start_row[:, GB:GB + (ND - 1) * GB + 1:GB], clampd[:, :], ALU.subtract)
                        nc.vector.drain()
                        nc.vector.tensor_reduce(flags[:, 1:2], over[:, 0:ND], AX, ALU.max)
                        nc.vector.drain()
                        nc.vector.tensor_scalar(flags[:, 0:1], flags[:, 0:1], float(GE), None, ALU.is_gt)
                        nc.vector.tensor_scalar(flags[:, 1:2], flags[:, 1:2], float(WE), None, ALU.is_gt)
                        dve.wait_ge(s_badT, 1)
                        nc.vector.tensor_reduce(flags[:, 2:3], bad_row[:, 0:2], AX, ALU.add)

        def adjacency():
            NBAT = 8
            BT = 2 * GT
            with ExitStack() as c:
                kw = sb("kw", [P, 2, GB * GT], I32, c)
                b_i = sb("b_i", [P, GB * GT], I32, c)
                s_i = sb("s_i", [P, GB * GT], I32, c)
                d_i = sb("d_i", [P, GB * GT], I32, c)
                b_f = sb("b_f", [P, GB * GT], F32, c)
                dl = sb("dl", [P, GB * GT], F32, c)
                lo = sb("lo", [P, GB * GT], F32, c)
                hi = sb("hi", [P, GB * GT], F32, c)
                k2 = sb("k2", [P, GB * GT], F32, c)
                gofs_i = sb("gofs_i", [P, GB * GT], I32, c)
                gofs = sb("gofs", [P, GB * GT], F32, c)
                dbase = sb("dbase", [P, 1], F32, c)
                io_i = sb("io_i", [P, KG], I32, c)
                io_k = sb("io_k", [P, KG], F16, c)
                io_b = sb("io_b", [P, P], BF16, c)
                ohb = sb("ohb", [P, 2, BT, P], BF16, c)
                ohk = sb("ohk", [P, 2, BT, KG], BF16, c)
                adj = sb("adj", [P, 2, NB, P], BF16, c)
                zero = sb("zero", [P, 6250], F32, c)
                pA = ps("pA", [P, 4, 512], c=c)
                pD = ps("pD", [P, 512], c=c)
                s_io, s_ioc, s_z, s_zd = sem("a_io"), sem("a_ioc"), sem("a_z"), sem("a_zd")
                s_kw = [sem("a_kw0"), sem("a_kw1")]
                s_fld, s_ch, s_oh, s_grp, s_ev = sem("a_fld"), sem("a_ch"), sem("a_oh"), sem("a_grp"), sem("a_ev")
                s_st = [sem("a_st0"), sem("a_st1")]
                s_deg, s_spgo = sem("a_deg"), sem("a_spgo")
                per = SLOTS * PW // P // 6250
                flat = slotT.rearrange("(p r) w -> p (r w)", p=P)
                ZN = flat.shape[1]
                NCH = 10
                with nc.Block() as block:
                    @block.sync
                    def _(sp):
                        with sp.Fori(0, ND // 2) as it:
                            for u in range(2):
                                sp.wait_ge(s_fld, 2 * it + u + 1)
                                sp.sem_inc(s_spgo, 1)
                                for g in range(GB):
                                    at = sp.value_load(group_at[0:1, bass.ds((2 * it + u) * GB + g, 1)], min_val=0, max_val=E - GE)
                                    sp.dma_start(kw[:, u, g * GT:(g + 1) * GT],
                                                 keyT[bass.ds(at, GE)].rearrange("(p j) -> p j", p=P)).then_inc(s_kw[u], 16)

                    @block.gpsimd
                    def _(pool):
                        nc.gpsimd.iota(io_i[:, :], pattern=[[1, KG]], base=0, channel_multiplier=0).then_inc(s_io, 1)
                        nc.gpsimd.iota(gofs_i[:, :], pattern=[[GR, GB], [0, GT]], base=0, channel_multiplier=0).then_inc(s_io, 1)
                        pool.wait_ge(s_z, 1)
                        for a in range(0, ZN, 6250):
                            z = min(6250, ZN - a)
                            pool.dma_start(flat[:, a:a + z], zero[:, 0:z]).then_inc(s_zd, 16)
                        pool.wait_ge(s_zd, 16 * -(-ZN // 6250))

                    @block.vector
                    def _(dve):
                        nc.vector.memset(zero[:, :], 0.0).then_inc(s_z, 1)
                        dve.wait_ge(s_io, 2)
                        nc.vector.tensor_copy(io_k[:, :], io_i[:, :])
                        nc.vector.tensor_copy(io_b[:, :], io_i[:, 0:P])
                        nc.vector.tensor_copy(gofs[:, :], gofs_i[:, :])
                        nc.vector.memset(dbase[:, :], 0.0)
                        nc.vector.drain()
                        dve.sem_inc(s_fld, 2)
                        with dve.Fori(0, ND // 2) as it:
                            for u in range(2):
                                D = 2 * it + u
                                step = Chain(dve, s_ch, D * 5)
                                dve.wait_ge(s_kw[u], it * (16 * GB) + 16 * GB)
                                nc.vector.tensor_scalar(b_i[:, :], kw[:, u, :], P - 1, None, ALU.bitwise_and)
                                nc.vector.tensor_scalar(s_i[:, :], kw[:, u, :], 7, 63, ALU.logical_shift_right, ALU.bitwise_and)
                                step(nc.vector.tensor_scalar(d_i[:, :], kw[:, u, :], 13, None, ALU.logical_shift_right))
                                dve.sem_inc(s_fld, 1)
                                nc.vector.tensor_copy(b_f[:, :], b_i[:, :])
                                step(nc.vector.scalar_tensor_tensor(dl[:, :], d_i[:, :], dbase[:, :], gofs[:, :], ALU.subtract, ALU.subtract))
                                nc.vector.tensor_scalar(lo[:, :], dl[:, :], 0.0, DROP, ALU.is_lt, ALU.mult)
                                nc.vector.tensor_scalar(hi[:, :], dl[:, :], GR - 0.5, DROP, ALU.is_gt, ALU.mult)
                                nc.vector.tensor_scalar(dbase[:, :], dbase[:, :], float(P), None, ALU.add)
                                step(nc.vector.scalar_tensor_tensor(k2[:, :], s_i[:, :], float(GR), dl[:, :], ALU.mult, ALU.add))
                                step(nc.vector.tensor_tensor(k2[:, :], k2[:, :], lo[:, :], ALU.add))
                                step(nc.vector.tensor_tensor(k2[:, :], k2[:, :], hi[:, :], ALU.add))
                                for b in range(NBAT):
                                    dve.wait_ge(s_grp, D * GB + 2 * b + 2)
                                    for j in range(BT):
                                        t = b * BT + j
                                        nc.vector.tensor_scalar(ohb[:, b % 2, j, :], io_b[:, :], b_f[:, t:t + 1], None, ALU.is_equal)
                                        last = nc.vector.tensor_scalar(ohk[:, b % 2, j, :], io_k[:, :], k2[:, t:t + 1], None, ALU.is_equal)
                                    last.then_inc(s_oh, 1)
                        dve.wait_ge(s_deg, ND + 2)
                        nc.vector.tensor_copy(deg[:, :], pD[:, 0:2 * ND:2])

                    @block.tensor
                    def _(pe):
                        pe.sem_inc(s_grp, 4)
                        with pe.Fori(0, ND // 2) as it:
                            for u in range(2):
                                D = 2 * it + u
                                for b in range(NBAT):
                                    pe.wait_ge(s_oh, D * NBAT + b + 1)
                                    for g in range(2):
                                        n = 2 * b + g
                                        pe.wait_ge(s_ev, D * GB + n + 1)
                                        for j in range(GT):
                                            m = nc.tensor.matmul(pA[:, n % 4, 0:KG], ohb[:, b % 2, g * GT + j, :], ohk[:, b % 2, g * GT + j, :],
                                                                 start=j == 0, stop=j == GT - 1)
                                        m.then_inc(s_grp, 1)
                                pe.wait_ge(s_ev, D * GB + GB + 4)
                                for n in range(NB):
                                    m = nc.tensor.matmul(pD[:, bass.ds(2 * D, 2)], adj[:, u, n, :], ones_b[:, :], start=n == 0, stop=n == NB - 1)
                                m.then_inc(s_deg, 1)

                    @block.scalar
                    def _(act):
                        act.wait_ge(s_z, 1)
                        for u in range(2):
                            act.dma_start(adjT[u, :, 0:P], zero[:, 0:P // 2].bitcast(BF16)).then_inc(s_st[u], 16)
                        act.sem_inc(s_ev, 4)
                        act.sem_inc(s_deg, 2)
                        with act.Fori(0, ND // 2) as it:
                            for u in range(2):
                                D = 2 * it + u
                                for n in range(GB):
                                    act.wait_ge(s_grp, D * GB + n + 5)
                                    if n == 0:
                                        act.wait_ge(s_st[u], it * 16 + 16)
                                        act.wait_ge(s_deg, D + 1)
                                    nc.scalar.activation(adj[:, u, :, n * GR:(n + 1) * GR],
                                                         pA[:, n % 4, 0:KG].rearrange("p (s d) -> p s d", d=GR), ACT.Copy).then_inc(s_ev, 1)
                                act.wait_ge(s_ev, D * GB + GB + 4)
                                act.dma_start(adjT[bass.ds(D, 1), :, :].rearrange("o p f -> p (o f)"),
                                              adj[:, u, :, :].rearrange("p s d -> p (s d)")).then_inc(s_st[u], 16)
                        for u in range(2):
                            act.wait_ge(s_st[u], 16 * (ND // 2 + 1))

        def split(dve, parts, rest, step):
            step(nc.vector.tensor_scalar(parts[0], rest, 1.0, None, ALU.mult))
            step(nc.vector.tensor_tensor(rest, rest, parts[0], ALU.subtract))
            step(nc.vector.tensor_scalar(parts[1], rest, 1.0, None, ALU.mult))
            step(nc.vector.tensor_tensor(parts[2], rest, parts[1], ALU.subtract))

        def propagate(h_all):
            MD = 5
            NM = ND // MD
            assert NM * STEPS == ND
            CT = 8
            chunks = [(a, min(a + CT, WT)) for a in range(0, WT, CT)]
            subs = [(a, min(a + 4, WT)) for a in range(0, WT, 4)]
            NS = len(subs)
            assert len(chunks) == MD
            halves = [(0, 3), (3, 5)]
            with ExitStack() as c:
                adj = sb("p_adj", [P, MD, NB * P], BF16, c)
                parts = sb("p_parts", [P, NB, 3, H], BF16, c)
                nparts = sb("p_nparts", [P, ND, 3, H], BF16, c)
                x08 = sb("p_x08", [P, ND, H], F32, c)
                g_all = sb("p_g", [P, ND, H], F32, c)
                dinv = sb("p_dinv", [P, ND], F32, c)
                dinv02 = sb("p_dinv02", [P, ND], F32, c)
                root = sb("p_root", [P, ND], F32, c)
                rest = sb("p_rest", [P, 3, H], F32, c)
                acc = sb("p_acc", [P, 3, H], F32, c)
                kwin = sb("p_kwin", [P, WT], I32, c)
                cwin = sb("p_cwin", [P, WT], F32, c)
                attr = sb("p_attr", [P, WT, R], F32, c)
                attrT = sb("p_attrT", [R, 4, P], F32, c)
                hid = sb("p_hid", [H + 1, 4, P], F32, c)
                f_i = sb("p_fi", [P, 4, WT], I32, c)
                meta = sb("p_meta", [P, WT, 4], F32, c)
                inv = sb("p_inv", [P, WT], F32, c)
                sx = sb("p_sx", [P, WT], F32, c)
                sxb = sb("p_sxb", [P, WT], BF16, c)
                dcol = sb("p_dcol", [P, 1], F32, c)
                base = sb("p_base", [P, 1], F32, c)
                io_i = sb("p_ioi", [P, NB, WT], I32, c)
                io_s = sb("p_ios", [P, NB, WT], BF16, c)
                cont = sb("p_cont", [P, NB, WT], BF16, c)
                oh = sb("p_oh", [P, NB, WT], BF16, c)
                run = sb("p_run", [P, NB, WT], BF16, c)
                tot = sb("p_tot", [P, NB], BF16, c)
                rk = sb("p_rk", [P, NB, WT], F32, c)
                rank = sb("p_rank", [P, WT], F32, c)
                rmax = sb("p_rmax", [P, 1], F32, c)
                rtop = sb("p_rtop", [P, 1], F32, c)
                pos = sb("p_pos", [P, WT], F32, c)
                slot = sb("p_slot", [P, WT], U32, c)
                pay = sb("p_pay", [P, WT, PW], F32, c)
                pL = ps("pL", [P, 2, 512], c=c)
                pT = ps("pT", [P, 512], c=c)
                pH = ps("pH", [P, 512], c=c)
                pG = ps("pG", [P, 2, 512], c=c)
                pR = ps("pR", [P, 512], c=c)
                seed = dram("seed", [P, 4])
                s_io, s_init, s_dv, s_ds = sem("p_io"), sem("p_init"), sem("p_dv"), sem("p_ds")
                s_A = [sem(f"p_A{q}") for q in range(MD)]
                s_pz = sem("p_pz")
                s_upd = [sem("p_upd0"), sem("p_upd1")]
                s_gp = sem("p_gp")
                s_kf, s_win, s_attr = sem("p_kf"), sem("p_win"), sem("p_attr")
                s_T, s_aT, s_h, s_hid, s_g = sem("p_T"), sem("p_aT"), sem("p_h"), sem("p_hid"), sem("p_g")
                s_pay, s_free, s_go = sem("p_pay"), sem("p_free"), sem("p_go")
                s_sc = [sem(f"p_sc{q}") for q in range(MD)]
                s_tot, s_off, s_ch, s_gone, s_spgo = sem("p_tot"), sem("p_off"), sem("p_ch"), sem("p_gone"), sem("p_spgo")
                wide = lambda a, n: a.unsqueeze(2).to_broadcast([P, n, H])
                NCH = 36

                with nc.Block() as block:
                    @block.sync
                    def _(sp):
                        with sp.Fori(0, STEPS) as k:
                            with sp.Fori(0, NM) as m:
                                it = k * NM + m
                                for q in range(MD):
                                    sp.wait_ge(s_pz, it * MD + q + 1)
                                    sp.sem_inc(s_spgo, 1)
                                    sp.dma_start(adj[:, q, :], adjT[bass.ds(m * MD + q, 1), :, :].rearrange("o p f -> p (o f)")).then_inc(s_A[q], 16)
                                    if q == 0:
                                        at = sp.value_load(block_at[0:1, bass.ds(it, 1)], min_val=0, max_val=E - WE)
                                        sp.wait_ge(s_kf, it + 1)
                                        sp.sem_inc(s_spgo, 1)
                                        sp.dma_start(kwin[:, :], keyT[bass.ds(at, WE)].rearrange("(p j) -> p j", p=P)).then_inc(s_win, 16)
                                        sp.dma_start(cwin[:, :], cwT[bass.ds(at, WE)].rearrange("(p j) -> p j", p=P)).then_inc(s_win, 16)
                                        sp.wait_ge(s_T, it * NS + NS)
                                        sp.sem_inc(s_spgo, 1)
                                        sp.dma_start(attr[:, :, :], edge_attr[bass.ds(at, WE), :].rearrange("(p j) f -> p j f", p=P)).then_inc(s_attr, 16)

                    @block.gpsimd
                    def _(pool):
                        nc.gpsimd.iota(io_i[:, :, :], pattern=[[1, NB], [0, WT]], base=0, channel_multiplier=0).then_inc(s_io, 1)
                        pool.wait_ge(s_init, 1)
                        last_n = chunks[-1][1] - chunks[-1][0]
                        for n in range(last_n):
                            pool.dma_start(seed[:, n:n + 1] if False else seed, ones[:, 0:4]).then_inc(s_sc[MD - 1], 16)
                            pool.wait_ge(s_sc[MD - 1], 16 * n + 16)
                        pool.sem_inc(s_free, MD - 1)
                        with pool.Fori(0, ND) as it:
                            for q, (a, b) in enumerate(chunks):
                                pool.wait_ge(s_pay, it * MD + q + 3)
                                pool.sem_inc(s_go, 1)
                                for t in range(a, b):
                                    pool.indirect_dma_start(slotT, bass.IndirectOffsetOnAxis(ap=slot[:, t:t + 1], axis=0), pay[:, t, :], None,
                                                            bounds_check=SLOTS - 1, oob_is_err=False).then_inc(s_sc[q], 16)
                                w = (q - 1) % MD
                                n = 16 * (chunks[w][1] - chunks[w][0])
                                pool.wait_ge(s_sc[w], it * n + n)
                                pool.sem_inc(s_free, 1)
                        pool.wait_ge(s_sc[MD - 1], 16 * last_n * (ND + 1))

                    @block.tensor
                    def _(pe):
                        pe.sem_inc(s_pz, MD)
                        pe.sem_inc(s_T, NS)
                        pe.sem_inc(s_h, 1)
                        pe.sem_inc(s_g, 1)
                        with pe.Fori(0, STEPS) as k:
                            pe.wait_ge(s_gp, k + 1)
                            pe.sem_inc(s_gone, 1)
                            with pe.Fori(0, NM) as m:
                                it = k * NM + m
                                for q in range(MD):
                                    def transposes(s):
                                        a, b = subs[s]
                                        if s == 0:
                                            pe.wait_ge(s_attr, it * 16 + 16)
                                            pe.sem_inc(s_gone, 1)
                                        pe.wait_ge(s_aT, it * NS + s + 1)
                                        pe.sem_inc(s_gone, 1)
                                        for t in range(a, b):
                                            x_ = nc.tensor.transpose(pT[0:R, (t - a) * P:(t - a + 1) * P], attr[:, t, :], ident[:, :])
                                        x_.then_inc(s_T, 1)

                                    def hidden(s):
                                        a, b = subs[s]
                                        pe.wait_ge(s_aT, it * NS + s + 2)
                                        pe.wait_ge(s_hid, it * NS + s + 1)
                                        pe.sem_inc(s_gone, 1)
                                        nc.tensor.matmul(pH[0:H, 0:(b - a) * P], w1T[:, :],
                                                         attrT[:, 0:b - a, :].rearrange("r t e -> r (t e)")).then_inc(s_h, 1)

                                    def gates(s):
                                        a, b = subs[s]
                                        pe.wait_ge(s_hid, it * NS + s + 2)
                                        if s % 2 == 0:
                                            pe.wait_ge(s_pay, it * MD + (q + 1 if q >= 2 else 2 - q))
                                        pe.sem_inc(s_gone, 1)
                                        for t in range(a, b):
                                            o = t - chunks[q][0]
                                            x_ = nc.tensor.matmul(pG[:, q % 2, o * H:(o + 1) * H], hid[:, t - a, :], w2T[:, :])
                                        x_.then_inc(s_g, 1)

                                    half = 0 if q < 3 else 1
                                    o = q - halves[half][0]

                                    def product(a, b):
                                        for n in range(a, b):
                                            x_ = nc.tensor.matmul(pL[:, half, o * H3:(o + 1) * H3], adj[:, q, n * P:(n + 1) * P],
                                                                  parts[:, n, :, :].rearrange("p t f -> p (t f)"), start=n == 0, stop=n == NB - 1)
                                        if b == NB:
                                            x_.then_inc(s_pz, 1)
                                    two = 2 * q + 1 < NS
                                    transposes(2 * q)
                                    pe.wait_ge(s_A[q], it * 16 + 16)
                                    if o == 0:
                                        pe.wait_ge(s_upd[half], it + 1)
                                    product(0, 13)
                                    hidden(2 * q)
                                    if two:
                                        transposes(2 * q + 1)
                                    product(13, 25)
                                    gates(2 * q)
                                    if two:
                                        hidden(2 * q + 1)
                                    product(25, 37)
                                    if two:
                                        gates(2 * q + 1)
                                    if q == 0:
                                        pe.wait_ge(s_tot, it + 1)
                                        nc.tensor.matmul(pR[:, 0:NB], above_b[:, :], tot[:, :]).then_inc(s_off, 1)
                                    product(37, NB)

                    @block.scalar
                    def _(act):
                        act.wait_ge(s_dv, 1)
                        nc.scalar.activation(root[:, :], root[:, :], ACT.Sqrt).then_inc(s_ds, 1)
                        nc.scalar.activation(hid[:, :, :].rearrange("h t e -> h (t e)"),
                                             ones[0:H + 1, 0:1].to_broadcast([H + 1, 4 * P]), ACT.Copy).then_inc(s_hid, 1)
                        act.wait_ge(s_hid, 1)
                        act.sem_inc(s_aT, 1)
                        with act.Fori(0, ND) as it:
                            for s, (a, b) in enumerate(subs):
                                act.wait_ge(s_T, it * NS + s + 1 + NS)
                                act.wait_ge(s_h, it * NS + s + 1)
                                nc.scalar.activation(attrT[:, 0:b - a, :].rearrange("r t e -> r (t e)"), pT[0:R, 0:(b - a) * P], ACT.Copy).then_inc(s_aT, 1)
                                act.wait_ge(s_h, it * NS + s + 2)
                                act.wait_ge(s_g, it * NS + s + 1)
                                nc.scalar.activation(hid[0:H, 0:b - a, :].rearrange("h t e -> h (t e)"), pH[0:H, 0:(b - a) * P],
                                                     ACT.Silu, bias=b1c[:, :]).then_inc(s_hid, 1)

                    @block.vector
                    def _(dve):
                        nc.vector.tensor_scalar(root[:, :], deg[:, :], 1.0, None, ALU.add).then_inc(s_dv, 1)
                        nc.vector.memset(x08[:, ND - 1, :], 0.0)
                        nc.vector.memset(g_all[:, ND - 1, :], 0.0)
                        nc.vector.memset(pay[:, :, :], 0.0)
                        nc.vector.memset(slot[:, :], 0)
                        nc.vector.memset(meta[:, :, 0:1], 1.0)
                        nc.vector.memset(cont[:, :, :], 1.0)
                        nc.vector.memset(dcol[:, :], 0.0)
                        nc.vector.memset(rtop[:, :], 0.0)
                        nc.vector.memset(base[:, :], float(-NB))
                        nc.vector.tensor_scalar(x08[:, 0:NB, :], x_sb[:, :, :], ALPHA, None, ALU.mult)
                        dve.wait_ge(s_ds, 1)
                        nc.vector.drain()
                        nc.vector.memset(cont[:, :, 0:1], 0.0)
                        nc.vector.reciprocal(dinv[:, :], root[:, :])
                        nc.vector.drain()
                        nc.vector.tensor_scalar(dinv02[:, :], dinv[:, :], 1.0 - ALPHA, None, ALU.mult)
                        nc.vector.tensor_tensor(g_all[:, 0:NB, :], x_sb[:, :, :], wide(dinv[:, 0:NB], NB), ALU.mult)
                        nc.vector.drain()
                        nc.vector.tensor_copy(h_all[:, :, :], g_all[:, :, :])
                        nc.vector.drain()
                        split(dve, [parts[:, :, t, :] for t in range(3)], h_all[:, 0:NB, :], lambda i: nc.vector.drain())
                        nc.vector.drain().then_inc(s_gp, 1)
                        dve.wait_ge(s_io, 1)
                        nc.vector.tensor_copy(io_s[:, :, :], io_i[:, :, :])
                        nc.vector.drain().then_inc(s_init, 1)
                        dve.sem_inc(s_kf, 1)
                        dve.sem_inc(s_pay, 2)
                        dve.sem_inc(s_upd[0], 1)
                        dve.sem_inc(s_upd[1], 1)

                        def update(it, m, step, half):
                            a, b = halves[half]
                            n = b - a
                            at = bass.ds(m * MD + a, n)
                            dve.wait_ge(s_pz, it * MD + b + MD)
                            step(nc.vector.tensor_reduce(acc[:, 0:n, :], pL[:, half, 0:n * H3].rearrange("p (d t f) -> p d f t", t=3, f=H), AX, ALU.add))
                            dve.sem_inc(s_upd[half], 1)
                            step(nc.vector.tensor_tensor(acc[:, 0:n, :], acc[:, 0:n, :], g_all[:, at, :], ALU.add))
                            step(nc.vector.tensor_tensor(acc[:, 0:n, :], acc[:, 0:n, :], wide(dinv02[:, at], n), ALU.mult))
                            step(nc.vector.tensor_tensor(h_all[:, at, :], acc[:, 0:n, :], x08[:, at, :], ALU.add))
                            step(nc.vector.tensor_tensor(rest[:, 0:n, :], h_all[:, at, :], wide(dinv[:, at], n), ALU.mult))
                            nc.vector.tensor_scalar(g_all[:, at, :], rest[:, 0:n, :], 1.0, None, ALU.mult)
                            split(dve, [nparts[:, at, t, :] for t in range(3)], rest[:, 0:n, :], step)

                        def ranks(it, step):
                            dve.wait_ge(s_win, it * 32 + 32)
                            nc.vector.tensor_copy(meta[:, :, 1:2], cwin[:, :].unsqueeze(2))
                            nc.vector.tensor_scalar(f_i[:, 0, :], kwin[:, :], 7, 63, ALU.logical_shift_right, ALU.bitwise_and)
                            nc.vector.tensor_scalar(f_i[:, 1, :], kwin[:, :], 20, None, ALU.logical_shift_right)
                            nc.vector.tensor_scalar(f_i[:, 2, :], kwin[:, :], P - 1, None, ALU.bitwise_and)
                            step(nc.vector.tensor_scalar(f_i[:, 3, :], kwin[:, :], 13, P - 1, ALU.logical_shift_right, ALU.bitwise_and))
                            dve.sem_inc(s_kf, 1)
                            nc.vector.tensor_scalar(meta[:, :, 2:4], f_i[:, 2:4, :].rearrange("p c t -> p t c"), 1.0, None, ALU.add)
                            step(nc.vector.tensor_scalar(inv[:, :], f_i[:, 1, :], dcol[:, :], DROP, ALU.not_equal, ALU.mult))
                            nc.vector.tensor_scalar(dcol[:, :], dcol[:, :], 1.0, None, ALU.add)
                            step(nc.vector.tensor_tensor(sx[:, :], inv[:, :], f_i[:, 0, :], ALU.add))
                            step(nc.vector.tensor_copy(sxb[:, :], sx[:, :]))
                            step(nc.vector.tensor_tensor(oh[:, :, :], io_s[:, :, :], sxb[:, :].unsqueeze(1).to_broadcast([P, NB, WT]), ALU.is_equal))
                            flat = lambda a: a[:, :, :].rearrange("p s j -> p (s j)")
                            step(nc.vector.tensor_tensor_scan(flat(run), flat(cont), flat(oh), 0.0, ALU.mult, ALU.add))
                            step(nc.vector.tensor_copy(tot[:, :], run[:, :, WT - 1]))
                            dve.sem_inc(s_tot, 1)
                            dve.wait_ge(s_off, it + 1)
                            step(nc.vector.tensor_tensor(rk[:, :, :], run[:, :, :], pR[:, 0:NB].unsqueeze(2).to_broadcast([P, NB, WT]), ALU.add))
                            step(nc.vector.tensor_tensor(rk[:, :, :], rk[:, :, :], oh[:, :, :], ALU.mult))
                            step(nc.vector.tensor_reduce(rank[:, :], rk[:, :, :].rearrange("p s j -> p j s"), AX, ALU.add))
                            nc.vector.tensor_reduce(rmax[:, :], rank[:, :], AX, ALU.max)
                            step(nc.vector.scalar_tensor_tensor(pos[:, :], rank[:, :], float(NB), sx[:, :], ALU.mult, ALU.add))
                            nc.vector.tensor_tensor(rtop[:, :], rtop[:, :], rmax[:, :], ALU.max)
                            step(nc.vector.tensor_scalar(pos[:, :], pos[:, :], base[:, :], None, ALU.add))
                            step(nc.vector.tensor_scalar(base[:, :], base[:, :], float(NB * P), None, ALU.add))

                        def rows_out(it, q, step):
                            a, b = chunks[q]
                            dve.wait_ge(s_g, it * NS + min(2 * q + 2, NS) + 1)
                            dve.wait_ge(s_free, it * MD + q + 1)
                            nc.vector.tensor_copy(pay[:, a:b, H:PW], meta[:, a:b, :])
                            nc.vector.tensor_copy(slot[:, a:b], pos[:, a:b])
                            step(nc.vector.tensor_tensor(pay[:, a:b, 0:H], pG[:, q % 2, 0:(b - a) * H].rearrange("p (t f) -> p t f", f=H),
                                                         wide(meta[:, a:b, 1], b - a), ALU.mult))
                            dve.sem_inc(s_pay, 1)

                        with dve.Fori(0, STEPS) as k:
                            with dve.Fori(0, NM) as m:
                                it = k * NM + m
                                step = Chain(dve, s_ch, it * NCH)
                                ranks(it, step)
                                for q in range(3):
                                    rows_out(it, q, step)
                                update(it, m, step, 0)
                                for q in range(3, MD):
                                    rows_out(it, q, step)
                                update(it, m, step, 1)
                                assert step.n == NCH, step.n
                            nc.vector.tensor_copy(parts[:, :, :, :].rearrange("p s t f -> p (s t f)"),
                                                  nparts[:, 0:NB, :, :].rearrange("p s t f -> p (s t f)"))
                            nc.vector.drain().then_inc(s_gp, 1)

                with nc.Block() as block:
                    rrow = sb("p_rrow", [1, 4], F32, c)
                    s_tr, s_tm = sem("p_tr"), sem("p_tm")

                    @block.tensor
                    def _(pe):
                        nc.tensor.transpose(pT[0:1, 0:P], rtop[:, :], ident[:, :]).then_inc(s_tr, 1)

                    @block.vector
                    def _(dve):
                        dve.wait_ge(s_tr, 1)
                        nc.vector.tensor_reduce(rrow[:, 0:1], pT[0:1, 0:P], AX, ALU.max)
                        nc.vector.drain()
                        nc.vector.tensor_scalar(flags[:, 3:4], rrow[:, 0:1], P + 0.5, None, ALU.is_gt)
                        nc.vector.drain()
                        nc.vector.tensor_reduce(rrow[:, 1:2], flags[:, :], AX, ALU.add)
                        nc.vector.drain()
                        nc.vector.tensor_scalar(rrow[:, 1:2], rrow[:, 1:2], 1.0, None, ALU.min)
                        nc.vector.drain()
                        nc.vector.tensor_copy(flag_i[:, :], rrow[:, 1:2])

        def convolve(agg):
            with ExitStack() as c:
                NCK = NB // CH
                W1c = H + 1
                AHEAD, OHB = 3, 4
                BUF = [0, 1, 2, 0, 1, 2, 0, 1, 2, 3, 0, 1, 2, 3]
                assert len(BUF) == 2 * NCK
                tabp = sb("c_tab", [P, ND, 3, WD], BF16, c)
                embp = sb("c_emb", [P, NB, 3, G], BF16, c)
                big = sb("c_big", [P, NB, WD], F32, c)
                cur = sb("c_cur", [P, 2, 3, WD], BF16, c)
                rows = sb("c_rows", [P, 2, NB, PW], F32, c)
                io_i = sb("c_ioi", [P, P], I32, c)
                io_b = sb("c_iob", [P, P], BF16, c)
                ohd = sb("c_ohd", [P, OHB, CH, P], BF16, c)
                ohs = sb("c_ohs", [P, OHB, CH, P], BF16, c)
                ohs_f = sb("c_ohsf", [P, 2, CH, P], F32, c)
                ohdT = sb("c_ohdT", [P, 2, CH, P], BF16, c)
                ohsT = sb("c_ohsT", [P, 2, CH, P], BF16, c)
                es = sb("c_es", [P, 2, CH, G], F32, c)
                pr = sb("c_pr", [P, CH, G], F32, c)
                ad = sb("c_ad", [P, CH], F32, c)
                ac = sb("c_ac", [P, CH], F32, c)
                gx = sb("c_gx", [P, CH, W1c], F32, c)
                msg = sb("c_msg", [P, 2, CH, W1c], F32, c)
                pD = ps("cD", [P, 1024], BF16, c)
                pS = ps("cS", [P, 1024], BF16, c)
                pG = ps("cG", [P, 2, 8, P], c=c)
                pO = ps("cO", [P, 2, 512], c=c)
                s_io, s_rdy, s_spgo = sem("c_io"), sem("c_rdy"), sem("c_spgo")
                s_rows = [sem("c_rows0"), sem("c_rows1")]
                s_oh, s_T, s_TC, s_conv = sem("c_oh"), sem("c_T"), sem("c_TC"), sem("c_conv")
                s_G, s_ac, s_gx, s_msg, s_O, s_agg = sem("c_G"), sem("c_ac"), sem("c_gx"), sem("c_msg"), sem("c_O"), sem("c_agg")
                s_ch, s_cur, s_done, s_es = sem("c_ch"), sem("c_cur"), sem("c_done"), sem("c_es")
                PAIRS = ND // 2

                def pairs(eng, body):
                    with eng.Fori(0, PAIRS - 1) as it:
                        for k in range(2 * NCK):
                            body(it, k, it * (2 * NCK) + k, False)
                    for k in range(2 * NCK):
                        body(PAIRS - 1, k, (PAIRS - 1) * (2 * NCK) + k, True)

                with nc.Block() as block:
                    @block.sync
                    def _(sp):
                        slots = slotT.rearrange("(d r s) w -> d r (s w)", r=P, s=NB)
                        with sp.Fori(0, PAIRS) as it:
                            for u in range(2):
                                sp.wait_ge(s_done, 2 * it + u + 1)
                                sp.sem_inc(s_spgo, 1)
                                sp.dma_start(rows[:, u, :, :].rearrange("p s w -> p (s w)"),
                                             slots[bass.ds(2 * it + u, 1), :, :].rearrange("o r f -> r (o f)")).then_inc(s_rows[u], 16)

                    @block.gpsimd
                    def _(pool):
                        nc.gpsimd.iota(io_i[:, :], pattern=[[1, P]], base=1, channel_multiplier=0).then_inc(s_io, 1)
                        pool.wait_ge(s_rdy, 1)

                        def body(it, k, i, last):
                            u, ck = divmod(k, NCK)
                            S = slice(ck * CH, (ck + 1) * CH)
                            pool.wait_ge(s_ac, i + 1)
                            nc.gpsimd.tensor_tensor(gx[:, :, 0:H], rows[:, u, S, 0:H], ac[:, :].unsqueeze(2).to_broadcast([P, CH, H]),
                                                    ALU.add).then_inc(s_gx, 1)
                        pairs(pool, body)

                    @block.vector
                    def _(dve):
                        dr = lambda i: nc.vector.drain()
                        nc.vector.memset(tabp[:, ND - 1, :, :], 0.0)
                        nc.vector.memset(agg[:, :, :], 0.0)
                        nc.vector.memset(gx[:, :, :], 1.0)
                        nc.vector.memset(msg[:, 1, :, :], 0.0)
                        nc.vector.memset(ohs_f[:, 1, :, :], 0.0)
                        dve.wait_ge(s_io, 1)
                        nc.vector.tensor_copy(io_b[:, :], io_i[:, :])
                        nc.vector.tensor_copy(big[:, :, :], dst_n[:, :, :])
                        nc.vector.drain()
                        split(dve, [tabp[:, 0:NB, t, :] for t in range(3)], big[:, :, :], dr)
                        nc.vector.drain()
                        nc.vector.tensor_copy(big[:, :, 0:G], emb_n[:, :, :])
                        nc.vector.drain()
                        split(dve, [embp[:, :, t, :] for t in range(3)], big[:, :, 0:G], dr)
                        nc.vector.drain().then_inc(s_rdy, 1)
                        dve.sem_inc(s_done, 2)
                        dve.sem_inc(s_msg, 2)
                        dve.sem_inc(s_agg, 2)

                        def add_sums(k, i):
                            ck, par = (k - 1) % NCK, (k - 1) % 2
                            A = agg[:, ck * CH:(ck + 1) * CH, :]
                            dve.wait_ge(s_O, i + 2)
                            nc.vector.tensor_tensor(A, A, pO[:, par, 0:CH * W1c].rearrange("p (s w) -> p s w", w=W1c), ALU.add).then_inc(s_agg, 1)

                        def onehot(oh, k, col):
                            u, ck = k % (2 * NCK) // NCK, k % NCK
                            for j in range(CH):
                                x_ = nc.vector.tensor_scalar(oh[:, BUF[k % (2 * NCK)], j, :], io_b[:, :],
                                                             rows[:, u, ck * CH + j, col:col + 1], None, ALU.is_equal)
                            return x_

                        dve.wait_ge(s_rows[0], 16)
                        for k in range(AHEAD):
                            onehot(ohd, k, H + 3)
                            onehot(ohs, k, H + 2).then_inc(s_oh, 1)

                        def body(it, k, i, last):
                            u, ck = divmod(k, NCK)
                            par = k % 2
                            k3 = k + AHEAD
                            ahead = not last or k3 < 2 * NCK
                            step = Chain(dve, s_ch, i * 2)
                            g = pG[:, par, 0:CH, :]
                            dve.wait_ge(s_es, i + 1)
                            step(nc.vector.tensor_tensor(pr[:, :, :], es[:, par, :, :], g[:, :, W1c:WD], ALU.mult))
                            step(nc.vector.tensor_reduce(ad[:, :], pr[:, :, :], AX, ALU.add))
                            nc.vector.tensor_tensor(ac[:, :], ad[:, :], rows[:, u, ck * CH:(ck + 1) * CH, H + 1], ALU.mult).then_inc(s_ac, 1)
                            if ahead:
                                if k3 % NCK == 0:
                                    u3 = k3 // NCK % 2
                                    dve.wait_ge(s_rows[u3], (it + k3 // (2 * NCK)) * 16 + 16)
                                dve.wait_ge(s_T, i + 1)
                                dve.wait_ge(s_conv, i + 2)
                                onehot(ohd, k3, H + 3)
                            dve.wait_ge(s_O, i + 1)
                            dve.wait_ge(s_gx, i + 1)
                            nc.vector.tensor_tensor(msg[:, par, :, :], gx[:, :, :], g[:, :, 0:W1c], ALU.mult).then_inc(s_msg, 1)
                            if ck == NCK - 1:
                                dve.sem_inc(s_done, 1)
                            if ahead:
                                onehot(ohs, k3, H + 2).then_inc(s_oh, 1)
                            add_sums(k, i)
                        pairs(dve, body)
                        add_sums(2 * NCK, ND * NCK)

                    @block.scalar
                    def _(act):
                        act.wait_ge(s_rdy, 1)
                        act.sem_inc(s_conv, 1)

                        def load_cur(D, u):
                            nc.scalar.activation(cur[:, u, :, :], tabp[:, D, :, :].rearrange("p o t w -> p (o t) w"), ACT.Copy).then_inc(s_cur, 1)

                        def copies(k):
                            nc.scalar.activation(ohdT[:, k % 2, :, :].rearrange("p s e -> p (s e)"), pD[:, 0:CH * P], ACT.Copy)
                            nc.scalar.activation(ohsT[:, k % 2, :, :].rearrange("p s e -> p (s e)"), pS[:, 0:CH * P], ACT.Copy).then_inc(s_TC, 1)

                        def convert(k):
                            nc.scalar.activation(ohs_f[:, k % 2, :, :], ohs[:, BUF[k % (2 * NCK)], :, :], ACT.Copy).then_inc(s_conv, 1)

                        load_cur(slice(0, 1), 0)
                        act.wait_ge(s_T, 1)
                        copies(0)
                        convert(0)

                        def body(it, k, i, last):
                            u, ck = divmod(k, NCK)
                            end = last and k == 2 * NCK - 1
                            if not end:
                                act.wait_ge(s_T, i + 2)
                                act.wait_ge(s_G, i + 1)
                                copies(k + 1)
                            act.wait_ge(s_G, i + 2)
                            nc.scalar.activation(es[:, k % 2, :, :], pG[:, k % 2, 0:CH, WD:WD + G], ACT.Copy).then_inc(s_es, 1)
                            if end:
                                return
                            if ck == 3 and not (last and u == 1):
                                load_cur(bass.ds(2 * it + u + 1, 1), 1 - u)
                            act.wait_ge(s_O, i + 2)
                            convert(k + 1)
                        pairs(act, body)

                    @block.tensor
                    def _(pe):
                        pe.wait_ge(s_rdy, 1)
                        pe.sem_inc(s_G, 1)
                        pe.sem_inc(s_O, 1)

                        def transposes(k):
                            b = BUF[k % (2 * NCK)]
                            for j in range(CH):
                                nc.tensor.transpose(pD[:, j * P:(j + 1) * P], ohd[:, b, j, :], ident_b[:, :])
                            for j in range(CH):
                                m = nc.tensor.transpose(pS[:, j * P:(j + 1) * P], ohs[:, b, j, :], ident_b[:, :])
                            m.then_inc(s_T, 1)

                        def sums(k, i):
                            pe.wait_ge(s_msg, i + 2)
                            pe.wait_ge(s_conv, i + 1)
                            pe.wait_ge(s_agg, i + 1)
                            par = (k - 1) % 2
                            for j in range(CH):
                                m = nc.tensor.matmul(pO[:, par, j * W1c:(j + 1) * W1c], ohs_f[:, par, j, :], msg[:, par, j, :])
                            m.then_inc(s_O, 1)

                        pe.wait_ge(s_oh, 1)
                        transposes(0)

                        def body(it, k, i, last):
                            u, ck = divmod(k, NCK)
                            par = k % 2
                            if not (last and k == 2 * NCK - 1):
                                pe.wait_ge(s_oh, i + 2)
                                pe.wait_ge(s_TC, i + 1)
                                transposes(k + 1)
                            pe.wait_ge(s_TC, i + 1)
                            if ck == 0:
                                pe.wait_ge(s_cur, 2 * it + u + 1)
                            pe.wait_ge(s_msg, i + 1)
                            for j in range(CH):
                                for t in range(3):
                                    nc.tensor.matmul(pG[:, par, j, 0:WD], ohdT[:, par, j, :], cur[:, u, t, :], start=t == 0, stop=t == 2)
                                for t in range(3):
                                    m = nc.tensor.matmul(pG[:, par, j, WD:WD + G], ohsT[:, par, j, :], embp[:, ck * CH + j, t, :], start=t == 0, stop=t == 2)
                            m.then_inc(s_G, 1)
                            sums(k, i)
                        pairs(pe, body)
                        sums(2 * NCK, ND * NCK)

        def layer_norm_parts(name, t, tmp):
            s_var, s_std = sem(name + "_var"), sem(name + "_std")
            wide = lambda a: a[:, :].unsqueeze(2).to_broadcast([P, NB, H])

            def vector(dve):
                nc.vector.tensor_reduce(s1[:, :], t, AX, ALU.add)
                nc.vector.drain()
                nc.vector.tensor_scalar(s1[:, :], s1[:, :], 1.0 / H, None, ALU.mult)
                nc.vector.drain()
                nc.vector.tensor_tensor(t, t, wide(s1), ALU.subtract)
                nc.vector.drain()
                nc.vector.tensor_tensor(tmp, t, t, ALU.mult)
                nc.vector.drain()
                nc.vector.tensor_reduce(s2[:, :], tmp, AX, ALU.add).then_inc(s_var, 1)
                dve.wait_ge(s_std, 1)
                nc.vector.reciprocal(s2[:, :], s1[:, :])
                nc.vector.drain()
                nc.vector.tensor_tensor(t, t, wide(s2), ALU.mult)
                nc.vector.drain()

            def scalar(act):
                act.wait_ge(s_var, 1)
                nc.scalar.activation(s1[:, :], s2[:, :], ACT.Sqrt, bias=epsc[:, :], scale=1.0 / H).then_inc(s_std, 1)

            return vector, scalar

        def node_block(name, vector, scalar=None, load=None, store=()):
            s_in, s_v, s_out = sem(name + "_in"), sem(name + "_vec"), sem(name + "_out")
            with nc.Block() as block:
                @block.sync
                def _(sp):
                    if load:
                        sp.dma_start(load[0], load[1]).then_inc(s_in, 16)
                        sp.wait_ge(s_in, 16)
                    sp.wait_ge(s_v, 1)
                    for to, what in store:
                        sp.dma_start(to, what).then_inc(s_out, 16)
                    if store:
                        sp.wait_ge(s_out, 16 * len(store))

                @block.vector
                def _(dve):
                    if load:
                        dve.wait_ge(s_in, 16)
                    vector(dve)
                    nc.vector.drain().then_inc(s_v, 1)

                if scalar:
                    block.scalar(scalar)

        bcast = lambda a: a[:, :].unsqueeze(2).to_broadcast([P, NB, H])

        def norm0_block(h, tmp, store=()):
            ln, ln_s = layer_norm_parts("ln0", x_sb[:, :, :], tmp)

            def first_norm(dve):
                nc.vector.tensor_tensor(x_sb[:, :, :], x_sb[:, :, :], h, ALU.add)
                nc.vector.drain()
                ln(dve)
                nc.vector.tensor_tensor(dst_n[:, :, 0:H], x_sb[:, :, :], bcast(mult), ALU.mult)
            node_block("norm0", first_norm, ln_s, store=store)

        def final_block(agg, v, h, tmp, load=None):
            ln1, ln1s = layer_norm_parts("ln1", v, tmp)
            ln2, ln2s = layer_norm_parts("ln2", h, tmp)

            def last(dve):
                nc.vector.tensor_scalar(s1[:, :], agg[:, :, H], 1e-8, None, ALU.max)
                nc.vector.drain()
                nc.vector.reciprocal(s2[:, :], s1[:, :])
                nc.vector.drain()
                nc.vector.tensor_tensor(v, agg[:, :, 0:H], bcast(s2), ALU.mult)
                nc.vector.drain()
                nc.vector.tensor_tensor(v, v, x_sb[:, :, :], ALU.add)
                nc.vector.drain()
                ln1(dve)
                nc.vector.tensor_tensor(v, v, gb[:, 0, :].unsqueeze(1).to_broadcast([P, NB, H]), ALU.mult)
                nc.vector.drain()
                nc.vector.tensor_tensor(v, v, gb[:, 1, :].unsqueeze(1).to_broadcast([P, NB, H]), ALU.add)
                nc.vector.drain()
                nc.vector.tensor_tensor(h, v, x_sb[:, :, :], ALU.add)
                nc.vector.drain()
                ln2(dve)

            def last_s(act):
                ln1s(act)
                ln2s(act)
            node_block("final", last, last_s, load=load, store=[
                (out[0:(NB - 1) * P, :].rearrange("(b p) w -> p b w", p=P), h[:, 0:NB - 1, :]),
                (out[(NB - 1) * P:N, :], h[0:LAST, NB - 1, :])])

        def fast_path():
            with own_semaphores():
                index_edges()
            with own_semaphores():
                adjacency()
            with ExitStack() as c:
                h_all = sb("h_all", [P, ND, H], F32, c)
                with own_semaphores():
                    propagate(h_all)
                tmp = sb("n_tmp", [P, NB, H], F32, c)
                agg = sb("n_agg", [P, NB, H + 1], F32, c)
                v = sb("n_v", [P, NB, H], F32, c)
                with own_semaphores():
                    norm0_block(h_all[:, 0:NB, :], tmp[:, :, :])
                with own_semaphores():
                    convolve(agg)
                with own_semaphores():
                    final_block(agg, v[:, :, :], h_all[:, 0:NB, :], tmp[:, :, :])

        def general_path():
            with ExitStack() as c:
                sb_ = lambda name, shape, dt=F32: sb(name, shape, dt, c)
                h_sb, u_sb, v_sb = sb_("h_sb", [P, NB, H]), sb_("u_sb", [P, NB, H]), sb_("v_sb", [P, NB, H])
                g_sb, dinv = sb_("g_sb", [P, NB, H]), sb_("g_dinv", [P, NB])
                zrow = sb_("zrow", [P, NB, H + 1])
                ew, cw = sb_("g_ew", [SP_, ST]), sb_("g_cw", [SP_, ST])
                src_sb, dst_sb = sb_("g_src", [SP_, ST], I32), sb_("g_dst", [SP_, ST], I32)
                kf, ku, su = sb_("kf", [SP_, 1]), sb_("ku", [SP_, 1], U32), sb_("su", [SP_, 1], U32)
                wf, wu, cwc = sb_("wf", [SP_, 1]), sb_("wu", [SP_, 1], U32), sb_("cwc", [SP_, 1])
                diag, eq, dup = sb_("diag", [SP_, SP_]), sb_("eq", [SP_, SP_]), sb_("dup", [SP_, SP_])
                rows, cur = sb_("rows", [SP_, H + 1]), sb_("cur", [SP_, H + 1])
                dstrow, srcrow, prod, ad = sb_("dstrow", [SP_, WD]), sb_("srcrow", [SP_, G]), sb_("prod", [SP_, G]), sb_("ad", [SP_, 1])
                attr, attrT, hid = sb_("attr", [SP_, R]), sb_("attrT", [R, SP_]), sb_("hid", [H + 1, SP_])
                pk, psum_rows, pa, ph, pg = (ps(n, [P, 512], F32, c) for n in ("pk", "psum_rows", "pa", "ph", "pg"))

                def zero_table(name, table, W):
                    s = sem(name)
                    with nc.Block() as block:
                        @block.sync
                        def _(sp):
                            sp.dma_start(nodes(table), zrow[:, :, 0:W]).then_inc(s, 16)
                            sp.wait_ge(s, 16)

                def add_pass(name, table, W, key, other, messages):
                    s_free = sem(name + "_free")
                    s_key = sem(name + "_key")
                    s_go = sem(name + "_go")
                    s_gath = [sem(f"{name}_gath{n}") for n in range(3 if messages else 2)]
                    s_kt = sem(name + "_kt")
                    s_eq = sem(name + "_eq")
                    s_msg = sem(name + "_msg")
                    s_sum = sem(name + "_sum")
                    s_new = sem(name + "_new")
                    s_scat = sem(name + "_scat")
                    s_attr, s_aT, s_aTc = sem(name + "_attr"), sem(name + "_aT"), sem(name + "_aTc")
                    s_h, s_hc, s_g = sem(name + "_h"), sem(name + "_hc"), sem(name + "_g")
                    s_v, s_pe = sem(name + "_v"), sem(name + "_pe")
                    NV = 13 if messages else 7

                    with nc.Block() as block:
                        @block.gpsimd
                        def _(pool):
                            pool.sem_inc(s_free, 1)
                            with pool.Fori(0, ST) as t:
                                pool.wait_ge(s_key, t + 1)
                                pool.sem_inc(s_go, 1)
                                off = lambda a: bass.IndirectOffsetOnAxis(ap=a[:, :], axis=0)
                                pool.indirect_dma_start(cur[:, 0:W], None, table, off(ku)).then_inc(s_gath[0], 16)
                                if messages:
                                    pool.indirect_dma_start(dstrow[:, :], None, dstT, off(su)).then_inc(s_gath[1], 16)
                                    pool.indirect_dma_start(srcrow[:, :], None, srcT, off(ku)).then_inc(s_gath[2], 16)
                                else:
                                    pool.indirect_dma_start(rows[:, 0:W], None, gT, off(su)).then_inc(s_gath[1], 16)
                                pool.wait_ge(s_new, t + 1)
                                pool.sem_inc(s_go, 1)
                                pool.indirect_dma_start(table, off(wu), cur[:, 0:W], None, bounds_check=NP - 1,
                                                        oob_is_err=False).then_inc(s_scat, 16)
                                pool.wait_ge(s_scat, t * 16 + 16)
                                pool.sem_inc(s_free, 1)

                        @block.vector
                        def _(dve):
                            with dve.Fori(0, ST) as t:
                                step = Chain(dve, s_v, t * NV)
                                dve.wait_ge(s_free, t + 1)
                                nc.vector.tensor_copy(kf[:, :], key[:, bass.ds(t, 1)])
                                nc.vector.tensor_copy(ku[:, :], key[:, bass.ds(t, 1)])
                                step(nc.vector.tensor_copy(su[:, :], other[:, bass.ds(t, 1)]))
                                dve.sem_inc(s_key, 1)
                                step(nc.vector.tensor_scalar(diag[:, :], ident[0:SP_, 0:SP_], kf[:, :], None, ALU.mult))
                                dve.sem_inc(s_eq, 1)
                                dve.wait_ge(s_kt, t + 1)
                                step(nc.vector.tensor_scalar(eq[:, :], pk[0:SP_, 0:SP_], kf[:, :], None, ALU.is_equal))
                                step(nc.vector.tensor_tensor(dup[:, :], eq[:, :], below[0:SP_, 0:SP_], ALU.mult))
                                step(nc.vector.tensor_reduce(wf[:, :], dup[:, :], AX, ALU.max))
                                step(nc.vector.tensor_scalar(wu[:, :], wf[:, :], float(1 << 20), kf[:, :], ALU.mult, ALU.add))
                                for s in s_gath:
                                    dve.wait_ge(s, t * 16 + 16)
                                if messages:
                                    step(nc.vector.tensor_copy(cwc[:, :], cw[:, bass.ds(t, 1)]))
                                    step(nc.vector.tensor_tensor(prod[:, :], dstrow[:, H + 1:WD], srcrow[:, :], ALU.mult))
                                    step(nc.vector.tensor_reduce(ad[:, :], prod[:, :], AX, ALU.add))
                                    dve.wait_ge(s_g, t + 1)
                                    step(nc.vector.tensor_scalar(rows[:, 0:H], pg[0:SP_, 0:H], ad[:, :], cwc[:, :], ALU.add, ALU.mult))
                                    step(nc.vector.tensor_tensor(rows[:, 0:H], rows[:, 0:H], dstrow[:, 0:H], ALU.mult))
                                    step(nc.vector.tensor_copy(rows[:, H:H + 1], dstrow[:, H:H + 1]))
                                dve.sem_inc(s_msg, 1)
                                dve.wait_ge(s_sum, t + 1)
                                step(nc.vector.tensor_tensor(cur[:, 0:W], cur[:, 0:W], psum_rows[0:SP_, 0:W], ALU.add))
                                dve.sem_inc(s_new, 1)
                                assert step.n == NV

                        @block.tensor
                        def _(pe):
                            with pe.Fori(0, ST) as t:
                                if messages:
                                    pe.wait_ge(s_attr, t * 16 + 16)
                                    pe.sem_inc(s_pe, 1)
                                    nc.tensor.transpose(pa[0:R, 0:SP_], attr[:, :], ident[0:SP_, 0:SP_]).then_inc(s_aT, 1)
                                    pe.wait_ge(s_aTc, t + 1)
                                    pe.sem_inc(s_pe, 1)
                                    nc.tensor.matmul(ph[0:H, 0:SP_], w1T[:, :], attrT[:, :]).then_inc(s_h, 1)
                                    pe.wait_ge(s_hc, t + 2)
                                    pe.sem_inc(s_pe, 1)
                                    nc.tensor.matmul(pg[0:SP_, 0:H], hid[:, :], w2T[:, :]).then_inc(s_g, 1)
                                pe.wait_ge(s_eq, t + 1)
                                nc.tensor.matmul(pk[0:SP_, 0:SP_], ones[0:SP_, 0:SP_], diag[:, :]).then_inc(s_kt, 1)
                                pe.wait_ge(s_msg, t + 1)
                                nc.tensor.matmul(psum_rows[0:SP_, 0:W], eq[:, :], rows[:, 0:W]).then_inc(s_sum, 1)

                        if messages:
                            @block.sync
                            def _(sp):
                                tiles = edge_attr.rearrange("(p j) f -> p j f", p=SP_)
                                with sp.Fori(0, ST) as t:
                                    sp.wait_ge(s_free, t + 1)
                                    sp.dma_start(attr[:, :], tiles[:, bass.ds(t, 1), :].rearrange("p o f -> p (o f)")).then_inc(s_attr, 16)

                            @block.scalar
                            def _(act):
                                nc.scalar.activation(hid[:, :], ones[0:H + 1, 0:SP_], ACT.Copy).then_inc(s_hc, 1)
                                act.wait_ge(s_hc, 1)
                                with act.Fori(0, ST) as t:
                                    act.wait_ge(s_aT, t + 1)
                                    nc.scalar.activation(attrT[:, :], pa[0:R, 0:SP_], ACT.Copy).then_inc(s_aTc, 1)
                                    act.wait_ge(s_h, t + 1)
                                    nc.scalar.activation(hid[0:H, :], ph[0:H, 0:SP_], ACT.Silu, bias=b1c[:, :]).then_inc(s_hc, 1)

                with own_semaphores():
                    s_ld, s_z = sem("g_ld"), sem("g_z")
                    with nc.Block() as block:
                        cut = cutoff("gcut", block, ew, cw, None)

                        @block.sync
                        def _(sp):
                            sp.wait_ge(s_z, 1)
                            node_in(sp, x_sb, x, s_ld)
                            sp.dma_start(src_sb[:, :], src.rearrange("(p j) -> p j", p=SP_)).then_inc(s_ld, 16)
                            sp.dma_start(dst_sb[:, :], dst.rearrange("(p j) -> p j", p=SP_)).then_inc(s_ld, 16)
                            sp.dma_start(ew[:, :], edge_weight.rearrange("(p j) -> p j", p=SP_)).then_inc(s_ld, 16)

                        @block.vector
                        def _(dve):
                            nc.vector.memset(x_sb[:, NB - 1, :], 0.0)
                            nc.vector.memset(zrow[:, :, :], 0.0)
                            nc.vector.drain().then_inc(s_z, 1)
                            dve.wait_ge(s_ld, 80)
                            cut(dve)

                def fill_ones(dve):
                    nc.vector.memset(u_sb[:, :, :], 1.0)
                with own_semaphores():
                    node_block("ones", fill_ones, store=[(nodes(gT), u_sb[:, :, :])])
                    zero_table("zero_deg", sumT, H)
                    add_pass("deg", sumT, H, dst_sb, src_sb, False)

                with own_semaphores():
                    s_dv, s_ds = sem("s_dv"), sem("s_ds")

                    def degree(dve):
                        nc.vector.tensor_scalar(s1[:, :], v_sb[:, :, 0], 1.0, None, ALU.add).then_inc(s_dv, 1)
                        dve.wait_ge(s_ds, 1)
                        nc.vector.reciprocal(dinv[:, :], s2[:, :])
                        nc.vector.drain()
                        nc.vector.tensor_tensor(g_sb[:, :, :], x_sb[:, :, :], bcast(dinv), ALU.mult)

                    def degree_root(act):
                        act.wait_ge(s_dv, 1)
                        nc.scalar.activation(s2[:, :], s1[:, :], ACT.Sqrt).then_inc(s_ds, 1)
                    node_block("deg_n", degree, degree_root, load=(v_sb[:, :, :], nodes(sumT)), store=[(nodes(gT), g_sb[:, :, :])])

                with nc.Fori(0, STEPS):
                    with own_semaphores():
                        zero_table("zero", sumT, H)
                        add_pass("prop", sumT, H, dst_sb, src_sb, False)

                        def update(dve):
                            nc.vector.tensor_tensor(v_sb[:, :, :], v_sb[:, :, :], g_sb[:, :, :], ALU.add)
                            nc.vector.drain()
                            nc.vector.tensor_tensor(v_sb[:, :, :], v_sb[:, :, :], bcast(dinv), ALU.mult)
                            nc.vector.tensor_scalar(u_sb[:, :, :], x_sb[:, :, :], ALPHA, None, ALU.mult)
                            nc.vector.drain()
                            nc.vector.scalar_tensor_tensor(h_sb[:, :, :], v_sb[:, :, :], 1.0 - ALPHA, u_sb[:, :, :], ALU.mult, ALU.add)
                            nc.vector.drain()
                            nc.vector.tensor_tensor(g_sb[:, :, :], h_sb[:, :, :], bcast(dinv), ALU.mult)
                        node_block("upd", update, load=(v_sb[:, :, :], nodes(sumT)), store=[(nodes(gT), g_sb[:, :, :])])

                with own_semaphores():
                    norm0_block(h_sb[:, :, :], u_sb[:, :, :], store=[(nodes(dstT), dst_n[:, :, :]), (nodes(srcT), emb_n[:, :, :])])
                with own_semaphores():
                    zero_table("zero_agg", aggT, H + 1)
                    add_pass("conv", aggT, H + 1, src_sb, dst_sb, True)
                with own_semaphores():
                    final_block(zrow, v_sb[:, :, :], h_sb[:, :, :], u_sb[:, :, :], load=(zrow[:, :, :], nodes(aggT)))

        with own_semaphores():
            setup()
        fast_path()
        misfit = nc.values_load(flag_i[0:1, 0:1], min_val=0, max_val=1)
        with nc.If(misfit > 0):
            nc.all_engine_barrier()
            general_path()


_INS = ["x", "src", "dst", "edge_attr_40", "edge_weight", "node_type_119", "node_vec", "L1_gnn_W1", "L1_gnn_b1",
        "L1_gnn_W2", "L1_gnn_b2", "L1_gnn_emb", "L1_gnn_adaptW", "L1_gnn_gamma", "L1_gnn_beta"]


def kernel(**inputs):
    import numpy as _np
    import concourse.bacc as _bacc
    from concourse.bass_utils import run_bass_kernel_spmd as _run

    nc = _bacc.Bacc("TRN2", target_bir_lowering=False, num_devices=1)
    arrays, args = {}, []
    for name in _INS:
        a = _np.ascontiguousarray(inputs[name])
        arrays[f"in_{name}_dram"] = a
        args.append(nc.dram_tensor(f"in_{name}_dram", a.shape, mybir.dt.from_np(a.dtype), kind="ExternalInput").ap())
    args.append(nc.dram_tensor("out_0_dram", inputs["x"].shape, F32, kind="ExternalOutput").ap())
    gnn(nc, *args)
    r = _run(nc, [arrays], core_ids=[0])
    return r.results[0]["out_0_dram"]
```

```python
from contextlib import ExitStack, contextmanager
from math import pi

import concourse.bass as bass
from concourse import mybir

F32 = mybir.dt.float32
BF16 = mybir.dt.bfloat16
F16 = mybir.dt.float16
I32 = mybir.dt.int32
U32 = mybir.dt.uint32
ALU = mybir.AluOpType
ACT = mybir.ActivationFunctionType
AX = mybir.AxisListType.X

P = 128
STEPS, ALPHA = 5, 0.8
CUTOFF, EPS = 6.0, 1e-5


class Chain:

    def __init__(self, engine, sem, base=0):
        self.engine, self.sem, self.base, self.n = engine, sem, base, 0

    def __call__(self, ins):
        self.n += 1
        ins.then_inc(self.sem, 1)
        self.engine.wait_ge(self.sem, self.base + self.n)


class Windows:
    pass


def gnn(nc, x, src, dst, edge_attr, edge_weight, node_type, node_vec, W1, b1, W2, b2, emb, adaptW, gamma, beta, out):
    N, H = x.shape
    E, R = edge_attr.shape
    G = emb.shape[1]
    NB = -(-N // P)
    LAST = N - (NB - 1) * P
    NP = NB * P
    SP_ = 125
    ST = E // SP_
    assert SP_ * ST == E
    WD = H + 1 + G

    with ExitStack() as ctx:
        def sb(name, shape, dt=F32, c=ctx):
            return c.enter_context(nc.sbuf_tensor(name, shape, dt))

        def ps(name, shape, dt=F32, c=ctx):
            return c.enter_context(nc.psum_tensor(name, shape, dt))

        seen = set()

        def sem(name):
            while name in seen:
                name += "_"
            seen.add(name)
            return nc.alloc_semaphore(name=name)

        @contextmanager
        def own_semaphores():
            before = nc.snapshot_sems()
            yield
            nc.all_engine_barrier()
            nc.clear_and_free_semaphores(nc.allocated_since(before))
            nc.all_engine_barrier()

        def dram(name, shape, dt=F32):
            return nc.dram_tensor(name, shape, dt, kind="Internal").ap()

        gT = dram("g_table", [NP, H])
        sumT = dram("sum_table", [NP, H])
        dstT = dram("dst_table", [NP, WD])
        srcT = dram("src_table", [NP, G])
        aggT = dram("agg_table", [NP, H + 1])
        nodes = lambda t: t.rearrange("(b p) w -> p b w", p=P)

        ND = 2 * -(-NB // 2)
        GR = 8
        GB = P // GR
        GT = 3
        GE = GT * P
        NQ = ND * GB + 1
        QC = -(-NQ // P)
        WT = 35
        WE = WT * P
        KG = NB * GR
        PW = H + 3
        SLOTS = ND * NB * P
        DROP = float(1 << 22)
        CH = 7
        assert NB % CH == 0 and ND * GB * GR >= N and ND // 5 * 5 == ND

        keyT = dram("key_table", [E], I32)
        cwT = dram("cw_table", [E])
        startT = dram("start_table", [QC * P])
        adjT = dram("adj_table", [ND, P, NB * P], BF16)
        slotT = dram("slot_table", [SLOTS + 2 * NB * P, PW])
        slots_of = lambda D: slotT.rearrange("(d r s) w -> r d (s w)", r=P, s=NB)[:, bass.ds(D, 1), :]

        x_sb = sb("x_sb", [P, NB, H])
        emb_n = sb("emb_n", [P, NB, G])
        dst_n = sb("dst_n", [P, NB, WD])
        mult = sb("mult", [P, NB])
        z_sb = sb("z_sb", [P, NB], I32)
        ident = sb("ident", [P, P])
        ident_b = sb("ident_b", [P, P], BF16)
        ones = sb("ones", [P, P])
        ones_b = sb("ones_b", [P, 2], BF16)
        below = sb("below", [P, P])
        above_b = sb("above_b", [P, P], BF16)
        w1 = sb("w1", [H, R])
        w1T = sb("w1T", [R, H])
        b1c = sb("b1c", [H, 1])
        w2T = sb("w2T", [H + 1, H])
        w2 = sb("w2", [H, H])
        aw = sb("aw", [G, G])
        awT = sb("awT", [G, G])
        gb = sb("gb", [P, 2, H])
        s1 = sb("s1", [P, NB])
        s2 = sb("s2", [P, NB])
        halfpi = sb("halfpi", [P, 1])
        epsc = sb("epsc", [P, 1])
        start_row = sb("start_row", [1, QC * P])
        group_at = sb("group_at", [1, ND * GB], I32)
        block_at = sb("block_at", [1, ND], I32)
        flags = sb("flags", [1, 4])
        flag_i = sb("flag_i", [1, 1], I32)
        deg = sb("deg", [P, ND])

        def node_in(eng, tile, table, s):
            eng.dma_start(tile[:, 0:NB - 1, :], table[0:(NB - 1) * P, :].rearrange("(b p) w -> p b w", p=P)).then_inc(s, 16)
            eng.dma_start(tile[0:LAST, NB - 1, :], table[(NB - 1) * P:N, :]).then_inc(s, 16)

        def setup():
            s_load, s_const, s_mask = sem("s_load"), sem("s_const"), sem("s_mask")
            s_wT, s_wTc = sem("s_wT"), sem("s_wTc")
            LOADS = 16 * 13
            with nc.Block() as block, ExitStack() as c:
                tp = ps("tp", [P, 512], c=c)

                @block.gpsimd
                def _(pool):
                    pool.wait_ge(s_const, 1)
                    nc.gpsimd.affine_select(out=ident[:, :], in_=ident[:, :], compare_op=ALU.not_equal, fill=1.0, base=0,
                                            pattern=[[-1, P]], channel_multiplier=1).then_inc(s_mask, 1)
                    nc.gpsimd.affine_select(out=below[:, :], in_=ones[:, :], compare_op=ALU.is_gt, fill=0.0, base=0,
                                            pattern=[[-1, P]], channel_multiplier=1).then_inc(s_mask, 1)

                @block.vector
                def _(dve):
                    nc.vector.memset(ident[:, :], 0.0)
                    nc.vector.memset(ones[:, :], 1.0)
                    nc.vector.memset(ones_b[:, :], 1.0)
                    nc.vector.memset(x_sb[:, NB - 1, :], 0.0)
                    nc.vector.memset(mult[:, NB - 1:NB], 0.0)
                    nc.vector.memset(z_sb[:, NB - 1:NB], 0)
                    nc.vector.memset(halfpi[:, :], pi / 2)
                    nc.vector.memset(epsc[:, :], EPS)
                    nc.vector.drain().then_inc(s_const, 1)
                    dve.wait_ge(s_mask, 2)
                    nc.vector.tensor_copy(ident_b[:, :], ident[:, :])
                    nc.vector.tensor_tensor(above_b[:, :], ones[:, :], below[:, :], ALU.subtract)
                    nc.vector.drain()
                    nc.vector.tensor_tensor(above_b[:, :], above_b[:, :], ident_b[:, :], ALU.subtract)
                    dve.wait_ge(s_wT, 1)
                    nc.vector.tensor_copy(w1T[:, :], tp[0:R, 0:H])
                    nc.vector.tensor_copy(w2T[0:H, :], tp[0:H, P:P + H])
                    nc.vector.tensor_copy(awT[:, :], tp[0:G, 2 * P:2 * P + G]).then_inc(s_wTc, 1)

                @block.sync
                def _(sp):
                    sp.wait_ge(s_const, 1)
                    node_in(sp, x_sb, x, s_load)
                    with nc.allow_non_contiguous_dma(reason="one word per node"):
                        node_in(sp, mult.rearrange("p (b o) -> p b o", o=1), node_vec.rearrange("(n o) -> n o", o=1), s_load)
                        node_in(sp, z_sb.rearrange("p (b o) -> p b o", o=1), node_type.rearrange("(n o) -> n o", o=1), s_load)
                        sp.dma_start(b1c[:, :], b1.rearrange("(n o) -> n o", o=1)).then_inc(s_load, 16)
                    sp.dma_start(w1[:, :], W1).then_inc(s_load, 16)
                    sp.dma_start(w2[:, :], W2).then_inc(s_load, 16)
                    sp.dma_start(aw[:, :], adaptW).then_inc(s_load, 16)
                    sp.dma_start(w2T[H:H + 1, :], b2.rearrange("(o n) -> o n", o=1)).then_inc(s_load, 16)
                    sp.dma_start(gb[:, 0, :], gamma.rearrange("(o n) -> o n", o=1).to_broadcast([P, H])).then_inc(s_load, 16)
                    sp.dma_start(gb[:, 1, :], beta.rearrange("(o n) -> o n", o=1).to_broadcast([P, H])).then_inc(s_load, 16)
                    sp.wait_ge(s_load, LOADS)

                @block.tensor
                def _(pe):
                    pe.wait_ge(s_load, LOADS)
                    pe.wait_ge(s_mask, 2)
                    nc.tensor.transpose(tp[0:R, 0:H], w1[:, :], ident[0:H, 0:H])
                    nc.tensor.transpose(tp[0:H, P:P + H], w2[:, :], ident[0:H, 0:H])
                    nc.tensor.transpose(tp[0:G, 2 * P:2 * P + G], aw[:, :], ident[0:G, 0:G]).then_inc(s_wT, 1)

        def adapted(block, c):
            eT = sb("eT", [G, 2, 4 * P], c=c)
            pt = ps("pt", [G, 2, 512], c=c)
            pq = ps("pq", [P, 2, 512], c=c)
            s_eT, s_eTc, s_q, s_qc = sem("s_eT"), sem("s_eTc"), sem("s_q"), sem("s_qc")
            lots = [(a, min(a + 4, NB)) for a in range(0, NB, 4)]

            @block.tensor
            def _(pe):
                for n, (a, b) in enumerate(lots):
                    if n >= 2:
                        pe.wait_ge(s_eTc, n - 1)
                    for i in range(a, b):
                        x_ = nc.tensor.transpose(pt[:, n % 2, (i - a) * P:(i - a + 1) * P], emb_n[:, i, :], ident[:, :])
                    x_.then_inc(s_eT, 1)
                    pe.wait_ge(s_eTc, n + 1)
                    if n >= 2:
                        pe.wait_ge(s_qc, n - 1)
                    for i in range(a, b):
                        x_ = nc.tensor.matmul(pq[:, n % 2, (i - a) * G:(i - a + 1) * G], eT[:, n % 2, (i - a) * P:(i - a + 1) * P], awT[:, :])
                    x_.then_inc(s_q, 1)

            def copies(act):
                for n, (a, b) in enumerate(lots):
                    act.wait_ge(s_eT, n + 1)
                    if n >= 2:
                        act.wait_ge(s_q, n - 1)
                    nc.scalar.activation(eT[:, n % 2, 0:(b - a) * P], pt[:, n % 2, 0:(b - a) * P], ACT.Copy).then_inc(s_eTc, 1)
                    act.wait_ge(s_q, n + 1)
                    nc.scalar.activation(dst_n[:, a:b, H + 1:WD], pq[:, n % 2, 0:(b - a) * G].rearrange("p (s g) -> p s g", g=G), ACT.Copy).then_inc(s_qc, 1)
            return copies

        def cutoff(name, block, ew, cw):
            s_arg, s_sin = sem(name + "_arg"), sem(name + "_sin")

            def vector(dve):
                nc.vector.tensor_scalar(cw[:, :], ew[:, :], CUTOFF, None, ALU.min).then_inc(s_arg, 1)
                dve.wait_ge(s_sin, 1)
                nc.vector.tensor_scalar(ew[:, :], ew[:, :], CUTOFF, None, ALU.is_lt)
                nc.vector.tensor_scalar(cw[:, :], cw[:, :], 1.0, 0.5, ALU.add, ALU.mult)
                nc.vector.drain()
                nc.vector.tensor_tensor(cw[:, :], cw[:, :], ew[:, :], ALU.mult)

            @block.scalar
            def _(act):
                act.wait_ge(s_arg, 1)
                nc.scalar.activation(cw[:, :], cw[:, :], ACT.Sin, bias=halfpi[0:SP_, :], scale=-pi / CUTOFF).then_inc(s_sin, 1)
            return vector

        def index_edges(zero):
            with ExitStack() as c:
                src_sb = sb("src_sb", [SP_, ST], I32, c)
                dst_sb = sb("dst_sb", [SP_, ST], I32, c)
                next_d = sb("next_d", [SP_, 1], I32, c)
                key_sb = sb("key_sb", [SP_, ST], I32, c)
                ew = sb("ew", [SP_, ST], F32, c)
                cw = sb("cw", [SP_, ST], F32, c)
                first_i = sb("first_i", [P, SP_], I32, c)
                first = sb("first", [P, SP_], F32, c)
                junk = sb("junk", [P, SP_], F32, c)
                bound_i = sb("bound_i", [P, QC], I32, c)
                bound = sb("bound", [P, QC], F32, c)
                row = sb("row", [P, QC], F32, c)
                row_u = sb("row_u", [P, QC], U32, c)
                cnt = sb("cnt", [P, QC], F32, c)
                got = sb("got", [P, 2, ST], I32, c)
                gotf = sb("gotf", [P, ST], F32, c)
                gotj = sb("gotj", [P, ST], F32, c)
                bad = sb("bad", [P, 2], F32, c)
                pair = sb("pair", [SP_, ST], F32, c)
                clamp = sb("clamp", [1, ND * GB], F32, c)
                clampd = sb("clampd", [1, ND], F32, c)
                over = sb("over", [1, ND * GB], F32, c)
                bad_row = ps("bad_row", [1, 512], c=c)
                s_ld, s_first, s_io, s_row, s_got = sem("i_ld"), sem("i_first"), sem("i_io"), sem("i_row"), [sem("i_got0"), sem("i_got1")]
                s_st, s_key, s_stT, s_back, s_cwr = sem("i_st"), sem("i_key"), sem("i_stT"), sem("i_back"), sem("i_cwr")
                s_bad, s_badT, s_gotd = sem("i_bad"), sem("i_badT"), sem("i_gotd")
                s_z, s_zd = sem("i_z"), sem("i_zd")
                with nc.Block() as block:
                    cut = cutoff("icut", block, ew, cw)

                    @block.sync
                    def _(sp):
                        with nc.allow_non_contiguous_dma(reason="one word per row of edges"):
                            sp.dma_start(first_i[:, :], dst.rearrange("(o p j) -> o p j", o=1, j=ST)[:, :, 0].to_broadcast([P, SP_])).then_inc(s_first, 16)
                            sp.dma_start(next_d[0:SP_ - 1, :], dst[ST:E].rearrange("(p j) -> p j", j=ST)[:, 0:1]).then_inc(s_ld, 16)
                        sp.dma_start(dst_sb[:, :], dst.rearrange("(p j) -> p j", p=SP_)).then_inc(s_ld, 16)
                        sp.dma_start(src_sb[:, :], src.rearrange("(p j) -> p j", p=SP_)).then_inc(s_ld, 16)
                        sp.dma_start(ew[:, :], edge_weight.rearrange("(p j) -> p j", p=SP_)).then_inc(s_ld, 16)
                        sp.wait_ge(s_stT, 1)
                        with nc.allow_non_contiguous_dma(reason="a few words"):
                            sp.dma_start(startT.rearrange("(c p) -> p c", p=P), cnt[:, :]).then_inc(s_st, 16)
                        sp.wait_ge(s_st, 16)
                        sp.dma_start(start_row[:, :], startT.rearrange("(o n) -> o n", o=1)).then_inc(s_back, 16)
                        sp.wait_ge(s_key, 1)
                        sp.dma_start(keyT.rearrange("(p j) -> p j", p=SP_), key_sb[:, :]).then_inc(s_st, 16)
                        sp.wait_ge(s_cwr, 1)
                        sp.dma_start(cwT.rearrange("(p j) -> p j", p=SP_), cw[:, :]).then_inc(s_st, 16)
                        sp.wait_ge(s_z, 1)
                        for D in range(2):
                            sp.dma_start(slots_of(D), zero[:, :].unsqueeze(1)).then_inc(s_zd, 16)
                        sp.wait_ge(s_st, 48)
                        sp.wait_ge(s_back, 16)
                        sp.wait_ge(s_zd, 16 * 2)

                    @block.gpsimd
                    def _(pool):
                        nc.gpsimd.iota(bound_i[:, :], pattern=[[GR * P, QC]], base=0, channel_multiplier=GR).then_inc(s_io, 1)
                        pool.wait_ge(s_row, 1)
                        for n in range(QC):
                            if n >= 2:
                                pool.wait_ge(s_gotd, n - 1)
                            pool.indirect_dma_start(got[:, n % 2, :], None, dst.rearrange("(p j) -> p j", p=SP_),
                                                    bass.IndirectOffsetOnAxis(ap=row_u[:, n:n + 1], axis=0)).then_inc(s_got[n % 2], 16)

                    @block.tensor
                    def _(pe):
                        pe.wait_ge(s_bad, 1)
                        nc.tensor.matmul(bad_row[:, 0:2], ones[:, 0:1], bad[:, :]).then_inc(s_badT, 1)

                    @block.vector
                    def _(dve):
                        nc.vector.memset(bad[:, :], 0.0)
                        nc.vector.memset(zero[:, :], 0.0).then_inc(s_z, 1)
                        dve.wait_ge(s_io, 1)
                        nc.vector.tensor_copy(bound[:, :], bound_i[:, :])
                        dve.wait_ge(s_first, 16)
                        nc.vector.tensor_copy(first[:, :], first_i[:, :])
                        nc.vector.drain()
                        for n in range(QC):
                            nc.vector.tensor_scalar(junk[:, :], first[:, :], bound[:, n:n + 1], None, ALU.is_lt, ALU.add,
                                                    accum_out=row[:, n:n + 1])
                            nc.vector.drain()
                        nc.vector.tensor_scalar(row[:, :], row[:, :], -1.0, 0.0, ALU.add, ALU.max)
                        nc.vector.drain()
                        nc.vector.tensor_copy(row_u[:, :], row[:, :]).then_inc(s_row, 1)
                        dve.wait_ge(s_ld, 64)
                        nc.vector.scalar_tensor_tensor(key_sb[:, :], dst_sb[:, :], 13, src_sb[:, :], ALU.logical_shift_left,
                                                       ALU.bitwise_or).then_inc(s_key, 1)
                        cut(dve)
                        nc.vector.drain().then_inc(s_cwr, 1)
                        nc.vector.tensor_tensor(pair[:, 0:ST - 1], dst_sb[:, 0:ST - 1], dst_sb[:, 1:ST], ALU.is_gt)
                        nc.vector.tensor_tensor(bad[0:SP_ - 1, 1:2], dst_sb[0:SP_ - 1, ST - 1:ST], next_d[0:SP_ - 1, :], ALU.is_gt)
                        nc.vector.drain()
                        nc.vector.tensor_reduce(bad[0:SP_, 0:1], pair[:, 0:ST - 1], AX, ALU.max)
                        nc.vector.drain().then_inc(s_bad, 1)
                        for n in range(QC):
                            dve.wait_ge(s_got[n % 2], 16 * (n // 2) + 16)
                            nc.vector.tensor_copy(gotf[:, :], got[:, n % 2, :]).then_inc(s_gotd, 1)
                            nc.vector.drain()
                            nc.vector.tensor_scalar(gotj[:, :], gotf[:, :], bound[:, n:n + 1], None, ALU.is_lt, ALU.add,
                                                    accum_out=cnt[:, n:n + 1])
                            nc.vector.drain()
                        nc.vector.scalar_tensor_tensor(cnt[:, :], row[:, :], float(ST), cnt[:, :], ALU.mult, ALU.add)
                        nc.vector.drain().then_inc(s_stT, 1)
                        dve.wait_ge(s_back, 16)
                        nc.vector.tensor_scalar(clamp[:, :], start_row[:, 0:ND * GB], float(E - GE), None, ALU.min)
                        blocks = start_row[:, 0:ND * GB].rearrange("o (d g) -> o d g", g=GB)
                        nc.vector.tensor_scalar(clampd[:, :], blocks[:, :, 0], float(E - WE), None, ALU.min)
                        nc.vector.drain()
                        nc.vector.tensor_copy(group_at[:, :], clamp[:, :])
                        nc.vector.tensor_copy(block_at[:, :], clampd[:, :])
                        nc.vector.tensor_tensor(over[:, :], start_row[:, 1:ND * GB + 1], clamp[:, :], ALU.subtract)
                        nc.vector.drain()
                        nc.vector.tensor_reduce(flags[:, 0:1], over[:, :], AX, ALU.max)
                        nc.vector.drain()
                        nc.vector.tensor_tensor(over[:, 0:ND], start_row[:, GB:GB + (ND - 1) * GB + 1:GB], clampd[:, :], ALU.subtract)
                        nc.vector.drain()
                        nc.vector.tensor_reduce(flags[:, 1:2], over[:, 0:ND], AX, ALU.max)
                        nc.vector.drain()
                        nc.vector.tensor_scalar(flags[:, 0:1], flags[:, 0:1], float(GE), None, ALU.is_gt)
                        nc.vector.tensor_scalar(flags[:, 1:2], flags[:, 1:2], float(WE), None, ALU.is_gt)
                        dve.wait_ge(s_badT, 1)
                        nc.vector.tensor_reduce(flags[:, 2:3], bad_row[:, 0:2], AX, ALU.add)

        def edge_windows(c):
            CT = 8
            chunks = [(a, min(a + CT, WT)) for a in range(0, WT, CT)]
            subs = [(a, min(a + 4, WT)) for a in range(0, WT, 4)]
            NS, MC = len(subs), len(chunks)
            NW = 18
            kwin = sb("w_kwin", [P, WT], I32, c)
            cwin = sb("w_cwin", [P, WT], F32, c)
            attr = sb("w_attr", [P, WT, R], F32, c)
            attrT = sb("w_attrT", [R, 4, P], F32, c)
            hid = sb("w_hid", [H + 1, 4, P], F32, c)
            f_i = sb("w_fi", [P, 4, WT], I32, c)
            meta = sb("w_meta", [P, WT, 3], F32, c)
            inv = sb("w_inv", [P, WT], F32, c)
            sx = sb("w_sx", [P, WT], F32, c)
            sxb = sb("w_sxb", [P, WT], BF16, c)
            dcol = sb("w_dcol", [P, 1], F32, c)
            base = sb("w_base", [P, 1], F32, c)
            io_s = sb("w_ios", [P, NB, WT], BF16, c)
            cont = sb("w_cont", [P, NB, WT], BF16, c)
            oh = sb("w_oh", [P, NB, WT], BF16, c)
            run = sb("w_run", [P, NB, WT], BF16, c)
            tot = sb("w_tot", [P, NB], BF16, c)
            rk = sb("w_rk", [P, NB, WT], BF16, c)
            rank = sb("w_rank", [P, WT], F32, c)
            rmax = sb("w_rmax", [P, 1], F32, c)
            rtop = sb("w_rtop", [P, 1], F32, c)
            pos = sb("w_pos", [P, WT], F32, c)
            slot = sb("w_slot", [P, WT], U32, c)
            pay = sb("w_pay", [P, WT, PW], F32, c)
            pT = ps("w_pT", [P, 512], c=c)
            pH = ps("w_pH", [P, 512], c=c)
            pG = ps("w_pG", [P, 2, 512], c=c)
            pR = ps("w_pR", [P, 512], c=c)
            seed = dram("seed", [P, 4])
            s_init, s_kf, s_win, s_attr = sem("w_init"), sem("w_kf"), sem("w_win"), sem("w_attr")
            s_T, s_aT, s_h, s_hid, s_g = sem("w_T"), sem("w_aT"), sem("w_h"), sem("w_hid"), sem("w_g")
            s_pay, s_free = sem("w_pay"), sem("w_free")
            s_sc = [sem(f"w_sc{q}") for q in range(MC)]
            s_tot, s_off, s_ch = sem("w_tot"), sem("w_off"), sem("w_ch")
            s_pe, s_pool, s_sp = sem("w_pe"), sem("w_pool"), sem("w_sp")
            last_n = chunks[-1][1] - chunks[-1][0]

            def load_keys(sp, w):
                at = sp.value_load(block_at[0:1, bass.ds(w, 1)], min_val=0, max_val=E - WE)
                sp.wait_ge(s_kf, w + 1)
                sp.sem_inc(s_sp, 1)
                sp.dma_start(kwin[:, :], keyT[bass.ds(at, WE)].rearrange("(p j) -> p j", p=P)).then_inc(s_win, 16)
                sp.dma_start(cwin[:, :], cwT[bass.ds(at, WE)].rearrange("(p j) -> p j", p=P)).then_inc(s_win, 16)
                return at

            def load_attr(sp, w, at):
                sp.wait_ge(s_T, w * NS + NS)
                sp.sem_inc(s_sp, 1)
                sp.dma_start(attr[:, :, :], edge_attr[bass.ds(at, WE), :].rearrange("(p j) f -> p j f", p=P)).then_inc(s_attr, 16)

            def pool_start(pool):
                pool.wait_ge(s_init, 1)
                for n in range(last_n):
                    pool.dma_start(seed, ones[:, 0:4]).then_inc(s_sc[MC - 1], 16)
                    pool.wait_ge(s_sc[MC - 1], 16 * n + 16)
                pool.sem_inc(s_free, MC - 1)

            def scatter(pool, w):
                for q, (a, b) in enumerate(chunks):
                    pool.wait_ge(s_pay, w * MC + q + 3)
                    pool.sem_inc(s_pool, 1)
                    for t in range(a, b):
                        pool.indirect_dma_start(slotT, bass.IndirectOffsetOnAxis(ap=slot[:, t:t + 1], axis=0), pay[:, t, :], None,
                                                bounds_check=SLOTS - 1, oob_is_err=False).then_inc(s_sc[q], 16)
                    v = (q - 1) % MC
                    n = 16 * (chunks[v][1] - chunks[v][0])
                    pool.wait_ge(s_sc[v], w * n + n)
                    pool.sem_inc(s_free, 1)

            def pool_end(pool):
                pool.wait_ge(s_sc[MC - 1], 16 * last_n * (ND + 1))

            def pe_start(pe):
                pe.sem_inc(s_T, NS)
                pe.sem_inc(s_h, 1)
                pe.sem_inc(s_g, 1)

            def transposes(pe, w, s):
                a, b = subs[s]
                if s == 0:
                    pe.wait_ge(s_attr, w * 16 + 16)
                    pe.sem_inc(s_pe, 1)
                pe.wait_ge(s_aT, w * NS + s + 1)
                pe.sem_inc(s_pe, 1)
                for t in range(a, b):
                    x_ = nc.tensor.transpose(pT[0:R, (t - a) * P:(t - a + 1) * P], attr[:, t, :], ident[:, :])
                x_.then_inc(s_T, 1)

            def hidden(pe, w, s):
                a, b = subs[s]
                pe.wait_ge(s_aT, w * NS + s + 2)
                pe.wait_ge(s_hid, w * NS + s + 1)
                pe.sem_inc(s_pe, 1)
                nc.tensor.matmul(pH[0:H, 0:(b - a) * P], w1T[:, :],
                                 attrT[:, 0:b - a, :].rearrange("r t e -> r (t e)")).then_inc(s_h, 1)

            def gates(pe, w, s):
                a, b = subs[s]
                q = s // 2
                pe.wait_ge(s_hid, w * NS + s + 2)
                if s % 2 == 0:
                    pe.wait_ge(s_pay, w * MC + (q + 1 if q >= 2 else 2 - q))
                pe.sem_inc(s_pe, 1)
                for t in range(a, b):
                    o = t - chunks[q][0]
                    x_ = nc.tensor.matmul(pG[:, q % 2, o * H:(o + 1) * H], hid[:, t - a, :], w2T[:, :])
                x_.then_inc(s_g, 1)

            def pe_parts(pe, w, n):
                if 2 <= n < NS + 2:
                    gates(pe, w, n - 2)
                if 1 <= n < NS + 1:
                    hidden(pe, w, n - 1)
                if n < NS:
                    transposes(pe, w, n)

            def offsets(pe, w):
                pe.wait_ge(s_tot, w + 1)
                nc.tensor.matmul(pR[:, 0:NB], above_b[:, :], tot[:, :]).then_inc(s_off, 1)

            def act_start(act):
                act.wait_ge(s_init, 1)
                nc.scalar.activation(hid[:, :, :].rearrange("h t e -> h (t e)"),
                                     ones[0:H + 1, 0:1].to_broadcast([H + 1, 4 * P]), ACT.Copy).then_inc(s_hid, 1)
                act.wait_ge(s_hid, 1)
                act.sem_inc(s_aT, 1)

            def act_parts(act, w, n):
                if 1 <= n < NS + 1:
                    s = n - 1
                    a, b = subs[s]
                    act.wait_ge(s_h, w * NS + s + 2)
                    act.wait_ge(s_g, w * NS + s + 1)
                    nc.scalar.activation(hid[0:H, 0:b - a, :].rearrange("h t e -> h (t e)"), pH[0:H, 0:(b - a) * P],
                                         ACT.Silu, bias=b1c[:, :]).then_inc(s_hid, 1)
                if n < NS:
                    a, b = subs[n]
                    act.wait_ge(s_T, w * NS + n + 1 + NS)
                    act.wait_ge(s_h, w * NS + n + 1)
                    nc.scalar.activation(attrT[:, 0:b - a, :].rearrange("r t e -> r (t e)"), pT[0:R, 0:(b - a) * P],
                                         ACT.Copy).then_inc(s_aT, 1)

            def dve_start(dve):
                nc.vector.memset(pay[:, :, :], 0.0)
                nc.vector.memset(slot[:, :], 0)
                nc.vector.memset(cont[:, :, :], 1.0)
                nc.vector.memset(dcol[:, :], 0.0)
                nc.vector.memset(rtop[:, :], 0.0)
                nc.vector.memset(base[:, :], float(-NB))
                nc.vector.drain()
                nc.vector.memset(cont[:, :, 0:1], 0.0)
                nc.vector.drain().then_inc(s_init, 1)
                dve.sem_inc(s_kf, 1)
                dve.sem_inc(s_pay, 2)

            def window_chain(dve, w, done):
                chain = Chain(dve, s_ch, w * NW)
                chain.n = done
                return chain

            def fields(dve, w):
                step = window_chain(dve, w, 0)
                dve.wait_ge(s_win, w * 32 + 32)
                nc.vector.tensor_copy(meta[:, :, 0:1], cwin[:, :].unsqueeze(2))
                nc.vector.tensor_scalar(f_i[:, 0, :], kwin[:, :], 7, 63, ALU.logical_shift_right, ALU.bitwise_and)
                nc.vector.tensor_scalar(f_i[:, 1, :], kwin[:, :], 20, None, ALU.logical_shift_right)
                nc.vector.tensor_scalar(f_i[:, 2, :], kwin[:, :], P - 1, None, ALU.bitwise_and)
                step(nc.vector.tensor_scalar(f_i[:, 3, :], kwin[:, :], 13, P - 1, ALU.logical_shift_right, ALU.bitwise_and))
                dve.sem_inc(s_kf, 1)
                nc.vector.tensor_scalar(meta[:, :, 1:3], f_i[:, 2:4, :].rearrange("p c t -> p t c"), 1.0, None, ALU.add)
                step(nc.vector.tensor_scalar(inv[:, :], f_i[:, 1, :], dcol[:, :], DROP, ALU.not_equal, ALU.mult))
                nc.vector.tensor_scalar(dcol[:, :], dcol[:, :], 1.0, None, ALU.add)
                step(nc.vector.tensor_tensor(sx[:, :], inv[:, :], f_i[:, 0, :], ALU.add))
                step(nc.vector.tensor_copy(sxb[:, :], sx[:, :]))
                step(nc.vector.tensor_tensor(oh[:, :, :], io_s[:, :, :], sxb[:, :].unsqueeze(1).to_broadcast([P, NB, WT]), ALU.is_equal))
                assert step.n == 5

            def counts(dve, w):
                step = window_chain(dve, w, 5)
                flat = lambda a: a[:, :, :].rearrange("p s j -> p (s j)")
                step(nc.vector.tensor_tensor_scan(flat(run), flat(cont), flat(oh), 0.0, ALU.mult, ALU.add))
                step(nc.vector.tensor_copy(tot[:, :], run[:, :, WT - 1]))
                dve.sem_inc(s_tot, 1)
                assert step.n == 7

            def ranks(dve, w, part):
                step = window_chain(dve, w, 6 + part)
                if part == 1:
                    dve.wait_ge(s_off, w + 1)
                    step(nc.vector.tensor_tensor(rk[:, :, :], run[:, :, :], pR[:, 0:NB].unsqueeze(2).to_broadcast([P, NB, WT]), ALU.add))
                if part == 2:
                    step(nc.vector.tensor_tensor(rk[:, :, :], rk[:, :, :], oh[:, :, :], ALU.mult))
                if part == 3:
                    step(nc.vector.tensor_reduce(rank[:, :], rk[:, :, :].rearrange("p s j -> p j s"), AX, ALU.add))
                    nc.vector.tensor_reduce(rmax[:, :], rank[:, :], AX, ALU.max)
                    step(nc.vector.scalar_tensor_tensor(pos[:, :], rank[:, :], float(NB), sx[:, :], ALU.mult, ALU.add))
                    nc.vector.tensor_tensor(rtop[:, :], rtop[:, :], rmax[:, :], ALU.max)
                    step(nc.vector.tensor_scalar(pos[:, :], pos[:, :], base[:, :], None, ALU.add))
                    step(nc.vector.tensor_scalar(base[:, :], base[:, :], float(NB * P), None, ALU.add))
                    assert step.n == 13

            def rows_out(dve, w, q):
                a, b = chunks[q]
                step = window_chain(dve, w, 13 + q)
                dve.wait_ge(s_g, w * NS + min(2 * q + 2, NS) + 1)
                dve.wait_ge(s_free, w * MC + q + 1)
                nc.vector.tensor_copy(pay[:, a:b, H:PW], meta[:, a:b, :])
                nc.vector.tensor_copy(slot[:, a:b], pos[:, a:b])
                step(nc.vector.tensor_tensor(pay[:, a:b, 0:H], pG[:, q % 2, 0:(b - a) * H].rearrange("p (t f) -> p t f", f=H),
                                             meta[:, a:b, 0].unsqueeze(2).to_broadcast([P, b - a, H]), ALU.mult))
                dve.sem_inc(s_pay, 1)
            win = Windows()
            win.turns, win.chunks = NS + 2, MC
            win.io_s, win.rtop, win.pT = io_s, rtop, pT
            win.load_keys, win.load_attr = load_keys, load_attr
            win.pool_start, win.scatter, win.pool_end = pool_start, scatter, pool_end
            win.pe_start, win.pe_parts, win.offsets = pe_start, pe_parts, offsets
            win.act_start, win.act_parts = act_start, act_parts
            win.dve_start, win.fields, win.counts, win.ranks, win.rows_out = dve_start, fields, counts, ranks, rows_out
            return win

        def adjacency(win, zero):
            NBAT = 8
            BT = 2 * GT
            OB = 8
            with ExitStack() as c:
                kw = sb("kw", [P, 2, GB * GT], I32, c)
                b_i = sb("b_i", [P, GB * GT], I32, c)
                s_i = sb("s_i", [P, GB * GT], I32, c)
                d_i = sb("d_i", [P, GB * GT], I32, c)
                b_f = sb("b_f", [P, GB * GT], BF16, c)
                dl = sb("dl", [P, GB * GT], F32, c)
                lo = sb("lo", [P, GB * GT], F32, c)
                hi = sb("hi", [P, GB * GT], F32, c)
                k2 = sb("k2", [P, GB * GT], F32, c)
                gofs_i = sb("gofs_i", [P, GB * GT], I32, c)
                gofs = sb("gofs", [P, GB * GT], F32, c)
                dbase = sb("dbase", [P, 1], F32, c)
                io_i = sb("io_i", [P, KG], I32, c)
                io_k = sb("io_k", [P, KG], F16, c)
                io_w = sb("io_w", [P, NB, WT], I32, c)
                io_b = sb("io_b", [P, P, BT], BF16, c)
                ohb = sb("ohb", [P, OB, P, BT], BF16, c)
                ohk = sb("ohk", [P, OB, BT, KG], BF16, c)
                adj = sb("adj", [P, 2, NB, P], BF16, c)
                pA = ps("pA", [P, 2, 512], c=c)
                pD = ps("pD", [P, 512], c=c)
                s_io, s_zd, s_clear = sem("a_io"), sem("a_zd"), sem("a_clear")
                s_kw = [sem("a_kw0"), sem("a_kw1")]
                s_fld, s_ch, s_oh, s_grp, s_ev = sem("a_fld"), sem("a_ch"), sem("a_oh"), sem("a_grp"), sem("a_ev")
                s_st = [sem("a_st0"), sem("a_st1")]
                s_deg, s_spgo, s_emb = sem("a_deg"), sem("a_spgo"), sem("a_emb")
                with nc.Block() as block:
                    @block.sync
                    def _(sp):
                        sp.sem_inc(s_zd, 16)
                        with sp.Fori(0, ND // 2) as it:
                            for u in range(2):
                                sp.wait_ge(s_fld, 2 * it + u + 1)
                                sp.sem_inc(s_spgo, 1)
                                for g in range(GB):
                                    at = sp.value_load(group_at[0:1, bass.ds((2 * it + u) * GB + g, 1)], min_val=0, max_val=E - GE)
                                    sp.dma_start(kw[:, u, g * GT:(g + 1) * GT],
                                                 keyT[bass.ds(at, GE)].rearrange("(p j) -> p j", p=P)).then_inc(s_kw[u], 16)
                                if u == 0:
                                    at_w = win.load_keys(sp, it)
                            win.load_attr(sp, it, at_w)
                            sp.wait_ge(s_zd, it * 32 + 16)
                            sp.sem_inc(s_clear, 1)
                            for n in range(2):
                                sp.dma_start(slots_of(2 * it + 2 + n), zero[:, :].unsqueeze(1)).then_inc(s_zd, 16)
                        sp.wait_ge(s_zd, 16 * (ND + 1))

                    @block.gpsimd
                    def _(pool):
                        nc.gpsimd.iota(io_i[:, :], pattern=[[1, KG]], base=0, channel_multiplier=0).then_inc(s_io, 1)
                        nc.gpsimd.iota(gofs_i[:, :], pattern=[[GR, GB], [0, GT]], base=0, channel_multiplier=0).then_inc(s_io, 1)
                        nc.gpsimd.iota(io_w[:, :, :], pattern=[[1, NB], [0, WT]], base=0, channel_multiplier=0).then_inc(s_io, 1)
                        win.pool_start(pool)
                        for b in range(NB):
                            pool.indirect_dma_start(emb_n[:, b, :], None, emb, bass.IndirectOffsetOnAxis(
                                ap=z_sb[:, b:b + 1].bitcast(U32), axis=0)).then_inc(s_emb, 16)
                        with pool.Fori(0, ND // 2) as it:
                            pool.wait_ge(s_clear, it + 1)
                            win.scatter(pool, it)
                        pool.wait_ge(s_emb, 16 * NB)

                    @block.vector
                    def _(dve):
                        dve.wait_ge(s_io, 3)
                        nc.vector.tensor_copy(io_k[:, :], io_i[:, :])
                        nc.vector.tensor_copy(io_b[:, :, :], io_i[:, 0:P].unsqueeze(2).to_broadcast([P, P, BT]))
                        nc.vector.tensor_copy(win.io_s[:, :, :], io_w[:, :, :])
                        win.dve_start(dve)
                        nc.vector.tensor_copy(gofs[:, :], gofs_i[:, :])
                        nc.vector.memset(dbase[:, :], 0.0)
                        nc.vector.drain()
                        dve.sem_inc(s_fld, 2)
                        with dve.Fori(0, ND // 2) as it:
                            for u in range(2):
                                D = 2 * it + u
                                step = Chain(dve, s_ch, D * 5)
                                dve.wait_ge(s_kw[u], it * (16 * GB) + 16 * GB)
                                nc.vector.tensor_scalar(b_i[:, :], kw[:, u, :], P - 1, None, ALU.bitwise_and)
                                nc.vector.tensor_scalar(s_i[:, :], kw[:, u, :], 7, 63, ALU.logical_shift_right, ALU.bitwise_and)
                                step(nc.vector.tensor_scalar(d_i[:, :], kw[:, u, :], 13, None, ALU.logical_shift_right))
                                dve.sem_inc(s_fld, 1)
                                nc.vector.tensor_copy(b_f[:, :], b_i[:, :])
                                step(nc.vector.scalar_tensor_tensor(dl[:, :], d_i[:, :], dbase[:, :], gofs[:, :], ALU.subtract, ALU.subtract))
                                nc.vector.tensor_scalar(lo[:, :], dl[:, :], 0.0, DROP, ALU.is_lt, ALU.mult)
                                nc.vector.tensor_scalar(hi[:, :], dl[:, :], GR - 0.5, DROP, ALU.is_gt, ALU.mult)
                                nc.vector.tensor_scalar(dbase[:, :], dbase[:, :], float(P), None, ALU.add)
                                step(nc.vector.scalar_tensor_tensor(k2[:, :], s_i[:, :], float(GR), dl[:, :], ALU.mult, ALU.add))
                                step(nc.vector.tensor_tensor(lo[:, :], lo[:, :], hi[:, :], ALU.add))
                                step(nc.vector.tensor_tensor(k2[:, :], k2[:, :], lo[:, :], ALU.add))
                                for b in range(NBAT):
                                    dve.wait_ge(s_grp, D * GB + 2 * b + 2)
                                    nc.vector.tensor_tensor(ohb[:, b % OB, :, :], io_b[:, :, :],
                                                            b_f[:, b * BT:(b + 1) * BT].unsqueeze(1).to_broadcast([P, P, BT]), ALU.is_equal)
                                    for j in range(BT):
                                        t = b * BT + j
                                        last = nc.vector.tensor_scalar(ohk[:, b % OB, j, :], io_k[:, :], k2[:, t:t + 1], None, ALU.is_equal)
                                    last.then_inc(s_oh, 1)
                                    turn = u * NBAT + b
                                    if turn == 0:
                                        win.fields(dve, it)
                                    if turn == 1:
                                        win.counts(dve, it)
                                    if 5 <= turn < 8:
                                        win.ranks(dve, it, turn - 4)
                                    if turn >= 7 and turn % 2:
                                        win.rows_out(dve, it, (turn - 7) // 2)
                        dve.wait_ge(s_deg, ND + 2)
                        nc.vector.tensor_copy(deg[:, :], pD[:, 0:2 * ND:2])

                    @block.tensor
                    def _(pe):
                        pe.sem_inc(s_grp, 2 * OB)
                        win.pe_start(pe)
                        with pe.Fori(0, ND // 2) as it:
                            for u in range(2):
                                D = 2 * it + u
                                for b in range(NBAT):
                                    pe.wait_ge(s_oh, D * NBAT + b + 1)
                                    for g in range(2):
                                        n = 2 * b + g
                                        pe.wait_ge(s_ev, D * GB + n + 1)
                                        for j in range(GT):
                                            m = nc.tensor.matmul(pA[:, n % 2, 0:KG], ohb[:, b % OB, :, g * GT + j], ohk[:, b % OB, g * GT + j, :],
                                                                 start=j == 0, stop=j == GT - 1)
                                        m.then_inc(s_grp, 1)
                                    turn = u * NBAT + b
                                    if turn < win.turns:
                                        win.pe_parts(pe, it, turn)
                                    if turn == 1:
                                        win.offsets(pe, it)
                                pe.wait_ge(s_ev, D * GB + GB + 2)
                                for n in range(NB):
                                    m = nc.tensor.matmul(pD[:, bass.ds(2 * D, 2)], adj[:, u, n, :], ones_b[:, :], start=n == 0, stop=n == NB - 1)
                                m.then_inc(s_deg, 1)

                    @block.scalar
                    def _(act):
                        for u in range(2):
                            act.dma_start(adjT[u, :, 0:P], zero[:, 0:P // 2].bitcast(BF16)).then_inc(s_st[u], 16)
                        act.sem_inc(s_ev, 2)
                        act.sem_inc(s_deg, 2)
                        win.act_start(act)
                        with act.Fori(0, ND // 2) as it:
                            for u in range(2):
                                D = 2 * it + u
                                for n in range(GB):
                                    act.wait_ge(s_grp, D * GB + n + 1 + 2 * OB)
                                    if n == 0:
                                        act.wait_ge(s_st[u], it * 16 + 16)
                                        act.wait_ge(s_deg, D + 1)
                                    nc.scalar.activation(adj[:, u, :, n * GR:(n + 1) * GR],
                                                         pA[:, n % 2, 0:KG].rearrange("p (s d) -> p s d", d=GR), ACT.Copy).then_inc(s_ev, 1)
                                    turn = u * NBAT + n // 2
                                    if n % 2 and turn < win.turns:
                                        win.act_parts(act, it, turn)
                                act.wait_ge(s_ev, D * GB + GB + 2)
                                act.dma_start(adjT[bass.ds(D, 1), :, :].rearrange("o p f -> p (o f)"),
                                              adj[:, u, :, :].rearrange("p s d -> p (s d)")).then_inc(s_st[u], 16)
                        for u in range(2):
                            act.wait_ge(s_st[u], 16 * (ND // 2 + 1))

        def split(dve, parts, rest, step):
            step(nc.vector.tensor_scalar(parts[0], rest, 1.0, None, ALU.mult))
            step(nc.vector.tensor_tensor(rest, rest, parts[0], ALU.subtract))
            step(nc.vector.tensor_scalar(parts[1], rest, 1.0, None, ALU.mult))
            step(nc.vector.tensor_tensor(parts[2], rest, parts[1], ALU.subtract))

        def propagate(win, h_all):
            MD = 5
            NM = ND // MD
            assert NM * STEPS // 2 == ND // 2 and NM % 2 == 0
            halves = [(0, 3), (3, 5)]
            H3 = 3 * H
            with ExitStack() as c:
                adj = sb("p_adj", [P, MD, NB * P], BF16, c)
                parts = sb("p_parts", [P, NB, 3, H], BF16, c)
                nparts = sb("p_nparts", [P, ND, 3, H], BF16, c)
                x08 = sb("p_x08", [P, ND, H], F32, c)
                g_all = sb("p_g", [P, ND, H], F32, c)
                dinv = sb("p_dinv", [P, ND], F32, c)
                dinv02 = sb("p_dinv02", [P, ND], F32, c)
                root = sb("p_root", [P, ND], F32, c)
                rest = sb("p_rest", [P, 3, H], F32, c)
                acc = sb("p_acc", [P, 3, H], F32, c)
                pL = ps("pL", [P, 2, 512], c=c)
                s_dv, s_ds = sem("p_dv"), sem("p_ds")
                s_A = [sem(f"p_A{q}") for q in range(MD)]
                s_pz = sem("p_pz")
                s_upd = [sem("p_upd0"), sem("p_upd1")]
                s_gp = sem("p_gp")
                s_ch, s_gone, s_spgo = sem("p_ch"), sem("p_gone"), sem("p_spgo")
                wide = lambda a, n: a.unsqueeze(2).to_broadcast([P, n, H])
                NCH = 18
                TURNS0 = 6

                def iterations(eng, body, before=None, after=None):
                    with eng.Fori(0, STEPS) as k:
                        if before:
                            before(k)
                        with eng.Fori(0, NM // 2) as m2:
                            for v in range(2):
                                body(k * NM + 2 * m2 + v, (2 * m2 + v) * MD, v, k * (NM // 2) + m2 + ND // 2)
                        if after:
                            after(k)

                with nc.Block() as block:
                    @block.sync
                    def _(sp):
                        def body(it, D, v, w):
                            for q in range(MD):
                                sp.wait_ge(s_pz, it * MD + q + 1)
                                sp.sem_inc(s_spgo, 1)
                                sp.dma_start(adj[:, q, :], adjT[bass.ds(D + q, 1), :, :].rearrange("o p f -> p (o f)")).then_inc(s_A[q], 16)
                                if v == 0 and q == 0:
                                    at = win.load_keys(sp, w)
                                    win.load_attr(sp, w, at)
                        iterations(sp, body)

                    @block.gpsimd
                    def _(pool):
                        with pool.Fori(ND // 2, ND) as w:
                            win.scatter(pool, w)
                        win.pool_end(pool)

                    @block.tensor
                    def _(pe):
                        pe.sem_inc(s_pz, MD)

                        def before(k):
                            pe.wait_ge(s_gp, k + 1)
                            pe.sem_inc(s_gone, 1)

                        def body(it, D, v, w):
                            piece = 0
                            for q in range(MD):
                                half = 0 if q < halves[0][1] else 1
                                o = q - halves[half][0]
                                pe.wait_ge(s_A[q], it * 16 + 16)
                                if o == 0:
                                    pe.wait_ge(s_upd[half], it + 1)
                                for a, b in ((0, 13), (13, 25), (25, 37), (37, NB)):
                                    for n in range(a, b):
                                        x_ = nc.tensor.matmul(pL[:, half, o * H3:(o + 1) * H3], adj[:, q, n * P:(n + 1) * P],
                                                              parts[:, n, :, :].rearrange("p t f -> p (t f)"), start=n == 0, stop=n == NB - 1)
                                    if b == NB:
                                        x_.then_inc(s_pz, 1)
                                    if piece % 3 == 0 and piece // 3 < TURNS0:
                                        turn = piece // 3 + v * TURNS0
                                        if turn < win.turns:
                                            win.pe_parts(pe, w, turn)
                                    if v == 0 and piece == 10:
                                        win.offsets(pe, w)
                                    piece += 1
                        iterations(pe, body, before=before)

                    @block.scalar
                    def _(act):
                        act.wait_ge(s_dv, 1)
                        nc.scalar.activation(root[:, :], root[:, :], ACT.Sqrt).then_inc(s_ds, 1)
                        with act.Fori(ND // 2, ND) as w:
                            for turn in range(win.turns):
                                win.act_parts(act, w, turn)

                    @block.vector
                    def _(dve):
                        nc.vector.tensor_scalar(root[:, :], deg[:, :], 1.0, None, ALU.add).then_inc(s_dv, 1)
                        nc.vector.memset(x08[:, ND - 1, :], 0.0)
                        nc.vector.memset(g_all[:, ND - 1, :], 0.0)
                        nc.vector.tensor_scalar(x08[:, 0:NB, :], x_sb[:, :, :], ALPHA, None, ALU.mult)
                        dve.wait_ge(s_ds, 1)
                        nc.vector.reciprocal(dinv[:, :], root[:, :])
                        nc.vector.drain()
                        nc.vector.tensor_scalar(dinv02[:, :], dinv[:, :], 1.0 - ALPHA, None, ALU.mult)
                        nc.vector.tensor_tensor(g_all[:, 0:NB, :], x_sb[:, :, :], wide(dinv[:, 0:NB], NB), ALU.mult)
                        nc.vector.drain()
                        nc.vector.tensor_copy(h_all[:, :, :], g_all[:, :, :])
                        nc.vector.drain()
                        split(dve, [parts[:, :, t, :] for t in range(3)], h_all[:, 0:NB, :], lambda i: nc.vector.drain())
                        nc.vector.drain().then_inc(s_gp, 1)
                        dve.sem_inc(s_upd[0], 1)
                        dve.sem_inc(s_upd[1], 1)

                        def update(it, D, step, half):
                            a, b = halves[half]
                            n = b - a
                            at = bass.ds(D + a, n)
                            dve.wait_ge(s_pz, it * MD + b + MD)
                            step(nc.vector.tensor_reduce(acc[:, 0:n, :], pL[:, half, 0:n * H3].rearrange("p (d t f) -> p d f t", t=3, f=H), AX, ALU.add))
                            dve.sem_inc(s_upd[half], 1)
                            step(nc.vector.tensor_tensor(acc[:, 0:n, :], acc[:, 0:n, :], g_all[:, at, :], ALU.add))
                            step(nc.vector.tensor_tensor(acc[:, 0:n, :], acc[:, 0:n, :], wide(dinv02[:, at], n), ALU.mult))
                            step(nc.vector.tensor_tensor(h_all[:, at, :], acc[:, 0:n, :], x08[:, at, :], ALU.add))
                            step(nc.vector.tensor_tensor(rest[:, 0:n, :], h_all[:, at, :], wide(dinv[:, at], n), ALU.mult))
                            nc.vector.tensor_scalar(g_all[:, at, :], rest[:, 0:n, :], 1.0, None, ALU.mult)
                            split(dve, [nparts[:, at, t, :] for t in range(3)], rest[:, 0:n, :], step)

                        def body(it, D, v, w):
                            step = Chain(dve, s_ch, it * NCH)
                            if v == 0:
                                win.fields(dve, w)
                                win.counts(dve, w)
                                for part in (1, 2, 3):
                                    win.ranks(dve, w, part)
                                win.rows_out(dve, w, 0)
                                update(it, D, step, 0)
                                win.rows_out(dve, w, 1)
                            else:
                                win.rows_out(dve, w, 2)
                                win.rows_out(dve, w, 3)
                                update(it, D, step, 0)
                                win.rows_out(dve, w, 4)
                            update(it, D, step, 1)
                            assert step.n == NCH

                        def after(k):
                            nc.vector.tensor_copy(parts[:, :, :, :].rearrange("p s t f -> p (s t f)"),
                                                  nparts[:, 0:NB, :, :].rearrange("p s t f -> p (s t f)"))
                            nc.vector.drain().then_inc(s_gp, 1)
                        iterations(dve, body, after=after)

                with nc.Block() as block:
                    rrow = sb("p_rrow", [1, 4], F32, c)
                    s_tr = sem("p_tr")

                    @block.tensor
                    def _(pe):
                        nc.tensor.transpose(win.pT[0:1, 0:P], win.rtop[:, :], ident[:, :]).then_inc(s_tr, 1)

                    @block.vector
                    def _(dve):
                        dve.wait_ge(s_tr, 1)
                        nc.vector.tensor_reduce(rrow[:, 0:1], win.pT[0:1, 0:P], AX, ALU.max)
                        nc.vector.drain()
                        nc.vector.tensor_scalar(flags[:, 3:4], rrow[:, 0:1], P + 0.5, None, ALU.is_gt)
                        nc.vector.drain()
                        nc.vector.tensor_reduce(rrow[:, 1:2], flags[:, :], AX, ALU.add)
                        nc.vector.drain()
                        nc.vector.tensor_scalar(rrow[:, 1:2], rrow[:, 1:2], 1.0, None, ALU.min)
                        nc.vector.drain()
                        nc.vector.tensor_copy(flag_i[:, :], rrow[:, 1:2])

        def convolve(agg):
            with ExitStack() as c:
                NCK = NB // CH
                W1c = H + 1
                AHEAD = 4
                tabp = sb("c_tab", [P, ND, 3, WD], BF16, c)
                embp = sb("c_emb", [P, NB, 3, G], BF16, c)
                big = sb("c_big", [P, NB, WD], F32, c)
                cur = sb("c_cur", [P, 2, 3, WD], BF16, c)
                rows = sb("c_rows", [P, 2, NB, PW], F32, c)
                io_i = sb("c_ioi", [P, P], I32, c)
                io_b = sb("c_iob", [P, P, CH], BF16, c)
                ends = sb("c_ends", [P, 2, 2, NB], BF16, c)
                ohd = sb("c_ohd", [P, NCK, P, CH], BF16, c)
                ohs = sb("c_ohs", [P, NCK, P, CH], BF16, c)
                ohdT = sb("c_ohdT", [P, 2, CH, P], BF16, c)
                ohsT = sb("c_ohsT", [P, 2, CH, P], BF16, c)
                es = sb("c_es", [P, 2, CH, G], F32, c)
                pr = sb("c_pr", [P, CH, G], F32, c)
                ad = sb("c_ad", [P, CH], F32, c)
                ac = sb("c_ac", [P, CH], F32, c)
                gx = sb("c_gx", [P, CH, W1c], F32, c)
                msg = sb("c_msg", [P, 2, CH, W1c], F32, c)
                mp = sb("c_mp", [P, 2, 3, CH, W1c], BF16, c)
                pD = ps("cD", [P, 1024], BF16, c)
                pS = ps("cS", [P, 1024], BF16, c)
                pG = ps("cG", [P, 2, 8, P], c=c)
                pO = ps("cO", [P, 2, 512], c=c)
                s_io, s_rdy, s_spgo = sem("c_io"), sem("c_rdy"), sem("c_spgo")
                s_rows = [sem("c_rows0"), sem("c_rows1")]
                s_oh, s_Td, s_Ts, s_TCd, s_TC, s_G, s_es, s_ac, s_gx = (
                    sem("c_oh"), sem("c_Td"), sem("c_Ts"), sem("c_TCd"), sem("c_TC"), sem("c_G"), sem("c_es"), sem("c_ac"), sem("c_gx"))
                s_msg, s_p0, s_r, s_p1, s_p2, s_O, s_agg = (sem("c_msg"), sem("c_p0"), sem("c_r"), sem("c_p1"), sem("c_p2"),
                                                            sem("c_O"), sem("c_agg"))
                s_ch, s_cur, s_done = sem("c_ch"), sem("c_cur"), sem("c_done")
                PAIRS, ALL = ND // 2, ND * NCK

                def pairs(eng, body):
                    with eng.Fori(0, PAIRS - 1) as it:
                        for k in range(2 * NCK):
                            body(it, k, it * (2 * NCK) + k, False)
                    for k in range(2 * NCK):
                        body(PAIRS - 1, k, (PAIRS - 1) * (2 * NCK) + k, True)

                with nc.Block() as block:
                    @block.sync
                    def _(sp):
                        with sp.Fori(0, PAIRS) as it:
                            for u in range(2):
                                sp.wait_ge(s_done, 2 * it + u + 1)
                                sp.sem_inc(s_spgo, 1)
                                sp.dma_start(rows[:, u, :, :].rearrange("p s w -> p (s w)").unsqueeze(1),
                                             slots_of(2 * it + u)).then_inc(s_rows[u], 16)

                    @block.gpsimd
                    def _(pool):
                        nc.gpsimd.iota(io_i[:, :], pattern=[[1, P]], base=1, channel_multiplier=0).then_inc(s_io, 1)
                        pool.wait_ge(s_rdy, 1)
                        pool.sem_inc(s_p2, 1)

                        def without_first(k, i):
                            m = msg[:, (k - 1) % 2, :, :]
                            pool.wait_ge(s_p0, i + 1)
                            nc.gpsimd.tensor_tensor(m, m, mp[:, (k - 1) % 2, 0, :, :], ALU.subtract).then_inc(s_r, 1)

                        def third_part(k, i):
                            pool.wait_ge(s_p1, i + 1)
                            nc.gpsimd.tensor_tensor(mp[:, (k - 1) % 2, 2, :, :], msg[:, (k - 1) % 2, :, :], mp[:, (k - 1) % 2, 1, :, :],
                                                    ALU.subtract).then_inc(s_p2, 1)

                        def body(it, k, i, last):
                            u, ck = divmod(k, NCK)
                            S = slice(ck * CH, (ck + 1) * CH)
                            without_first(k, i)
                            pool.wait_ge(s_ac, i + 1)
                            nc.gpsimd.tensor_tensor(gx[:, :, 0:H], rows[:, u, S, 0:H], ac[:, :].unsqueeze(2).to_broadcast([P, CH, H]),
                                                    ALU.add).then_inc(s_gx, 1)
                            third_part(k, i)
                        pairs(pool, body)
                        without_first(0, ALL)
                        third_part(0, ALL)

                    @block.vector
                    def _(dve):
                        dr = lambda i: nc.vector.drain()
                        nc.vector.memset(tabp[:, ND - 1, :, :], 0.0)
                        nc.vector.memset(agg[:, :, :], 0.0)
                        nc.vector.memset(gx[:, :, :], 1.0)
                        nc.vector.memset(pO[:, 1, 0:CH * W1c], 0.0)
                        nc.vector.memset(msg[:, 1, :, :], 0.0)
                        nc.vector.memset(mp[:, 0, :, :, :], 0.0)
                        nc.vector.memset(ohs[:, NCK - 2:NCK, :, :], 0.0)
                        dve.wait_ge(s_io, 1)
                        nc.vector.tensor_copy(io_b[:, :, :], io_i[:, :].unsqueeze(2).to_broadcast([P, P, CH]))
                        nc.vector.tensor_copy(big[:, :, :], dst_n[:, :, :])
                        nc.vector.drain()
                        split(dve, [tabp[:, 0:NB, t, :] for t in range(3)], big[:, :, :], dr)
                        nc.vector.drain()
                        nc.vector.tensor_copy(big[:, :, 0:G], emb_n[:, :, :])
                        nc.vector.drain()
                        split(dve, [embp[:, :, t, :] for t in range(3)], big[:, :, 0:G], dr)
                        nc.vector.drain().then_inc(s_rdy, 1)
                        dve.sem_inc(s_done, 2)
                        dve.sem_inc(s_msg, 2)
                        dve.sem_inc(s_agg, 1)

                        def add_sums(k, i):
                            ck, par = (k - 3) % NCK, (k - 3) % 2
                            A = agg[:, ck * CH:(ck + 1) * CH, :]
                            dve.wait_ge(s_O, i + 2)
                            nc.vector.tensor_tensor(A, A, pO[:, par, 0:CH * W1c].rearrange("p (s w) -> p s w", w=W1c), ALU.add).then_inc(s_agg, 1)

                        def take_ends(u):
                            nc.vector.tensor_copy(ends[:, u, :, :], rows[:, u, :, H + 1:H + 3].rearrange("p s e -> p e s"))
                            nc.vector.drain()

                        def onehot(oh, k, end):
                            u, ck = k % (2 * NCK) // NCK, k % NCK
                            return nc.vector.tensor_tensor(oh[:, ck, :, :], io_b[:, :, :],
                                                           ends[:, u, end, ck * CH:(ck + 1) * CH].unsqueeze(1).to_broadcast([P, P, CH]), ALU.is_equal)

                        dve.wait_ge(s_rows[0], 16)
                        take_ends(0)
                        for k in range(AHEAD):
                            onehot(ohd, k, 1)
                            onehot(ohs, k, 0).then_inc(s_oh, 1)

                        def body(it, k, i, last):
                            u, ck = divmod(k, NCK)
                            par = k % 2
                            k_a = k + AHEAD
                            ahead = not last or k_a < 2 * NCK
                            g = pG[:, par, 0:CH, :]
                            dve.wait_ge(s_es, i + 1)
                            nc.vector.tensor_tensor(pr[:, :, :], es[:, par, :, :], g[:, :, W1c:WD], ALU.mult).then_inc(s_ch, 1)
                            add_sums(k, i)
                            dve.wait_ge(s_ch, 2 * i + 1)
                            nc.vector.tensor_reduce(ad[:, :], pr[:, :, :], AX, ALU.add).then_inc(s_ch, 1)
                            dve.wait_ge(s_ch, 2 * i + 2)
                            nc.vector.tensor_tensor(ac[:, :], ad[:, :], rows[:, u, ck * CH:(ck + 1) * CH, H], ALU.mult).then_inc(s_ac, 1)
                            if ahead:
                                if k_a % NCK == 0:
                                    u_a = k_a // NCK % 2
                                    dve.wait_ge(s_rows[u_a], (it + k_a // (2 * NCK)) * 16 + 16)
                                    take_ends(u_a)
                                dve.wait_ge(s_O, i + 2)
                                onehot(ohd, k_a, 1)
                                onehot(ohs, k_a, 0).then_inc(s_oh, 1)
                            dve.wait_ge(s_p2, i + 1)
                            dve.wait_ge(s_gx, i + 1)
                            nc.vector.tensor_tensor(msg[:, par, :, :], gx[:, :, :], g[:, :, 0:W1c], ALU.mult).then_inc(s_msg, 1)
                            if ck == NCK - 1:
                                dve.sem_inc(s_done, 1)
                        pairs(dve, body)
                        for k in range(2):
                            add_sums(k, ALL + k)
                        add_sums(2, ALL + 2)

                    @block.scalar
                    def _(act):
                        act.wait_ge(s_rdy, 1)

                        def load_cur(D, u):
                            nc.scalar.activation(cur[:, u, :, :], tabp[:, D, :, :].rearrange("p o t w -> p (o t) w"), ACT.Copy).then_inc(s_cur, 1)

                        def copy_d(k, i):
                            act.wait_ge(s_Td, i + 1)
                            nc.scalar.activation(ohdT[:, k % 2, :, :].rearrange("p s e -> p (s e)"), pD[:, 0:CH * P], ACT.Copy).then_inc(s_TCd, 1)

                        def copy_s(k, i):
                            act.wait_ge(s_Ts, i + 1)
                            nc.scalar.activation(ohsT[:, k % 2, :, :].rearrange("p s e -> p (s e)"), pS[:, 0:CH * P], ACT.Copy).then_inc(s_TC, 1)

                        def first_part(k, i):
                            act.wait_ge(s_msg, i + 2)
                            act.wait_ge(s_O, i + 2)
                            nc.scalar.activation(mp[:, (k - 1) % 2, 0, :, :], msg[:, (k - 1) % 2, :, :], ACT.Copy).then_inc(s_p0, 1)

                        def second_part(k, i):
                            act.wait_ge(s_r, i + 1)
                            nc.scalar.activation(mp[:, (k - 1) % 2, 1, :, :], msg[:, (k - 1) % 2, :, :], ACT.Copy).then_inc(s_p1, 1)

                        load_cur(slice(0, 1), 0)
                        for k in range(2):
                            copy_d(k, k)
                            copy_s(k, k)

                        def body(it, k, i, last):
                            u, ck = divmod(k, NCK)
                            more = not last or k + 2 < 2 * NCK
                            act.wait_ge(s_G, i + 1)
                            nc.scalar.activation(es[:, k % 2, :, :], pG[:, k % 2, 0:CH, WD:WD + G], ACT.Copy).then_inc(s_es, 1)
                            first_part(k, i)
                            if more:
                                copy_d(k + 2, i + 2)
                            second_part(k, i)
                            if more:
                                copy_s(k + 2, i + 2)
                            if ck == 3 and not (last and u == 1):
                                load_cur(bass.ds(2 * it + u + 1, 1), 1 - u)
                        pairs(act, body)
                        first_part(0, ALL)
                        second_part(0, ALL)

                    @block.tensor
                    def _(pe):
                        pe.wait_ge(s_rdy, 1)
                        pe.sem_inc(s_O, 2)

                        def transposes(k, i, first):
                            b = k % NCK
                            pe.wait_ge(s_oh, i + 1)
                            if not first:
                                pe.wait_ge(s_TCd, i)
                            for j in range(CH):
                                m = nc.tensor.transpose(pD[:, j * P:(j + 1) * P], ohd[:, b, :, j], ident_b[:, :])
                            m.then_inc(s_Td, 1)
                            if not first:
                                pe.wait_ge(s_TC, i)
                            for j in range(CH):
                                m = nc.tensor.transpose(pS[:, j * P:(j + 1) * P], ohs[:, b, :, j], ident_b[:, :])
                            m.then_inc(s_Ts, 1)

                        def sums(k, i):
                            pe.wait_ge(s_p2, i + 1)
                            pe.wait_ge(s_agg, i + 1)
                            for j in range(CH):
                                for t in range(3):
                                    m = nc.tensor.matmul(pO[:, k % 2, j * W1c:(j + 1) * W1c], ohs[:, (k - 2) % NCK, :, j], mp[:, k % 2, t, j, :],
                                                         start=t == 0, stop=t == 2)
                            m.then_inc(s_O, 1)

                        for k in range(2):
                            transposes(k, k, k == 0)

                        def body(it, k, i, last):
                            u, ck = divmod(k, NCK)
                            par = k % 2
                            pe.wait_ge(s_TC, i + 1)
                            if ck == 0:
                                pe.wait_ge(s_cur, 2 * it + u + 1)
                            pe.wait_ge(s_msg, i + 1)
                            for j in range(CH):
                                for t in range(3):
                                    nc.tensor.matmul(pG[:, par, j, 0:WD], ohdT[:, par, j, :], cur[:, u, t, :], start=t == 0, stop=t == 2)
                                for t in range(3):
                                    m = nc.tensor.matmul(pG[:, par, j, WD:WD + G], ohsT[:, par, j, :], embp[:, ck * CH + j, t, :], start=t == 0, stop=t == 2)
                            m.then_inc(s_G, 1)
                            if not last or k + 2 < 2 * NCK:
                                transposes(k + 2, i + 2, False)
                            sums(k, i)
                        pairs(pe, body)
                        for k in range(2):
                            sums(k, ALL + k)

        def layer_norm_parts(name, t, tmp):
            s_var, s_std = sem(name + "_var"), sem(name + "_std")
            wide = lambda a: a[:, :].unsqueeze(2).to_broadcast([P, NB, H])

            def vector(dve):
                nc.vector.tensor_reduce(s1[:, :], t, AX, ALU.add)
                nc.vector.drain()
                nc.vector.tensor_scalar(s1[:, :], s1[:, :], 1.0 / H, None, ALU.mult)
                nc.vector.drain()
                nc.vector.tensor_tensor(t, t, wide(s1), ALU.subtract)
                nc.vector.drain()
                nc.vector.tensor_tensor(tmp, t, t, ALU.mult)
                nc.vector.drain()
                nc.vector.tensor_reduce(s2[:, :], tmp, AX, ALU.add).then_inc(s_var, 1)
                dve.wait_ge(s_std, 1)
                nc.vector.reciprocal(s2[:, :], s1[:, :])
                nc.vector.drain()
                nc.vector.tensor_tensor(t, t, wide(s2), ALU.mult)
                nc.vector.drain()

            def scalar(act):
                act.wait_ge(s_var, 1)
                nc.scalar.activation(s1[:, :], s2[:, :], ACT.Sqrt, bias=epsc[:, :], scale=1.0 / H).then_inc(s_std, 1)

            return vector, scalar

        def node_block(name, vector, scalar=None, load=None, store=(), beside=None):
            s_in, s_v, s_out = sem(name + "_in"), sem(name + "_vec"), sem(name + "_out")
            with nc.Block() as block:
                @block.sync
                def _(sp):
                    if load:
                        sp.dma_start(load[0], load[1]).then_inc(s_in, 16)
                        sp.wait_ge(s_in, 16)
                    sp.wait_ge(s_v, 1)
                    for to, what in store:
                        sp.dma_start(to, what).then_inc(s_out, 16)
                    if store:
                        sp.wait_ge(s_out, 16 * len(store))

                @block.vector
                def _(dve):
                    if load:
                        dve.wait_ge(s_in, 16)
                    vector(dve)
                    nc.vector.drain().then_inc(s_v, 1)

                if beside:
                    with ExitStack() as c:
                        copies = beside(block, c)

                        @block.scalar
                        def _(act):
                            copies(act)
                            scalar(act)
                elif scalar:
                    block.scalar(scalar)

        bcast = lambda a: a[:, :].unsqueeze(2).to_broadcast([P, NB, H])

        def norm0_block(h, tmp, store=(), beside=None):
            ln, ln_s = layer_norm_parts("ln0", x_sb[:, :, :], tmp)

            def first_norm(dve):
                nc.vector.tensor_tensor(x_sb[:, :, :], x_sb[:, :, :], h, ALU.add)
                nc.vector.drain()
                ln(dve)
                nc.vector.tensor_copy(dst_n[:, :, H:H + 1], mult[:, :].unsqueeze(2))
                nc.vector.tensor_tensor(dst_n[:, :, 0:H], x_sb[:, :, :], bcast(mult), ALU.mult)
            node_block("norm0", first_norm, ln_s, store=store, beside=beside)

        def final_block(agg, v, h, tmp, load=None):
            ln1, ln1s = layer_norm_parts("ln1", v, tmp)
            ln2, ln2s = layer_norm_parts("ln2", h, tmp)

            def last(dve):
                nc.vector.tensor_scalar(s1[:, :], agg[:, :, H], 1e-8, None, ALU.max)
                nc.vector.drain()
                nc.vector.reciprocal(s2[:, :], s1[:, :])
                nc.vector.drain()
                nc.vector.tensor_tensor(v, agg[:, :, 0:H], bcast(s2), ALU.mult)
                nc.vector.drain()
                nc.vector.tensor_tensor(v, v, x_sb[:, :, :], ALU.add)
                nc.vector.drain()
                ln1(dve)
                nc.vector.tensor_tensor(v, v, gb[:, 0, :].unsqueeze(1).to_broadcast([P, NB, H]), ALU.mult)
                nc.vector.drain()
                nc.vector.tensor_tensor(v, v, gb[:, 1, :].unsqueeze(1).to_broadcast([P, NB, H]), ALU.add)
                nc.vector.drain()
                nc.vector.tensor_tensor(h, v, x_sb[:, :, :], ALU.add)
                nc.vector.drain()
                ln2(dve)

            def last_s(act):
                ln1s(act)
                ln2s(act)
            node_block("final", last, last_s, load=load, store=[
                (out[0:(NB - 1) * P, :].rearrange("(b p) w -> p b w", p=P), h[:, 0:NB - 1, :]),
                (out[(NB - 1) * P:N, :], h[0:LAST, NB - 1, :])])

        def fast_path():
            with ExitStack() as c:
                h_all = sb("h_all", [P, ND, H], F32, c)
                with ExitStack() as w:
                    zero = sb("zero", [P, NB * PW], F32, w)
                    with own_semaphores():
                        index_edges(zero)
                    with own_semaphores():
                        win = edge_windows(w)
                        adjacency(win, zero)
                        propagate(win, h_all)
                tmp = sb("n_tmp", [P, NB, H], F32, c)
                agg = sb("n_agg", [P, NB, H + 1], F32, c)
                v = sb("n_v", [P, NB, H], F32, c)
                with own_semaphores():
                    norm0_block(h_all[:, 0:NB, :], tmp[:, :, :], beside=adapted)
                with own_semaphores():
                    convolve(agg)
                with own_semaphores():
                    final_block(agg, v[:, :, :], h_all[:, 0:NB, :], tmp[:, :, :])

        def general_path():
            with ExitStack() as c:
                sb_ = lambda name, shape, dt=F32: sb(name, shape, dt, c)
                h_sb, u_sb, v_sb = sb_("h_sb", [P, NB, H]), sb_("u_sb", [P, NB, H]), sb_("v_sb", [P, NB, H])
                g_sb, dinv = sb_("g_sb", [P, NB, H]), sb_("g_dinv", [P, NB])
                zrow = sb_("zrow", [P, NB, H + 1])
                ew, cw = sb_("g_ew", [SP_, ST]), sb_("g_cw", [SP_, ST])
                src_sb, dst_sb = sb_("g_src", [SP_, ST], I32), sb_("g_dst", [SP_, ST], I32)
                kf, ku, su = sb_("kf", [SP_, 1]), sb_("ku", [SP_, 1], U32), sb_("su", [SP_, 1], U32)
                wf, wu, cwc = sb_("wf", [SP_, 1]), sb_("wu", [SP_, 1], U32), sb_("cwc", [SP_, 1])
                diag, eq, dup = sb_("diag", [SP_, SP_]), sb_("eq", [SP_, SP_]), sb_("dup", [SP_, SP_])
                rows, cur = sb_("rows", [SP_, H + 1]), sb_("cur", [SP_, H + 1])
                dstrow, srcrow, prod, ad = sb_("dstrow", [SP_, WD]), sb_("srcrow", [SP_, G]), sb_("prod", [SP_, G]), sb_("ad", [SP_, 1])
                attr, attrT, hid = sb_("attr", [SP_, R]), sb_("attrT", [R, SP_]), sb_("hid", [H + 1, SP_])
                pk, psum_rows, pa, ph, pg = (ps(n, [P, 512], F32, c) for n in ("pk", "psum_rows", "pa", "ph", "pg"))

                def zero_table(name, table, W):
                    s = sem(name)
                    with nc.Block() as block:
                        @block.sync
                        def _(sp):
                            sp.dma_start(nodes(table), zrow[:, :, 0:W]).then_inc(s, 16)
                            sp.wait_ge(s, 16)

                def add_pass(name, table, W, key, other, messages):
                    s_free = sem(name + "_free")
                    s_key = sem(name + "_key")
                    s_go = sem(name + "_go")
                    s_gath = [sem(f"{name}_gath{n}") for n in range(3 if messages else 2)]
                    s_kt = sem(name + "_kt")
                    s_eq = sem(name + "_eq")
                    s_msg = sem(name + "_msg")
                    s_sum = sem(name + "_sum")
                    s_new = sem(name + "_new")
                    s_scat = sem(name + "_scat")
                    s_attr, s_aT, s_aTc = sem(name + "_attr"), sem(name + "_aT"), sem(name + "_aTc")
                    s_h, s_hc, s_g = sem(name + "_h"), sem(name + "_hc"), sem(name + "_g")
                    s_v, s_pe = sem(name + "_v"), sem(name + "_pe")
                    NV = 13 if messages else 7

                    with nc.Block() as block:
                        @block.gpsimd
                        def _(pool):
                            pool.sem_inc(s_free, 1)
                            with pool.Fori(0, ST) as t:
                                pool.wait_ge(s_key, t + 1)
                                pool.sem_inc(s_go, 1)
                                off = lambda a: bass.IndirectOffsetOnAxis(ap=a[:, :], axis=0)
                                pool.indirect_dma_start(cur[:, 0:W], None, table, off(ku)).then_inc(s_gath[0], 16)
                                if messages:
                                    pool.indirect_dma_start(dstrow[:, :], None, dstT, off(su)).then_inc(s_gath[1], 16)
                                    pool.indirect_dma_start(srcrow[:, :], None, srcT, off(ku)).then_inc(s_gath[2], 16)
                                else:
                                    pool.indirect_dma_start(rows[:, 0:W], None, gT, off(su)).then_inc(s_gath[1], 16)
                                pool.wait_ge(s_new, t + 1)
                                pool.sem_inc(s_go, 1)
                                pool.indirect_dma_start(table, off(wu), cur[:, 0:W], None, bounds_check=NP - 1,
                                                        oob_is_err=False).then_inc(s_scat, 16)
                                pool.wait_ge(s_scat, t * 16 + 16)
                                pool.sem_inc(s_free, 1)

                        @block.vector
                        def _(dve):
                            with dve.Fori(0, ST) as t:
                                step = Chain(dve, s_v, t * NV)
                                dve.wait_ge(s_free, t + 1)
                                nc.vector.tensor_copy(kf[:, :], key[:, bass.ds(t, 1)])
                                nc.vector.tensor_copy(ku[:, :], key[:, bass.ds(t, 1)])
                                step(nc.vector.tensor_copy(su[:, :], other[:, bass.ds(t, 1)]))
                                dve.sem_inc(s_key, 1)
                                step(nc.vector.tensor_scalar(diag[:, :], ident[0:SP_, 0:SP_], kf[:, :], None, ALU.mult))
                                dve.sem_inc(s_eq, 1)
                                dve.wait_ge(s_kt, t + 1)
                                step(nc.vector.tensor_scalar(eq[:, :], pk[0:SP_, 0:SP_], kf[:, :], None, ALU.is_equal))
                                step(nc.vector.tensor_tensor(dup[:, :], eq[:, :], below[0:SP_, 0:SP_], ALU.mult))
                                step(nc.vector.tensor_reduce(wf[:, :], dup[:, :], AX, ALU.max))
                                step(nc.vector.tensor_scalar(wu[:, :], wf[:, :], float(1 << 20), kf[:, :], ALU.mult, ALU.add))
                                for s in s_gath:
                                    dve.wait_ge(s, t * 16 + 16)
                                if messages:
                                    step(nc.vector.tensor_copy(cwc[:, :], cw[:, bass.ds(t, 1)]))
                                    step(nc.vector.tensor_tensor(prod[:, :], dstrow[:, H + 1:WD], srcrow[:, :], ALU.mult))
                                    step(nc.vector.tensor_reduce(ad[:, :], prod[:, :], AX, ALU.add))
                                    dve.wait_ge(s_g, t + 1)
                                    step(nc.vector.tensor_scalar(rows[:, 0:H], pg[0:SP_, 0:H], ad[:, :], cwc[:, :], ALU.add, ALU.mult))
                                    step(nc.vector.tensor_tensor(rows[:, 0:H], rows[:, 0:H], dstrow[:, 0:H], ALU.mult))
                                    step(nc.vector.tensor_copy(rows[:, H:H + 1], dstrow[:, H:H + 1]))
                                dve.sem_inc(s_msg, 1)
                                dve.wait_ge(s_sum, t + 1)
                                step(nc.vector.tensor_tensor(cur[:, 0:W], cur[:, 0:W], psum_rows[0:SP_, 0:W], ALU.add))
                                dve.sem_inc(s_new, 1)
                                assert step.n == NV

                        @block.tensor
                        def _(pe):
                            with pe.Fori(0, ST) as t:
                                if messages:
                                    pe.wait_ge(s_attr, t * 16 + 16)
                                    pe.sem_inc(s_pe, 1)
                                    nc.tensor.transpose(pa[0:R, 0:SP_], attr[:, :], ident[0:SP_, 0:SP_]).then_inc(s_aT, 1)
                                    pe.wait_ge(s_aTc, t + 1)
                                    pe.sem_inc(s_pe, 1)
                                    nc.tensor.matmul(ph[0:H, 0:SP_], w1T[:, :], attrT[:, :]).then_inc(s_h, 1)
                                    pe.wait_ge(s_hc, t + 2)
                                    pe.sem_inc(s_pe, 1)
                                    nc.tensor.matmul(pg[0:SP_, 0:H], hid[:, :], w2T[:, :]).then_inc(s_g, 1)
                                pe.wait_ge(s_eq, t + 1)
                                nc.tensor.matmul(pk[0:SP_, 0:SP_], ones[0:SP_, 0:SP_], diag[:, :]).then_inc(s_kt, 1)
                                pe.wait_ge(s_msg, t + 1)
                                nc.tensor.matmul(psum_rows[0:SP_, 0:W], eq[:, :], rows[:, 0:W]).then_inc(s_sum, 1)

                        if messages:
                            @block.sync
                            def _(sp):
                                tiles = edge_attr.rearrange("(p j) f -> p j f", p=SP_)
                                with sp.Fori(0, ST) as t:
                                    sp.wait_ge(s_free, t + 1)
                                    sp.dma_start(attr[:, :], tiles[:, bass.ds(t, 1), :].rearrange("p o f -> p (o f)")).then_inc(s_attr, 16)

                            @block.scalar
                            def _(act):
                                nc.scalar.activation(hid[:, :], ones[0:H + 1, 0:SP_], ACT.Copy).then_inc(s_hc, 1)
                                act.wait_ge(s_hc, 1)
                                with act.Fori(0, ST) as t:
                                    act.wait_ge(s_aT, t + 1)
                                    nc.scalar.activation(attrT[:, :], pa[0:R, 0:SP_], ACT.Copy).then_inc(s_aTc, 1)
                                    act.wait_ge(s_h, t + 1)
                                    nc.scalar.activation(hid[0:H, :], ph[0:H, 0:SP_], ACT.Silu, bias=b1c[:, :]).then_inc(s_hc, 1)

                with own_semaphores():
                    s_ld, s_z = sem("g_ld"), sem("g_z")
                    with nc.Block() as block:
                        cut = cutoff("gcut", block, ew, cw)

                        @block.sync
                        def _(sp):
                            sp.wait_ge(s_z, 1)
                            node_in(sp, x_sb, x, s_ld)
                            sp.dma_start(src_sb[:, :], src.rearrange("(p j) -> p j", p=SP_)).then_inc(s_ld, 16)
                            sp.dma_start(dst_sb[:, :], dst.rearrange("(p j) -> p j", p=SP_)).then_inc(s_ld, 16)
                            sp.dma_start(ew[:, :], edge_weight.rearrange("(p j) -> p j", p=SP_)).then_inc(s_ld, 16)

                        @block.vector
                        def _(dve):
                            nc.vector.memset(x_sb[:, NB - 1, :], 0.0)
                            nc.vector.memset(zrow[:, :, :], 0.0)
                            nc.vector.drain().then_inc(s_z, 1)
                            dve.wait_ge(s_ld, 80)
                            cut(dve)

                def fill_ones(dve):
                    nc.vector.memset(u_sb[:, :, :], 1.0)
                with own_semaphores():
                    node_block("ones", fill_ones, store=[(nodes(gT), u_sb[:, :, :])])
                    zero_table("zero_deg", sumT, H)
                    add_pass("deg", sumT, H, dst_sb, src_sb, False)

                with own_semaphores():
                    s_dv, s_ds = sem("s_dv"), sem("s_ds")

                    def degree(dve):
                        nc.vector.tensor_scalar(s1[:, :], v_sb[:, :, 0], 1.0, None, ALU.add).then_inc(s_dv, 1)
                        dve.wait_ge(s_ds, 1)
                        nc.vector.reciprocal(dinv[:, :], s2[:, :])
                        nc.vector.drain()
                        nc.vector.tensor_tensor(g_sb[:, :, :], x_sb[:, :, :], bcast(dinv), ALU.mult)

                    def degree_root(act):
                        act.wait_ge(s_dv, 1)
                        nc.scalar.activation(s2[:, :], s1[:, :], ACT.Sqrt).then_inc(s_ds, 1)
                    node_block("deg_n", degree, degree_root, load=(v_sb[:, :, :], nodes(sumT)), store=[(nodes(gT), g_sb[:, :, :])])

                with nc.Fori(0, STEPS):
                    with own_semaphores():
                        zero_table("zero", sumT, H)
                        add_pass("prop", sumT, H, dst_sb, src_sb, False)

                        def update(dve):
                            nc.vector.tensor_tensor(v_sb[:, :, :], v_sb[:, :, :], g_sb[:, :, :], ALU.add)
                            nc.vector.drain()
                            nc.vector.tensor_tensor(v_sb[:, :, :], v_sb[:, :, :], bcast(dinv), ALU.mult)
                            nc.vector.tensor_scalar(u_sb[:, :, :], x_sb[:, :, :], ALPHA, None, ALU.mult)
                            nc.vector.drain()
                            nc.vector.scalar_tensor_tensor(h_sb[:, :, :], v_sb[:, :, :], 1.0 - ALPHA, u_sb[:, :, :], ALU.mult, ALU.add)
                            nc.vector.drain()
                            nc.vector.tensor_tensor(g_sb[:, :, :], h_sb[:, :, :], bcast(dinv), ALU.mult)
                        node_block("upd", update, load=(v_sb[:, :, :], nodes(sumT)), store=[(nodes(gT), g_sb[:, :, :])])

                with own_semaphores():
                    norm0_block(h_sb[:, :, :], u_sb[:, :, :], store=[(nodes(dstT), dst_n[:, :, :]), (nodes(srcT), emb_n[:, :, :])])
                with own_semaphores():
                    zero_table("zero_agg", aggT, H + 1)
                    add_pass("conv", aggT, H + 1, src_sb, dst_sb, True)
                with own_semaphores():
                    final_block(zrow, v_sb[:, :, :], h_sb[:, :, :], u_sb[:, :, :], load=(zrow[:, :, :], nodes(aggT)))

        with own_semaphores():
            setup()
        fast_path()
        misfit = nc.values_load(flag_i[0:1, 0:1], min_val=0, max_val=1)
        with nc.If(misfit > 0):
            nc.all_engine_barrier()
            general_path()


_INS = ["x", "src", "dst", "edge_attr_40", "edge_weight", "node_type_119", "node_vec", "L1_gnn_W1", "L1_gnn_b1",
        "L1_gnn_W2", "L1_gnn_b2", "L1_gnn_emb", "L1_gnn_adaptW", "L1_gnn_gamma", "L1_gnn_beta"]


def kernel(**inputs):
    import numpy as _np
    import concourse.bacc as _bacc
    from concourse.bass_utils import run_bass_kernel_spmd as _run

    nc = _bacc.Bacc("TRN2", target_bir_lowering=False, num_devices=1)
    arrays, args = {}, []
    for name in _INS:
        a = _np.ascontiguousarray(inputs[name])
        arrays[f"in_{name}_dram"] = a
        args.append(nc.dram_tensor(f"in_{name}_dram", a.shape, mybir.dt.from_np(a.dtype), kind="ExternalInput").ap())
    args.append(nc.dram_tensor("out_0_dram", inputs["x"].shape, F32, kind="ExternalOutput").ap())
    gnn(nc, *args)
    r = _run(nc, [arrays], core_ids=[0])
    return r.results[0]["out_0_dram"]
```
